# Optimizing a Trainium2 kernel written in Bass

```python
import numpy as np
import jax
import jax.numpy as jnp

def _softmax(x, axis=-1):
    return jax.nn.softmax(x, axis=axis)

def _gelu(x):
    return jax.nn.gelu(x, approximate=True)

def _silu(x):
    return jax.nn.silu(x)

def _sigmoid(x):
    return jax.nn.sigmoid(x)

def _layernorm(x, axis=-1, eps=1e-05):
    m = jnp.mean(x, axis=axis, keepdims=True)
    v = jnp.var(x, axis=axis, keepdims=True)
    return (x - m) / jnp.sqrt(v + eps)

def _scatter_add(tgt, idx, src, axis=0):
    return tgt.at[idx].add(src)

def _segment_sum(src, seg, n):
    return jax.ops.segment_sum(src, seg, n)
kernel_name = 'mk_gnn_preln_d2_gnn_r64_28d7dc'

def setup_inputs(seed: int=0):
    np.random.seed(seed)
    _w = jnp.asarray

    def _rec_inputs():
        import jax
        import jax.numpy as jnp
        _gk = jax.random.key(seed)
        x = -0.0003713 + 1 * jax.random.normal(jax.random.fold_in(_gk, 1), (100000, 128), jnp.float32)
        src = jax.random.randint(jax.random.fold_in(_gk, 2), (50000,), 0, 100000, jnp.int32)
        dst = jnp.minimum((100000 * jax.random.uniform(jax.random.fold_in(_gk, 3), (50000,)) ** 2.0).astype(jnp.int32), 99999)
        _o = jnp.argsort(dst, stable=True)
        src = src[_o]
        dst = dst[_o]
        edge_type_16 = jax.random.randint(jax.random.fold_in(_gk, 13), (50000,), 0, 16, jnp.int32)
        return (x, src, dst, edge_type_16)
    x, src, dst, edge_type_16 = _rec_inputs()

    def _L0_gnn_setup():
        import jax, jax.numpy as jnp
        import numpy as np
        N_NODES = 100000
        N_EDGES = 50000
        IN_FEAT = 128
        OUT_FEAT = 128
        NUM_RELS = 16
        NUM_BASES = 8
        key = jax.random.key(seed)
        ks = jax.random.split(key, 7)
        x = jax.random.normal(ks[0], (N_NODES, IN_FEAT), dtype=jnp.float32)
        src = jax.random.randint(ks[1], (N_EDGES,), 0, N_NODES, dtype=jnp.int64)
        dst = jax.random.randint(ks[2], (N_EDGES,), 0, N_NODES, dtype=jnp.int64)
        etypes = jax.random.randint(ks[3], (N_EDGES,), 0, NUM_RELS, dtype=jnp.int64)
        gain = float(np.sqrt(2.0))
        limit_w = gain * float(np.sqrt(6.0 / (IN_FEAT + OUT_FEAT)))
        weight = jax.random.uniform(ks[4], (NUM_BASES, IN_FEAT, OUT_FEAT), dtype=jnp.float32, minval=-limit_w, maxval=limit_w)
        limit_c = float(np.sqrt(6.0 / (NUM_RELS + NUM_BASES)))
        w_comp = jax.random.uniform(ks[5], (NUM_RELS, NUM_BASES), dtype=jnp.float32, minval=-limit_c, maxval=limit_c)
        h_bias = jnp.zeros((OUT_FEAT,), dtype=jnp.float32)
        return {'x': x, 'weight': weight, 'w_comp': w_comp, 'h_bias': h_bias, 'src': src, 'dst': dst, 'etypes': etypes}
    _L0_gnn_all = _L0_gnn_setup()
    _L0_gnn_in = {k: v for k, v in _L0_gnn_all.items() if k in ('weight', 'w_comp', 'h_bias')}
    del _L0_gnn_all

    def _L1_gnn_setup():
        import jax, jax.numpy as jnp
        import numpy as np
        N_NODES = 20000
        N_EDGES = 10000
        HID = 128
        N_LAYERS = 2
        NEG_SLOPE = 0.1

        def _leaky(v):
            return jnp.where(v >= 0, v, NEG_SLOPE * v)
        key = jax.random.key(seed)
        ks = jax.random.split(key, 8)
        s = 1.0 / np.sqrt(HID)
        x = jax.random.normal(ks[0], (N_NODES, HID), dtype=jnp.float32)
        enc_w = jax.random.uniform(ks[1], (HID, HID), minval=-s, maxval=s, dtype=jnp.float32)
        enc_b = jax.random.uniform(ks[2], (HID,), minval=-s, maxval=s, dtype=jnp.float32)
        lin_l_w = jax.random.uniform(ks[3], (N_LAYERS, HID, HID), minval=-s, maxval=s, dtype=jnp.float32)
        lin_l_b = jax.random.uniform(ks[4], (N_LAYERS, HID), minval=-s, maxval=s, dtype=jnp.float32)
        lin_r_w = jax.random.uniform(ks[5], (N_LAYERS, HID, HID), minval=-s, maxval=s, dtype=jnp.float32)
        edge_index = jax.random.randint(ks[6], (2, N_EDGES), 0, N_NODES, dtype=jnp.int64)
        return {'x': x, 'enc_w': enc_w, 'enc_b': enc_b, 'lin_l_w': lin_l_w, 'lin_l_b': lin_l_b, 'lin_r_w': lin_r_w, 'edge_index': edge_index}
    _L1_gnn_all = _L1_gnn_setup()
    _L1_gnn_in = {k: v for k, v in _L1_gnn_all.items() if k in ('enc_w', 'enc_b', 'lin_l_w', 'lin_l_b', 'lin_r_w')}
    del _L1_gnn_all
    return {'x': x, 'src': src, 'dst': dst, 'edge_type_16': edge_type_16, 'L0_gnn_weight': _L0_gnn_in['weight'], 'L0_gnn_w_comp': _L0_gnn_in['w_comp'], 'L0_gnn_h_bias': _L0_gnn_in['h_bias'], 'L1_gnn_enc_w': _L1_gnn_in['enc_w'], 'L1_gnn_enc_b': _L1_gnn_in['enc_b'], 'L1_gnn_lin_l_w': _L1_gnn_in['lin_l_w'], 'L1_gnn_lin_l_b': _L1_gnn_in['lin_l_b'], 'L1_gnn_lin_r_w': _L1_gnn_in['lin_r_w']}

def reference(x, src, dst, edge_type_16, L0_gnn_weight, L0_gnn_w_comp, L0_gnn_h_bias, L1_gnn_enc_w, L1_gnn_enc_b, L1_gnn_lin_l_w, L1_gnn_lin_l_b, L1_gnn_lin_r_w):
    import jax
    import jax.numpy as jnp

    def _L0_gnn_ref(x, weight, w_comp, h_bias, src, dst, etypes):
        import jax, jax.numpy as jnp
        import numpy as np
        N_NODES = 100000
        N_EDGES = 50000
        IN_FEAT = 128
        OUT_FEAT = 128
        NUM_RELS = 16
        NUM_BASES = 8
        W = jnp.einsum('rb,bio->rio', w_comp, weight)
        h = jnp.einsum('ni,rio->rno', x, W)
        msg = h[etypes, src]
        node_repr = jax.ops.segment_sum(msg, dst, num_segments=N_NODES)
        node_repr = node_repr + h_bias
        return node_repr

    def _L1_gnn_ref(x, enc_w, enc_b, lin_l_w, lin_l_b, lin_r_w, edge_index):
        import jax, jax.numpy as jnp
        import numpy as np
        N_NODES = 20000
        N_EDGES = 10000
        HID = 128
        N_LAYERS = 2
        NEG_SLOPE = 0.1

        def _leaky(v):
            return jnp.where(v >= 0, v, NEG_SLOPE * v)
        src, dst = (edge_index[0], edge_index[1])
        n = x.shape[0]
        deg = jax.ops.segment_sum(jnp.ones((src.shape[0],), x.dtype), dst, num_segments=n)
        inv_deg = (1.0 / jnp.maximum(deg, 1.0))[:, None]
        h = _leaky(x @ enc_w + enc_b)
        for l in range(N_LAYERS):
            msg = h[src]
            agg = jax.ops.segment_sum(msg, dst, num_segments=n) * inv_deg
            h = _leaky(agg @ lin_l_w[l] + lin_l_b[l] + h @ lin_r_w[l])
        return h
    edge_index = jnp.stack([src, dst])
    h = jnp.maximum(_layernorm(x, axis=-1), 0.0)
    x = x + _L0_gnn_ref(h, L0_gnn_weight, L0_gnn_w_comp, L0_gnn_h_bias, src, dst, edge_type_16)
    h = jnp.maximum(_layernorm(x, axis=-1), 0.0)
    x = x + _L1_gnn_ref(h, L1_gnn_enc_w, L1_gnn_enc_b, L1_gnn_lin_l_w, L1_gnn_lin_l_b, L1_gnn_lin_r_w, edge_index)
    return x

_drawn_inputs = setup_inputs


def setup_inputs(seed=0):
    import zlib

    import numpy as np

    out = dict(_drawn_inputs(seed))
    spreads = {'L0_gnn_h_bias': (0.0, 0.1)}
    factors = {'L1_gnn_enc_b': 8.0}
    for name, (base, spread) in spreads.items():
        noise = np.random.default_rng([zlib.crc32(name.encode()), seed]).standard_normal(out[name].shape)
        drawn = base * np.exp(spread * noise) if base else spread * noise
        out[name] = jnp.asarray(drawn.astype(out[name].dtype))
    for name, factor in factors.items():
        out[name] = (out[name] * factor).astype(out[name].dtype)
    return out
```

```python
import concourse.bass as bass
from concourse import mybir
from contextlib import ExitStack

F32 = mybir.dt.float32
BF16 = mybir.dt.bfloat16
I32 = mybir.dt.int32
ALU = mybir.AluOpType
ACT = mybir.ActivationFunctionType
AX = mybir.AxisListType

P = 128
EPS = 1e-5
SLOPE = 0.1
DMA = 16

HALF = 7
ROW = 4 * P
NB = 4
BLOCK = NB * P
SLOTS = 4
FILL = 16 * P
BASES_ON_ACT = 2


def at_least(m, n):
    return not isinstance(m, int) or m >= n


def before(m, n):
    return not isinstance(m, int) or m < n


def wait_apart(eng, passed, *waits):
    for semaphore, value in waits:
        eng.wait_ge(semaphore, value)
    eng.sem_inc(passed, 1)


def steps(eng, step, head, tail, total, unroll):
    for m in range(head):
        step(m, m % unroll)
    with eng.Fori(head // unroll, tail // unroll) as i:
        for u in range(unroll):
            step(i * unroll + u, u)
    for m in range(tail, total):
        step(m, m % unroll)


def gnn_kernel(nc, x, src, dst, etype, basis_w, w_comp, h_bias, enc_w, enc_b, lin_l_w, lin_l_b,
               lin_r_w, out):
    N = x.shape[0]
    E = src.shape[0]
    R, B = w_comp.shape
    ROWS = -(-E // ROW)
    EP = ROWS * ROW
    T = EP // P
    HALVES = T // HALF
    NOWHERE = 2 * N
    BLOCKS = -(-N // BLOCK)
    LAST_BASE = N - BLOCK
    FILLS = -(-N // FILL)
    assert T % (2 * HALF) == 0 and BLOCKS % SLOTS == 0 and ROWS <= P and FILLS < HALVES - 2
    Y = B * P

    ctx = ExitStack()
    with ctx:
        def sb(name, shape, dt=F32):
            return ctx.enter_context(nc.sbuf_tensor(name, shape, dt))

        def sem(name):
            return ctx.enter_context(nc.semaphore(name))

        def dram(name, shape, dt=F32):
            return nc.dram_tensor(name, shape, dt).ap()

        src_s = dram("src_sorted", [EP], I32)
        dst_s = dram("dst_sorted", [EP], I32)
        typ_s = dram("type_sorted", [EP], I32)
        src_u = dram("src_padded", [EP], I32)
        dst_u = dram("dst_padded", [EP], I32)
        typ_u = dram("type_padded", [EP], I32)
        dst_f = dram("dst_float", [EP + 2])
        agg = [dram(f"agg{k}", [N, P]) for k in range(3)]
        x1 = dram("x1", [N, P])
        g = [dram(f"g{k}", [N, P]) for k in range(2)]

        ident = sb("ident", [P, P])
        ones = sb("ones", [P, P])
        bias_row = sb("bias_row", [P, 3, P])
        fill_rows = sb("fill_rows", [P, 3, FILL // P * P])
        w_basis = sb("w_basis", [P, B, P])
        w_enc = sb("w_enc", [P, P])
        w_l = sb("w_l", [P, 2, P])
        w_r = sb("w_r", [P, 2, P])
        hb_col = sb("hb_col", [P, 1])
        comp = sb("comp", [P, R * B])
        enc_parts = sb("enc_parts", [P, NB, P], BF16)
        enc_rest = sb("enc_rest", [P, 2, P])
        enc_tmp = sb("enc_tmp", [P, P], BF16)
        ones_bf = sb("ones_bf", [P, P], BF16)
        dst_c = sb("dst_c", [P, T])
        src_c = sb("src_c", [P, T], I32)
        put_c = sb("put_c", [P, T], I32)
        typ_c = sb("typ_c", [P, T])
        inv_c = sb("inv_c", [P, T])
        coef = sb("coef", [P, T, B])

        def cut(ap, start, size):
            return ap[bass.ds(start, size)]

        def rows_of(ap, first):
            return ap[bass.ds(first, BLOCK), :].rearrange("(p j) f -> p (j f)", p=P)

        def fill_of(ap, first):
            return ap[bass.ds(first, FILL), :].rearrange("(p j) f -> p (j f)", p=P)

        def base_of(m):
            return LAST_BASE if isinstance(m, int) and m == BLOCKS - 1 else m * BLOCK

        def fill_base(m):
            return N - FILL if isinstance(m, int) and m == FILLS - 1 else m * FILL

        with ExitStack() as st:
            W = E // 100
            assert W * 100 == E
            cur = st.enter_context(nc.sbuf_tensor("dst_cur", [100, W], I32))
            nxt = st.enter_context(nc.sbuf_tensor("dst_nxt", [100, W], I32))
            down = st.enter_context(nc.sbuf_tensor("down", [100, W], F32))
            downs = st.enter_context(nc.sbuf_tensor("downs", [P, 1], F32))
            unsorted = st.enter_context(nc.sbuf_tensor("unsorted", [1, 1], I32))
            pad = st.enter_context(nc.sbuf_tensor("pad", [1, 2, EP - E], I32))
            ends = st.enter_context(nc.sbuf_tensor("ends", [1, 2], F32))
            total = st.enter_context(nc.psum_tensor("total", [1, 1], F32))
            s_w = sem("weights_loaded")
            s_set = sem("dve_set")
            s_id0, s_id1 = sem("ident_zeroed"), sem("ident_made")
            s_dst = sem("dst_loaded")
            s_pads = sem("pads_set")
            s_padded = sem("pads_stored")
            s_bias = sem("bias_loaded")
            s_fill = sem("fill_made")
            s_filled = sem("agg0_filled")
            s_downs = sem("downs_counted")
            s_total = sem("downs_totalled")
            with nc.Block() as block:
                @block.sync
                def _(sp):
                    sp.wait_ge(s_set, 1)
                    sp.dma_start(cur[:], dst.rearrange("(p w) -> p w", w=W)).then_inc(s_dst, DMA)
                    sp.dma_start(nxt[0:99, :], dst[1:1 + 99 * W].rearrange("(p w) -> p w", w=W)).then_inc(s_dst, DMA)
                    sp.dma_start(nxt[99:100, 0:W - 1], dst[1 + 99 * W:E].unsqueeze(0)).then_inc(s_dst, DMA)
                    for k, b in enumerate((h_bias, lin_l_b[0, :], lin_l_b[1, :])):
                        sp.dma_start(bias_row[:, k, :], b.partition_broadcast(P)).then_inc(s_bias, DMA)
                    sp.wait_ge(s_set, 2)
                    for r in range(3):
                        sp.dma_start(enc_rest[32 * r:32 * r + 1, 0, :], enc_b.unsqueeze(0)).then_inc(s_bias, DMA)
                    sp.dma_start(hb_col[:], h_bias.unsqueeze(1)).then_inc(s_w, DMA)
                    sp.dma_start(comp[:], w_comp.rearrange("r b -> (r b)").partition_broadcast(P)).then_inc(s_w, DMA)
                    sp.dma_start(w_basis[:], basis_w.rearrange("b i o -> i b o")).then_inc(s_w, DMA)
                    sp.dma_start(w_enc[:], enc_w).then_inc(s_w, DMA)
                    sp.dma_start(w_l[:], lin_l_w.rearrange("l i o -> i l o")).then_inc(s_w, DMA)
                    sp.dma_start(w_r[:], lin_r_w.rearrange("l i o -> i l o")).then_inc(s_w, DMA)
                    sp.wait_ge(s_pads, 4)
                    for k, arrays in enumerate(((src_s, typ_s, src_u, typ_u), (dst_s, dst_u))):
                        for a in arrays:
                            sp.dma_start(a[E:EP].unsqueeze(0), pad[:, k, :]).then_inc(s_padded, DMA)
                    sp.dma_start(dst_f[0:1].unsqueeze(0), ends[:, 0:1]).then_inc(s_padded, DMA)
                    sp.dma_start(dst_f[EP + 1:EP + 2].unsqueeze(0), ends[:, 1:2]).then_inc(s_padded, DMA)
                    sp.wait_ge(s_fill, 3)
                    with sp.Fori(0, FILLS - 1) as m:
                        sp.dma_start(fill_of(agg[0], m * FILL), fill_rows[:, 0, :]).then_inc(s_filled, DMA)
                    sp.wait_ge(s_filled, DMA * (FILLS - 1))
                    sp.dma_start(fill_of(agg[0], N - FILL), fill_rows[:, 0, :]).then_inc(s_filled, DMA)
                    sp.wait_ge(s_w, 6 * DMA)
                    sp.wait_ge(s_padded, 8 * DMA)
                    sp.wait_ge(s_filled, DMA * FILLS)

                @block.gpsimd
                def _(pool):
                    nc.gpsimd.memset(ident[:], 0.0).then_inc(s_id0, 1)
                    pool.wait_ge(s_id0, 1)
                    nc.gpsimd.affine_select(out=ident[:], in_=ident[:], compare_op=ALU.not_equal, fill=1.0, base=0,
                                            pattern=[[-1, P]], channel_multiplier=1).then_inc(s_id1, 1)

                @block.vector
                def _(dve):
                    chain = [2]

                    def link(ins):
                        chain[0] += 1
                        ins.then_inc(s_set, 1)
                        dve.wait_ge(s_set, chain[0])

                    nc.vector.memset(nxt[:], NOWHERE).then_inc(s_set, 1)
                    nc.vector.memset(enc_rest[:], 0.0).then_inc(s_set, 1)
                    link(nc.vector.memset(ones[:], 1.0))
                    link(nc.vector.memset(ones_bf[:], 1.0))
                    link(nc.vector.memset(downs[:], 0.0))
                    nc.vector.memset(pad[:, 0, :], 0).then_inc(s_pads, 1)
                    nc.vector.memset(pad[:, 1, :], NOWHERE).then_inc(s_pads, 1)
                    nc.vector.memset(ends[:, 0:1], -1.0).then_inc(s_pads, 1)
                    nc.vector.memset(ends[:, 1:2], float(2 * NOWHERE)).then_inc(s_pads, 1)
                    dve.wait_ge(s_dst, 3 * DMA)
                    link(nc.vector.tensor_tensor(down[:], nxt[:], cur[:], ALU.is_lt))
                    nc.vector.reduce_sum(downs[0:100, :], down[:], AX.X).then_inc(s_downs, 1)
                    dve.wait_ge(s_bias, 6 * DMA)
                    for k in range(3):
                        nc.vector.tensor_copy(fill_rows[:, k, :].rearrange("p (j f) -> p j f", f=P),
                                              bias_row[:, k, :].unsqueeze(1).to_broadcast([P, FILL // P, P])).then_inc(s_fill, 1)
                    link(nc.vector.memset(enc_parts[:], 0.0))
                    for r in range(3):
                        link(nc.vector.tensor_copy(enc_tmp[:], enc_rest[:, 0, :]))
                        for j in range(NB):
                            link(nc.vector.tensor_copy(enc_parts[32 * r:32 * r + 1, j, :], enc_tmp[32 * r:32 * r + 1, :]))
                        link(nc.vector.tensor_tensor(enc_rest[:, 1, :], enc_rest[:, 0, :], enc_tmp[:], ALU.subtract))
                        link(nc.vector.tensor_copy(enc_rest[:, 0, :], enc_rest[:, 1, :]))
                    dve.wait_ge(s_total, 1)
                    link(nc.vector.tensor_copy(unsorted[:], total[:]))

                @block.tensor
                def _(pe):
                    pe.wait_ge(s_downs, 1)
                    nc.tensor.matmul(total[:], downs[:], ones[:, 0:1], start=True, stop=True).then_inc(s_total, 1)

            CH = EP // 8
            GROUP = 8
            row_i = st.enter_context(nc.sbuf_tensor("row_i", [P, CH], I32))
            row_f = st.enter_context(nc.sbuf_tensor("row_f", [P, CH], F32))
            frac = st.enter_context(nc.sbuf_tensor("frac", [P, CH], F32))
            gap = st.enter_context(nc.sbuf_tensor("gap", [P, CH], F32))
            hit = st.enter_context(nc.sbuf_tensor("hit", [P, CH], BF16))
            cols_u = st.enter_context(nc.sbuf_tensor("cols_u", [P, 3, T], I32))
            dcol = st.enter_context(nc.sbuf_tensor("dcol", [P, T], F32))
            thr_i = st.enter_context(nc.sbuf_tensor("thr_i", [P, T], I32))
            thr = st.enter_context(nc.sbuf_tensor("thr", [P, 2, T], F32))
            below = st.enter_context(nc.sbuf_tensor("below", [P, T], F32))
            rank = st.enter_context(nc.sbuf_tensor("rank", [P, 2, T], F32))
            rank_i = st.enter_context(nc.sbuf_tensor("rank_i", [P, T], I32))
            stage = st.enter_context(nc.sbuf_tensor("stage", [P, 4, GROUP], I32))
            s_u = sem("padded_copied")
            s_cols = sem("columns_loaded")
            s_iota = sem("iotas_made")
            s_row = sem("row_loaded")
            s_rowused = sem("row_used")
            s_rk = sem("rank_steps")
            s_ranked = sem("ranked")
            s_staged = sem("staged")
            s_spread = [sem(f"spread{k}") for k in range(3)]
            s_direct = sem("sorted_copied")
            s_passed = sem("waits_passed")
            with nc.Block() as block:
                @block.sync
                def _(sp):
                    flag = sp.value_load(unsorted[0:1, 0:1], min_val=0, max_val=E)
                    with sp.If(flag != 0):
                        for a, b in ((src, src_u), (dst, dst_u), (etype, typ_u)):
                            sp.dma_start(b[0:E], a).then_inc(s_u, DMA)
                        sp.wait_ge(s_u, 3 * DMA)
                        with nc.allow_non_contiguous_dma(reason="edges into columns, in the rare order"):
                            for k, a in enumerate((dst_u, src_u, typ_u)):
                                sp.dma_start(cols_u[:, k, :], a.rearrange("(t p) -> p t", p=P)).then_inc(s_cols, DMA)
                        for c in range(8):
                            if c:
                                sp.wait_ge(s_rowused, c)
                            sp.dma_start(row_i[:], dst_u[c * CH:(c + 1) * CH].partition_broadcast(P)).then_inc(s_row, DMA)
                            sp.wait_ge(s_row, DMA * (c + 1))
                        sp.wait_ge(s_cols, 3 * DMA)
                    with sp.Else():
                        for a, b in ((src, src_s), (dst, dst_s), (etype, typ_s)):
                            sp.dma_start(b[0:E], a).then_inc(s_direct, DMA)
                        sp.wait_ge(s_direct, 3 * DMA)
                    sp.drain()

                @block.vector
                def _(dve):
                    flag = dve.value_load(unsorted[0:1, 0:1], min_val=0, max_val=E)
                    with dve.If(flag != 0):
                        dve.wait_ge(s_iota, 2)
                        nc.vector.tensor_scalar(thr[:, 0, :], thr_i[:], 1.0 / 65536, None, ALU.mult).then_inc(s_rk, 1)
                        nc.vector.tensor_scalar(frac[:], gap[:].bitcast(I32), 1.0 / 65536, None, ALU.mult).then_inc(s_rk, 1)
                        dve.wait_ge(s_cols, 3 * DMA)
                        nc.vector.tensor_copy(dcol[:], cols_u[:, 0, :]).then_inc(s_rk, 1)
                        nc.vector.memset(rank[:, 0, :], 0.0).then_inc(s_rk, 1)
                        done = 4
                        for c in range(8):
                            a, b = c % 2, 1 - c % 2
                            dve.wait_ge(s_rk, done)
                            dve.wait_ge(s_row, DMA * (c + 1))
                            nc.vector.tensor_copy(row_f[:], row_i[:]).then_inc(s_rowused, 1)
                            dve.wait_ge(s_rowused, c + 1)
                            with dve.Fori(0, T) as t:
                                nc.vector.scalar_tensor_tensor(gap[:], row_f[:], dcol[:, bass.ds(t, 1)], frac[:],
                                                               ALU.subtract, ALU.add).then_inc(s_rk, 1)
                                dve.wait_ge(s_rk, t * 2 + (done + 1))
                                nc.vector.tensor_scalar(hit[:], gap[:], thr[:, a, bass.ds(t, 1)], None, ALU.is_lt,
                                                        ALU.add, accum_out=below[:, bass.ds(t, 1)]).then_inc(s_rk, 1)
                                dve.wait_ge(s_rk, t * 2 + (done + 2))
                            done += 2 * T
                            nc.vector.tensor_tensor(rank[:, b, :], rank[:, a, :], below[:], ALU.add).then_inc(s_rk, 1)
                            nc.vector.tensor_scalar(thr[:, b, :], thr[:, a, :], -CH / 65536, None, ALU.add).then_inc(s_rk, 1)
                            done += 2
                        dve.wait_ge(s_rk, done)
                        nc.vector.tensor_copy(rank_i[:], rank[:, 0, :]).then_inc(s_ranked, 1)
                        dve.wait_ge(s_ranked, 1)
                    dve.drain()

                @block.gpsimd
                def _(pool):
                    flag = pool.value_load(unsorted[0:1, 0:1], min_val=0, max_val=E)
                    with pool.If(flag != 0):
                        nc.gpsimd.iota(thr_i[:], [[P, T]], base=0, channel_multiplier=1).then_inc(s_iota, 1)
                        nc.gpsimd.iota(gap[:].bitcast(I32), [[1, CH]], base=0, channel_multiplier=0).then_inc(s_iota, 1)
                        pool.wait_ge(s_ranked, 1)
                        pool.wait_ge(s_cols, 3 * DMA)
                        with pool.Fori(0, T // GROUP) as i:
                            col = bass.ds(i * GROUP, GROUP)
                            nc.gpsimd.tensor_copy(stage[:, 3, :], rank_i[:, col]).then_inc(s_staged, 1)
                            for k in range(3):
                                nc.gpsimd.tensor_copy(stage[:, k, :], cols_u[:, k, col]).then_inc(s_staged, 1)
                            wait_apart(pool, s_passed, (s_staged, i * 4 + 4))
                            for k, a in enumerate((dst_s, src_s, typ_s)):
                                for c in range(GROUP):
                                    nc.gpsimd.indirect_dma_start(
                                        a.unsqueeze(1), bass.IndirectOffsetOnAxis(ap=stage[:, 3, c:c + 1], axis=0),
                                        stage[:, k, c:c + 1], None).then_inc(s_spread[k], DMA)
                            wait_apart(pool, s_passed, *[(s_spread[k], i * (DMA * GROUP) + DMA * GROUP) for k in range(3)])
                    pool.drain()

        with ExitStack() as st:
            def row(name, dt=F32):
                return st.enter_context(nc.sbuf_tensor(name, [P, ROW], dt))

            src_i, dst_i, typ_i = row("src_i", I32), row("dst_i", I32), row("typ_i", I32)
            here, prev, succ = row("here"), row("prev"), row("succ")
            index_i, index = row("index_i", I32), row("index")
            starts, first, first_in = row("starts"), row("first"), row("first_in")
            firsts, degree, inverse = row("firsts"), row("degree"), row("inverse")
            ends_run, put = row("ends_run"), row("put")
            src_r, typ_r, kept = row("src_r"), row("typ_r"), row("kept")
            carry = st.enter_context(nc.sbuf_tensor("carry", [1, 2, P], F32))
            carry_col = st.enter_context(nc.sbuf_tensor("carry_col", [P, 1], F32))
            onehot = st.enter_context(nc.sbuf_tensor("onehot", [P, R, T], F32))
            turned = [st.enter_context(nc.psum_tensor(f"turned{k}", [P, 4, P], F32)) for k in range(5)]
            carry_ps = st.enter_context(nc.psum_tensor("carry_ps", [1, P], F32))
            carry_back = st.enter_context(nc.psum_tensor("carry_back", [P, 1], F32))
            s_rows = sem("rows_loaded")
            s_zero = sem("rows_zeroed")
            s_index = sem("index_made")
            s_here = sem("here_made")
            s_dstf = sem("dst_float_stored")
            s_shift = sem("shifts_loaded")
            s_v = sem("row_steps")
            s_lastcol = sem("last_column")
            s_carry = sem("carry_turned")
            s_scan = sem("carry_scanned")
            s_back = sem("carry_back_turned")
            s_ready = sem("row_ready")
            s_turned = sem("row_turned")
            s_col = sem("columns_made")
            s_one = sem("onehots")
            s_coef = sem("coef_steps")
            order = [src_r, here, put, typ_r, inverse]

            with nc.Block() as block:
                @block.sync
                def _(sp):
                    sp.wait_ge(s_zero, 3)
                    for a, b in ((dst_s, dst_i), (src_s, src_i), (typ_s, typ_i)):
                        sp.dma_start(b[0:ROWS, :], a.rearrange("(r k) -> r k", k=ROW)).then_inc(s_rows, DMA)
                    sp.wait_ge(s_here, 1)
                    sp.dma_start(dst_f[1:1 + EP].rearrange("(r k) -> r k", k=ROW), here[0:ROWS, :]).then_inc(s_dstf, DMA)
                    sp.wait_ge(s_dstf, DMA)
                    sp.wait_ge(s_zero, 5)
                    sp.dma_start(prev[0:ROWS, :], dst_f[0:EP].rearrange("(r k) -> r k", k=ROW)).then_inc(s_shift, DMA)
                    sp.dma_start(succ[0:ROWS, :], dst_f[2:2 + EP].rearrange("(r k) -> r k", k=ROW)).then_inc(s_shift, DMA)

                @block.gpsimd
                def _(pool):
                    nc.gpsimd.iota(index_i[:], [[1, ROW]], base=0, channel_multiplier=ROW).then_inc(s_index, 1)

                @block.vector
                def _(dve):
                    chain = [0]

                    def link(ins):
                        chain[0] += 1
                        ins.then_inc(s_v, 1)
                        dve.wait_ge(s_v, chain[0])

                    for a in (dst_i, src_i, typ_i, prev, succ):
                        nc.vector.memset(a[:], 0).then_inc(s_zero, 1)
                    dve.wait_ge(s_zero, 5)
                    dve.wait_ge(s_rows, 3 * DMA)
                    nc.vector.tensor_copy(here[:], dst_i[:]).then_inc(s_here, 1)
                    dve.wait_ge(s_here, 1)
                    link(nc.vector.tensor_copy(src_r[:], src_i[:]))
                    link(nc.vector.tensor_copy(typ_r[:], typ_i[:]))
                    dve.wait_ge(s_index, 1)
                    link(nc.vector.tensor_copy(index[:], index_i[:]))
                    dve.wait_ge(s_shift, 2 * DMA)
                    link(nc.vector.tensor_tensor(starts[:], here[:], prev[:], ALU.not_equal))
                    link(nc.vector.tensor_tensor(first_in[:], starts[:], index[:], ALU.mult))
                    link(nc.vector.tensor_tensor_scan(first[:], first_in[:], first_in[:], 0.0, ALU.max, ALU.max))
                    dve.wait_ge(s_v, chain[0])
                    nc.vector.tensor_copy(carry_col[:], first[:, ROW - 1:ROW]).then_inc(s_lastcol, 1)
                    dve.wait_ge(s_carry, 1)
                    link(nc.vector.memset(carry[:, 1, 0:1], 0.0))
                    link(nc.vector.tensor_copy(carry[:, 0, :], carry_ps[:]))
                    link(nc.vector.tensor_tensor_scan(carry[:, 1, 1:P], carry[:, 0, 0:P - 1], carry[:, 0, 0:P - 1], 0.0,
                                                      ALU.max, ALU.max))
                    nc.vector.drain().then_inc(s_scan, 1)
                    dve.wait_ge(s_back, 1)
                    link(nc.vector.tensor_copy(carry_col[:], carry_back[:]))
                    link(nc.vector.tensor_scalar(firsts[:], first[:], carry_col[:], None, ALU.max))
                    link(nc.vector.tensor_tensor(degree[:], index[:], firsts[:], ALU.subtract))
                    link(nc.vector.tensor_scalar(degree[:], degree[:], 1.0, None, ALU.add))
                    link(nc.vector.reciprocal(inverse[:], degree[:]))
                    link(nc.vector.tensor_tensor(ends_run[:], here[:], succ[:], ALU.is_equal))
                    link(nc.vector.tensor_scalar(kept[:], ends_run[:], float(NOWHERE), None, ALU.mult))
                    link(nc.vector.tensor_tensor(put[:], kept[:], here[:], ALU.add))
                    nc.vector.drain().then_inc(s_ready, 1)
                    for k, col in enumerate((src_c, dst_c, put_c, typ_c, inv_c)):
                        dve.wait_ge(s_turned, k + 1)
                        nc.vector.tensor_copy(col[:].rearrange("p (r c) -> p c r", c=4),
                                              turned[k][:, :, 0:ROWS]).then_inc(s_col, 1)
                    dve.wait_ge(s_col, 5)
                    for r in range(R):
                        nc.vector.tensor_scalar(onehot[:, r, :], typ_c[:], float(r), None, ALU.is_equal).then_inc(s_one, 1)
                    for r in range(R):
                        dve.wait_ge(s_one, r + 1)
                        for b in range(B):
                            w = comp[:, r * B + b:r * B + b + 1]
                            if r == 0:
                                nc.vector.tensor_scalar(coef[:, :, b], onehot[:, r, :], w, None, ALU.mult).then_inc(s_coef, 1)
                            else:
                                dve.wait_ge(s_coef, B * (r - 1) + b + 1)
                                nc.vector.scalar_tensor_tensor(coef[:, :, b], onehot[:, r, :], w, coef[:, :, b],
                                                               ALU.mult, ALU.add).then_inc(s_coef, 1)

                @block.tensor
                def _(pe):
                    pe.wait_ge(s_lastcol, 1)
                    nc.tensor.matmul(carry_ps[:], carry_col[:], ident[:], start=True, stop=True).then_inc(s_carry, 1)
                    pe.wait_ge(s_scan, 1)
                    nc.tensor.matmul(carry_back[:], carry[:, 1, :], ones[0:1, 0:1], start=True, stop=True).then_inc(s_back, 1)
                    pe.wait_ge(s_ready, 1)
                    for k, a in enumerate(order):
                        for c in range(4):
                            last = nc.tensor.transpose(turned[k][:, c, :], a[:, c * P:(c + 1) * P], ident[:])
                        last.then_inc(s_turned, 1)

        def clear(held):
            nc.clear_and_free_semaphores(held)
            nc.all_engine_barrier()

        def edge_pass(k, table):
            relational = k == 0
            held = []
            lag = 3 if relational else 2
            with ExitStack() as st:
                def buf(name, shape, dt=F32):
                    return st.enter_context(nc.sbuf_tensor(f"{name}_{k}", shape, dt))

                def bank(name, shape):
                    return st.enter_context(nc.psum_tensor(f"{name}_{k}", shape, F32))

                def psem(name):
                    held.append(nc.alloc_semaphore(f"{name}_{k}"))
                    return held[-1]

                gat = buf("gat", [P, 2, HALF, P])
                rows = buf("rows", [P, 2, HALF, P])
                gidx = buf("gidx", [P, 2, HALF], I32)
                pidx = buf("pidx", [P, 2, HALF], I32)
                dst_b = buf("dst_b", [P, 2, HALF * P + 1])
                same = buf("same", [P, 2, HALF, P])
                open_ = buf("open", [P, 2, HALF, P])
                sums = buf("sums", [P, 2, P])
                sum_ps = [bank(f"sum_ps{i}", [P, 512]) for i in range(2)]
                row_ps = [bank(f"row_ps{i}", [P, 512]) for i in range(1 if relational else 2)]
                s_gathered = [[psem(f"gathered{q}{j}") for j in range(HALF)] for q in range(2)]
                s_scattered = [[psem(f"scattered{q}{j}") for j in range(HALF)] for q in range(2)]
                s_gidx, s_pidx = psem("gather_index"), psem("scatter_index")
                s_dstb = [psem(f"dst_b{q}") for q in range(2)]
                s_same, s_open = psem("same_made"), psem("open_made")
                s_summed = psem("summed")
                s_carried = psem("carried")
                s_rowed = psem("rowed")
                s_rows = psem("rows_ready")
                s_start = psem("carry_zeroed")
                s_passed, s_dve_passed = psem("pool_passed"), psem("dve_passed")
                s_fills = [psem(f"filled{i}") for i in (1, 2)]
                if relational:
                    st6 = buf("st6", [P, 2, HALF, 6])
                    mv = buf("mv", [P, 2, HALF, 2])
                    var = buf("var", [P, 2, HALF])
                    std = buf("std", [P, 2, HALF])
                    rstd = buf("rstd", [P, 2, HALF])
                    shift = buf("shift", [P, 2, HALF])
                    h = buf("h", [P, 2, HALF, P])
                    ht = buf("ht", [P, 2, HALF, P])
                    part = buf("part", [P, 2, BASES_ON_ACT, P])
                    two = buf("two", [P, 2, 2, P])
                    msg = buf("msg", [P, 2, HALF, P])
                    sums_b = buf("sums_b", [P, 2, P])
                    y_ps = [bank(f"y_ps{i}", [P, Y]) for i in range(2)]
                    ht_ps = bank("ht_ps", [P, 512])
                    s_stat, s_mv, s_var = psem("stats"), psem("mean_var"), psem("var_eps")
                    s_std, s_rstd, s_shift = psem("std"), psem("rstd"), psem("shift")
                    s_h, s_turn, s_ht = psem("h"), psem("turned"), psem("ht")
                    s_y, s_part, s_acc, s_msg = psem("y"), psem("part"), psem("acc"), psem("msg")
                    s_biased = psem("biased")
                else:
                    msg = gat

                def tile(m, j):
                    return m * HALF + (j + 1)

                def use(m, q):
                    return (m // 2 + 1) * DMA if isinstance(m, int) else (m - q) * (DMA // 2) + DMA

                def group(m, a):
                    return m * 2 + (a + 1)

                with nc.Block() as block:
                    @block.gpsimd
                    def _(pool):
                        def step(m, q):
                            if before(m, HALVES):
                                if at_least(m, 2):
                                    pool.wait_ge(s_h if relational else s_summed, tile(m - 2, HALF - 1))
                                nc.gpsimd.tensor_copy(gidx[:, q, :], src_c[:, bass.ds(m * HALF, HALF)]).then_inc(s_gidx, 1)
                            if at_least(m, lag):
                                o, oq = m - lag, (q - lag) % 2
                                if at_least(m, lag + 2):
                                    for j in range(HALF):
                                        pool.wait_ge(s_scattered[oq][j], use(o - 2, oq))
                                nc.gpsimd.tensor_copy(pidx[:, oq, :], put_c[:, bass.ds(o * HALF, HALF)]).then_inc(s_pidx, 1)
                            wait_apart(pool, s_passed, *[(s_gidx, m + 1)] * before(m, HALVES),
                                       *[(s_pidx, m + (1 - lag))] * at_least(m, lag))
                            for j in range(HALF):
                                if before(m, HALVES):
                                    nc.gpsimd.indirect_dma_start(
                                        gat[:, q, j, :], None, table,
                                        bass.IndirectOffsetOnAxis(ap=gidx[:, q, j:j + 1], axis=0)).then_inc(s_gathered[q][j], DMA)
                                if at_least(m, lag):
                                    wait_apart(pool, s_passed, (s_rows, tile(o, j)))
                                    nc.gpsimd.indirect_dma_start(
                                        agg[k], bass.IndirectOffsetOnAxis(ap=pidx[:, oq, j:j + 1], axis=0),
                                        rows[:, oq, j, :], None, bounds_check=N - 1,
                                        oob_is_err=False).then_inc(s_scattered[oq][j], DMA)

                        steps(pool, step, 6, HALVES, HALVES + lag, 2)
                        for q in range(2):
                            for j in range(HALF):
                                pool.wait_ge(s_scattered[q][j], DMA * HALVES // 2)

                    @block.sync
                    def _(sp):
                        def step(m, q):
                            if at_least(m, 2):
                                sp.wait_ge(s_same, m - 1)
                                sp.wait_ge(s_open, m - 1)
                            sp.dma_start(dst_b[:, q, :], cut(dst_f, m * (HALF * P), HALF * P + 1)
                                         .partition_broadcast(P)).then_inc(s_dstb[q], DMA)
                            if relational and before(m, FILLS):
                                for i in (1, 2):
                                    if not before(m, FILLS - 1):
                                        sp.wait_ge(s_fills[i - 1], DMA * (FILLS - 1))
                                    sp.dma_start(fill_of(agg[i], fill_base(m)), fill_rows[:, i, :]).then_inc(s_fills[i - 1], DMA)

                        steps(sp, step, 4, 48, HALVES, 2)
                        if relational:
                            for i in range(2):
                                sp.wait_ge(s_fills[i], DMA * FILLS)

                    @block.vector
                    def _(dve):
                        nc.vector.memset(sums[:, 1, :], 0.0).then_inc(s_start, 1)
                        dve.wait_ge(s_start, 1)

                        def select(m, q):
                            dve.wait_ge(s_dstb[q], use(m, q))
                            if at_least(m, 2):
                                dve.wait_ge(s_summed, tile(m - 2, HALF - 1))
                                dve.wait_ge(s_carried, tile(m - 2, HALF - 1))
                            d = dst_b[:, q, 1:HALF * P + 1].rearrange("p (t e) -> p t e", e=P)
                            nc.vector.tensor_tensor(same[:, q, :, :], d,
                                                    dst_c[:, bass.ds(m * HALF, HALF)].unsqueeze(2).to_broadcast([P, HALF, P]),
                                                    ALU.is_equal).then_inc(s_same, 1)
                            before_ = dst_b[:, q, 0:HALF * P].rearrange("p (t e) -> p t e", e=P)[:, :, 0:1]
                            nc.vector.tensor_tensor(open_[:, q, :, :], d, before_.to_broadcast([P, HALF, P]),
                                                    ALU.is_equal).then_inc(s_open, 1)

                        def stats(m, q):
                            for j in range(HALF):
                                dve.wait_ge(s_gathered[q][j], use(m, q))
                                nc.vector.bn_stats(st6[:, q, j, :], gat[:, q, j, :]).then_inc(s_stat, 1)
                            for j in range(HALF):
                                wait_apart(dve, s_dve_passed, (s_stat, tile(m, j)))
                                nc.vector.bn_aggr(mv[:, q, j, :], st6[:, q, j, :]).then_inc(s_mv, 1)
                            dve.wait_ge(s_mv, tile(m, HALF - 1))
                            nc.vector.tensor_scalar(var[:, q, :], mv[:, q, :, 1], EPS, None, ALU.add).then_inc(s_var, 1)

                        def scales(m, q):
                            dve.wait_ge(s_std, m + 1)
                            if at_least(m, 2):
                                dve.wait_ge(s_h, tile(m - 2, HALF - 1))
                            nc.vector.reciprocal(rstd[:, q, :], std[:, q, :]).then_inc(s_rstd, 1)
                            dve.wait_ge(s_rstd, m + 1)
                            nc.vector.scalar_tensor_tensor(shift[:, q, :], mv[:, q, :, 0], -1.0, rstd[:, q, :],
                                                           ALU.mult, ALU.mult).then_inc(s_shift, 1)

                        def message(m, q, j):
                            y = y_ps[(q + j) % 2]
                            acc = two[:, (q + j) % 2, :, :]
                            dve.wait_ge(s_part, tile(m, j))
                            n = 0
                            for i in range(3):
                                for a in range(2):
                                    b = 2 * i + a
                                    c = coef[:, bass.ds(m * HALF + j, 1), b]
                                    prior = part[:, (q + j) % 2, a, :] if i == 0 else acc[:, a, :]
                                    if i:
                                        dve.wait_ge(s_acc, (m * HALF + j) * 6 + (n - 1))
                                    nc.vector.scalar_tensor_tensor(acc[:, a, :], y[:, b * P:(b + 1) * P], c, prior,
                                                                   ALU.mult, ALU.add).then_inc(s_acc, 1)
                                    n += 1
                            if at_least(m, 2):
                                dve.wait_ge(s_summed, tile(m - 2, j))
                            dve.wait_ge(s_acc, (m * HALF + j) * 6 + 6)
                            nc.vector.tensor_tensor(msg[:, q, j, :], acc[:, 0, :], acc[:, 1, :], ALU.add).then_inc(s_msg, 1)

                        def carry_on(m, q, j):
                            s = (q + j) % 2
                            dve.wait_ge(s_summed, tile(m, j))
                            if at_least(m, 1) or j >= 1:
                                dve.wait_ge(s_carried, tile(m, j) - 1)
                            if j == 0:
                                dve.wait_ge(s_open, m + 1)
                            if at_least(m, 1) or j >= 2:
                                dve.wait_ge(s_biased if relational else s_rowed, tile(m, j) - 2)
                            nc.vector.scalar_tensor_tensor(sums[:, s, :], open_[:, q, j, :], sums[:, 1 - s, P - 1:P],
                                                           sum_ps[s][:, 0:P], ALU.mult, ALU.add).then_inc(s_carried, 1)

                        def finish(m, q, j):
                            dve.wait_ge(s_rowed, tile(m, j))
                            if at_least(m, 2):
                                dve.wait_ge(s_scattered[q][j], use(m - 2, q))
                            nc.vector.scalar_tensor_tensor(rows[:, q, j, :], row_ps[(q + j) % 2][:, 0:P],
                                                           inv_c[:, bass.ds(m * HALF + j, 1)], bias_row[:, k, :],
                                                           ALU.mult, ALU.add).then_inc(s_rows, 1)

                        def prior_tile(m, q, j, what):
                            if j:
                                what(m, q, j - 1)
                            elif at_least(m, 1):
                                what(m - 1, 1 - q, HALF - 1)

                        def step(m, q):
                            if relational and before(m, HALVES - 1):
                                stats(m + 1, 1 - q)
                            select(m, q)
                            for j in range(HALF):
                                if relational:
                                    message(m, q, j)
                                    prior_tile(m, q, j, carry_on)
                                    if j == 0 and before(m, HALVES - 1):
                                        scales(m + 1, 1 - q)
                                else:
                                    carry_on(m, q, j)
                                    prior_tile(m, q, j, finish)

                        if relational:
                            stats(0, 0)
                            scales(0, 0)
                        steps(dve, step, 4, HALVES - 2, HALVES, 2)
                        prior_tile(HALVES, 0, 0, carry_on if relational else finish)

                    if relational:
                        @block.scalar
                        def _(act):
                            def deviation(m, q):
                                act.wait_ge(s_var, m + 1)
                                nc.scalar.activation(std[:, q, :], var[:, q, :], ACT.Sqrt).then_inc(s_std, 1)

                            def normalize(m, q, j):
                                act.wait_ge(s_shift, m + 1)
                                if at_least(m, 2):
                                    act.wait_ge(s_turn, group(m - 2, 1))
                                nc.scalar.activation(h[:, q, j, :], gat[:, q, j, :], ACT.Relu, bias=shift[:, q, j:j + 1],
                                                     scale=rstd[:, q, j:j + 1]).then_inc(s_h, 1)

                            def keep_turned(m, q, a):
                                lo, hi = (0, 4) if a == 0 else (4, HALF)
                                act.wait_ge(s_turn, group(m, a))
                                if at_least(m, 2):
                                    act.wait_ge(s_y, tile(m - 2, HALF - 1))
                                nc.scalar.activation(ht[:, q, lo:hi, :], ht_ps[:, 0:(hi - lo) * P]
                                                     .rearrange("p (t e) -> p t e", e=P), ACT.Copy).then_inc(s_ht, 1)

                            def begin(m, q, j):
                                s = (q + j) % 2
                                act.wait_ge(s_y, tile(m, j))
                                if at_least(m, 1) or j >= 2:
                                    act.wait_ge(s_acc, (m * HALF + j) * 6 - 6)
                                for a in range(BASES_ON_ACT):
                                    b = B - BASES_ON_ACT + a
                                    last = nc.scalar.activation(part[:, s, a, :], y_ps[s][:, b * P:(b + 1) * P], ACT.Copy,
                                                                scale=coef[:, bass.ds(m * HALF + j, 1), b])
                                last.then_inc(s_part, 1)

                            def add_bias(m, q, j):
                                s = (q + j) % 2
                                act.wait_ge(s_carried, tile(m, j))
                                if at_least(m, 1) or j >= 2:
                                    act.wait_ge(s_rowed, tile(m, j) - 2)
                                nc.scalar.activation(sums_b[:, s, :], sums[:, s, :], ACT.Identity,
                                                     bias=hb_col[:]).then_inc(s_biased, 1)

                            def keep_rows(m, q, j):
                                act.wait_ge(s_rowed, tile(m, j))
                                if at_least(m, 2):
                                    act.wait_ge(s_scattered[q][j], use(m - 2, q))
                                nc.scalar.activation(rows[:, q, j, :], row_ps[0][:, 0:P], ACT.Copy).then_inc(s_rows, 1)

                            def ago(m, q, j, n, what):
                                if j >= n:
                                    what(m, q, j - n)
                                elif at_least(m, 1):
                                    what(m - 1, 1 - q, HALF + j - n)

                            def step(m, q):
                                more = before(m, HALVES - 1)
                                if more:
                                    deviation(m + 1, 1 - q)
                                for j in range(HALF):
                                    begin(m, q, j)
                                    ago(m, q, j, 2, add_bias)
                                    ago(m, q, j, 3, keep_rows)
                                    if more and 1 <= j <= 4:
                                        for i in ((0, 1), (2, 3), (4, 5), (6,))[j - 1]:
                                            normalize(m + 1, 1 - q, i)
                                    if more and j == 4:
                                        keep_turned(m + 1, 1 - q, 0)
                                    if more and j == 6:
                                        keep_turned(m + 1, 1 - q, 1)

                            deviation(0, 0)
                            for j in range(HALF):
                                normalize(0, 0, j)
                            keep_turned(0, 0, 0)
                            keep_turned(0, 0, 1)
                            steps(act, step, 4, HALVES - 2, HALVES, 2)
                            for j in range(3):
                                if j < 2:
                                    ago(HALVES, 0, j, 2, add_bias)
                                ago(HALVES, 0, j, 3, keep_rows)

                    @block.tensor
                    def _(pe):
                        def turn(m, q, a):
                            lo, hi = (0, 4) if a == 0 else (4, HALF)
                            pe.wait_ge(s_h, tile(m, hi - 1))
                            if at_least(m, 1) or a:
                                pe.wait_ge(s_ht, group(m, a) - 1)
                            for t in range(lo, hi):
                                last = nc.tensor.transpose(ht_ps[:, (t - lo) * P:(t - lo + 1) * P], h[:, q, t, :], ident[:])
                            last.then_inc(s_turn, 1)

                        def products(m, q, j):
                            pe.wait_ge(s_ht, group(m, 0 if j < 4 else 1))
                            if at_least(m, 1) or j >= 2:
                                pe.wait_ge(s_acc, (m * HALF + j) * 6 - 6)
                            for c in range(Y // 512):
                                last = nc.tensor.matmul(y_ps[(q + j) % 2][:, c * 512:(c + 1) * 512], ht[:, q, j, :],
                                                        w_basis[:, 4 * c:4 * c + 4, :], start=True, stop=True)
                            last.then_inc(s_y, 1)

                        def sum_runs(m, q, j):
                            if relational:
                                pe.wait_ge(s_msg, tile(m, j))
                            else:
                                pe.wait_ge(s_gathered[q][j], use(m, q))
                            if j == 0:
                                pe.wait_ge(s_same, m + 1)
                            if at_least(m, 1) or j >= 2:
                                pe.wait_ge(s_carried, tile(m, j) - 2)
                            nc.tensor.matmul(sum_ps[(q + j) % 2][:, 0:P], msg[:, q, j, :], same[:, q, j, :],
                                             start=True, stop=True).then_inc(s_summed, 1)

                        def to_rows(m, q, j):
                            s = (q + j) % 2
                            if relational:
                                pe.wait_ge(s_biased, tile(m, j))
                                if at_least(m, 1) or j >= 1:
                                    pe.wait_ge(s_rows, tile(m, j) - 1)
                                nc.tensor.transpose(row_ps[0][:, 0:P], sums_b[:, s, :], ident[:]).then_inc(s_rowed, 1)
                            else:
                                pe.wait_ge(s_carried, tile(m, j))
                                if at_least(m, 1) or j >= 2:
                                    pe.wait_ge(s_rows, tile(m, j) - 2)
                                nc.tensor.matmul(row_ps[s][:, 0:P], sums[:, s, :], w_l[:, k - 1, :],
                                                 start=True, stop=True).then_inc(s_rowed, 1)

                        def ago(m, q, j, n, what):
                            if j >= n:
                                what(m, q, j - n)
                            elif at_least(m, 1):
                                what(m - 1, 1 - q, HALF + j - n)

                        def step(m, q):
                            for j in range(HALF):
                                if relational:
                                    products(m, q, j)
                                    ago(m, q, j, 1, sum_runs)
                                    ago(m, q, j, 2, to_rows)
                                    if before(m, HALVES - 1) and j in (4, 6):
                                        turn(m + 1, 1 - q, (j - 4) // 2)
                                else:
                                    sum_runs(m, q, j)
                                    ago(m, q, j, 1, to_rows)

                        if relational:
                            turn(0, 0, 0)
                            turn(0, 0, 1)
                        steps(pe, step, 4, HALVES - 2, HALVES, 2)
                        if relational:
                            ago(HALVES, 0, 0, 1, sum_runs)
                            ago(HALVES, 0, 0, 2, to_rows)
                            ago(HALVES, 0, 1, 2, to_rows)
                        else:
                            ago(HALVES, 0, 0, 1, to_rows)
            clear(held)

        def dense_pass(k, source, result):
            held = []
            with ExitStack() as st:
                def buf(name, shape, dt=F32):
                    return st.enter_context(nc.sbuf_tensor(f"{name}_d{k}", shape, dt))

                def psem(name):
                    held.append(nc.alloc_semaphore(f"{name}_d{k}"))
                    return held[-1]

                node = buf("node", [P, SLOTS, BLOCK])
                term = buf("term", [P, SLOTS, BLOCK])
                base = buf("base", [P, SLOTS, BLOCK])
                done = buf("done", [P, SLOTS, BLOCK])
                ht = buf("ht_d", [P, 2, BLOCK])
                tmp = buf("tmp", [P, 2, BLOCK])
                pre = buf("pre", [P, 2, BLOCK])
                ht_ps = [st.enter_context(nc.psum_tensor(f"ht_ps{i}_d{k}", [P, BLOCK], F32)) for i in range(2)]
                z_ps = [st.enter_context(nc.psum_tensor(f"z_ps{i}_d{k}", [P, BLOCK], F32)) for i in range(2)]
                s_node = [psem(f"node{q}") for q in range(SLOTS)]
                s_x1 = [psem(f"x1_{q}") for q in range(SLOTS)]
                s_kept = [psem(f"stored{q}") for q in range(SLOTS)]
                s_turn, s_ht, s_z = psem("turned"), psem("ht"), psem("z")
                s_done = psem("done")
                s_passed = psem("dve_passed")
                s_pre, s_tenth, s_base = psem("pre"), psem("tenth"), psem("base")
                if k == 0:
                    st6 = buf("st6", [P, 2, NB, 6])
                    mv = buf("mv", [P, 2, NB, 2])
                    var = buf("var", [P, 2, NB])
                    std = buf("std", [P, 2, NB])
                    rstd = buf("rstd", [P, 2, NB])
                    shift = buf("shift", [P, 2, NB])
                    h = buf("h", [P, 2, BLOCK])
                    s_stat, s_mv, s_var = psem("stats"), psem("mean_var"), psem("var_eps")
                    s_std, s_rstd, s_shift, s_h = psem("std"), psem("rstd"), psem("shift"), psem("h")
                weight = w_enc[:] if k == 0 else w_r[:, k - 1, :]
                loads = 3 if k == 2 else 2
                lag = 3 if k == 0 else 2

                def use(m, q, n=1):
                    if isinstance(m, int):
                        return (m // SLOTS + 1) * n * DMA
                    return (m - q) * (n * DMA // SLOTS) + n * DMA

                def two_(m, q):
                    return q % 2

                with nc.Block() as block:
                    @block.sync
                    def _(sp):
                        def load(m, q):
                            if at_least(m, SLOTS):
                                if k == 0:
                                    sp.wait_ge(s_h, m - (SLOTS - 1))
                                    sp.wait_ge(s_base, m - (SLOTS - 1))
                                    sp.wait_ge(s_x1[q], use(m - SLOTS, q))
                                else:
                                    sp.wait_ge(s_turn, m - (SLOTS - 1))
                                    sp.wait_ge(s_done, m - (SLOTS - 1))
                            sp.dma_start(node[:, q, :], rows_of(source, base_of(m))).then_inc(s_node[q], DMA)
                            sp.dma_start(term[:, q, :], rows_of(agg[k], base_of(m))).then_inc(s_node[q], DMA)
                            if k == 2:
                                sp.dma_start(base[:, q, :], rows_of(x1, base_of(m))).then_inc(s_node[q], DMA)

                        def store(m, q, what, to, ready, landed):
                            sp.wait_ge(ready, m + 1)
                            if isinstance(m, int) and m == BLOCKS - 1:
                                sp.wait_ge(landed[(q - 1) % SLOTS], use(m - 1, (q - 1) % SLOTS))
                            sp.dma_start(rows_of(to, base_of(m)), what[:, q, :]).then_inc(landed[q], DMA)

                        def step(m, q):
                            if before(m, BLOCKS):
                                load(m, q)
                            if k == 0 and at_least(m, 2) and before(m, BLOCKS + 2):
                                store(m - 2, (q - 2) % SLOTS, base, x1, s_base, s_x1)
                            if at_least(m, lag + 2):
                                store(m - lag - 2, (q - lag - 2) % SLOTS, done, result, s_done, s_kept)

                        steps(sp, step, 2 * SLOTS, BLOCKS - SLOTS, BLOCKS + lag + 2, SLOTS)
                        for q in range(SLOTS):
                            sp.wait_ge(s_kept[q], DMA * BLOCKS // SLOTS)
                            if k == 0:
                                sp.wait_ge(s_x1[q], DMA * BLOCKS // SLOTS)

                    @block.tensor
                    def _(pe):
                        def turn(m, q):
                            if k == 0:
                                pe.wait_ge(s_h, m + 1)
                            else:
                                pe.wait_ge(s_node[q], use(m, q, loads))
                            if at_least(m, 2):
                                pe.wait_ge(s_ht, m - 1)
                            for j in range(NB):
                                a = h[:, q % 2, j * P:(j + 1) * P] if k == 0 else node[:, q, j * P:(j + 1) * P]
                                last = nc.tensor.transpose(ht_ps[q % 2][:, j * P:(j + 1) * P], a, ident[:])
                            last.then_inc(s_turn, 1)

                        def product(m, q):
                            pe.wait_ge(s_ht, m + 1)
                            if at_least(m, 2):
                                pe.wait_ge(s_done if k == 0 else s_pre, m - 1)
                            if k == 0:
                                nc.tensor.matmul(z_ps[q % 2][:], ones_bf[0:96, :], enc_parts[0:96, :, :],
                                                 start=True, stop=False)
                            for j in range(NB):
                                last = nc.tensor.matmul(z_ps[q % 2][:, j * P:(j + 1) * P], ht[:, q % 2, j * P:(j + 1) * P],
                                                        weight, start=(k > 0), stop=(k > 0 or j == NB - 1))
                            last.then_inc(s_z, 1)

                        def step(m, q):
                            if before(m, BLOCKS):
                                turn(m, q)
                            if at_least(m, 1):
                                product(m - 1, (q - 1) % SLOTS)

                        steps(pe, step, SLOTS, BLOCKS, BLOCKS + 1, SLOTS)

                    @block.scalar
                    def _(act):
                        def normalize(m, q):
                            s = q % 2
                            act.wait_ge(s_var, m + 1)
                            nc.scalar.activation(std[:, s, :], var[:, s, :], ACT.Sqrt).then_inc(s_std, 1)
                            act.wait_ge(s_shift, m + 1)
                            if at_least(m, 2):
                                act.wait_ge(s_turn, m - 1)
                            for j in range(NB):
                                last = nc.scalar.activation(h[:, s, j * P:(j + 1) * P], base[:, q, j * P:(j + 1) * P],
                                                            ACT.Relu, bias=shift[:, s, j:j + 1], scale=rstd[:, s, j:j + 1])
                            last.then_inc(s_h, 1)

                        def tenth(m, q):
                            act.wait_ge(s_z, m + 1)
                            if at_least(m, 2):
                                act.wait_ge(s_done, m - 1)
                            nc.scalar.activation(tmp[:, q % 2, :], z_ps[q % 2][:], ACT.Copy, scale=SLOPE).then_inc(s_tenth, 1)

                        def keep_turned(m, q):
                            act.wait_ge(s_turn, m + 1)
                            if at_least(m, 2):
                                act.wait_ge(s_z, m - 1)
                            nc.scalar.activation(ht[:, q % 2, :], ht_ps[q % 2][:], ACT.Copy).then_inc(s_ht, 1)

                        def step(m, q):
                            if k == 0 and before(m, BLOCKS):
                                normalize(m, q)
                            if k == 0 and at_least(m, 2):
                                tenth(m - 2, (q - 2) % SLOTS)
                            if before(m, BLOCKS):
                                keep_turned(m, q)

                        steps(act, step, SLOTS, BLOCKS, BLOCKS + (2 if k == 0 else 0), SLOTS)

                    @block.vector
                    def _(dve):
                        def prepare(m, q):
                            s = q % 2
                            dve.wait_ge(s_node[q], use(m, q, loads))
                            nc.vector.tensor_tensor(base[:, q, :], node[:, q, :], term[:, q, :], ALU.add).then_inc(s_base, 1)
                            dve.wait_ge(s_base, m + 1)
                            for j in range(NB):
                                nc.vector.bn_stats(st6[:, s, j, :], base[:, q, j * P:(j + 1) * P]).then_inc(s_stat, 1)
                            for j in range(NB):
                                wait_apart(dve, s_passed, (s_stat, m * NB + (j + 1)))
                                nc.vector.bn_aggr(mv[:, s, j, :], st6[:, s, j, :]).then_inc(s_mv, 1)
                            dve.wait_ge(s_mv, m * NB + NB)
                            nc.vector.tensor_scalar(var[:, s, :], mv[:, s, :, 1], EPS, None, ALU.add).then_inc(s_var, 1)

                        def scales(m, q):
                            s = q % 2
                            dve.wait_ge(s_std, m + 1)
                            if at_least(m, 2):
                                dve.wait_ge(s_h, m - 1)
                            nc.vector.reciprocal(rstd[:, s, :], std[:, s, :]).then_inc(s_rstd, 1)
                            dve.wait_ge(s_rstd, m + 1)
                            nc.vector.scalar_tensor_tensor(shift[:, s, :], mv[:, s, :, 0], -1.0, rstd[:, s, :],
                                                           ALU.mult, ALU.mult).then_inc(s_shift, 1)

                        def free(m, q):
                            if at_least(m, SLOTS):
                                dve.wait_ge(s_kept[q], use(m - SLOTS, q))

                        def leaky_enc(m, q):
                            dve.wait_ge(s_tenth, m + 1)
                            free(m, q)
                            nc.vector.tensor_tensor(done[:, q, :], z_ps[q % 2][:], tmp[:, q % 2, :],
                                                    ALU.max).then_inc(s_done, 1)

                        def add_term(m, q):
                            dve.wait_ge(s_z, m + 1)
                            nc.vector.tensor_tensor(pre[:, q % 2, :], z_ps[q % 2][:], term[:, q, :], ALU.add).then_inc(s_pre, 1)

                        def leaky(m, q):
                            dve.wait_ge(s_pre, m + 1)
                            to = done[:, q, :] if k == 1 else tmp[:, q % 2, :]
                            free(m, q)
                            nc.vector.scalar_tensor_tensor(to, pre[:, q % 2, :], SLOPE, pre[:, q % 2, :], ALU.mult,
                                                           ALU.max).then_inc(s_done if k == 1 else s_tenth, 1)
                            if k == 2:
                                dve.wait_ge(s_tenth, m + 1)
                                nc.vector.tensor_tensor(done[:, q, :], tmp[:, q % 2, :], base[:, q, :],
                                                        ALU.add).then_inc(s_done, 1)

                        def step(m, q):
                            if k == 0:
                                if before(m, BLOCKS):
                                    prepare(m, q)
                                if at_least(m, 3):
                                    leaky_enc(m - 3, (q - 3) % SLOTS)
                                if before(m, BLOCKS):
                                    scales(m, q)
                            else:
                                if before(m, BLOCKS + 1) and at_least(m, 1):
                                    add_term(m - 1, (q - 1) % SLOTS)
                                if at_least(m, 1):
                                    leaky(m - 1, (q - 1) % SLOTS)

                        steps(dve, step, 2 * SLOTS, BLOCKS, BLOCKS + (3 if k == 0 else 1), SLOTS)
            clear(held)

        edge_pass(0, x)
        dense_pass(0, x, g[0])
        edge_pass(1, g[0])
        dense_pass(1, g[0], g[1])
        edge_pass(2, g[1])
        dense_pass(2, g[1], out)


_INS = ['x', 'src', 'dst', 'edge_type_16', 'L0_gnn_weight', 'L0_gnn_w_comp', 'L0_gnn_h_bias', 'L1_gnn_enc_w',
        'L1_gnn_enc_b', 'L1_gnn_lin_l_w', 'L1_gnn_lin_l_b', 'L1_gnn_lin_r_w']
_OUTS = [((100000, 128), 'float32')]


def kernel(**inputs):
    import numpy as _np
    import concourse.bacc as _bacc
    from concourse import mybir as _mybir
    from concourse.bass_utils import run_bass_kernel_spmd as _run

    nc = _bacc.Bacc("TRN2", target_bir_lowering=False, num_devices=1)
    arrays, args = {}, []
    for name in _INS:
        a = _np.ascontiguousarray(inputs[name])
        arrays[f"in_{name}_dram"] = a
        args.append(nc.dram_tensor(f"in_{name}_dram", a.shape, _mybir.dt.from_np(a.dtype), kind="ExternalInput").ap())
    for i, (shape, dtype) in enumerate(_OUTS):
        dt = _mybir.dt.from_np(_np.dtype(dtype))
        args.append(nc.dram_tensor(f"out_{i}_dram", shape, dt, kind="ExternalOutput").ap())
    gnn_kernel(nc, *args)
    r = _run(nc, [arrays], core_ids=[0])
    got = tuple(r.results[0][f"out_{i}_dram"] for i in range(len(_OUTS)))
    return got[0]
```

```python
import concourse.bass as bass
from concourse import mybir
from contextlib import ExitStack

F32 = mybir.dt.float32
BF16 = mybir.dt.bfloat16
I32 = mybir.dt.int32
ALU = mybir.AluOpType
ACT = mybir.ActivationFunctionType
AX = mybir.AxisListType

P = 128
EPS = 1e-5
SLOPE = 0.1
DMA = 16

HALF = 7
ROW = 4 * P
NB = 4
BLOCK = NB * P
SLOTS = 4
WALK = 7
LAST = 8 * P
FILL = 16 * P
BASES_ON_ACT = 2


def at_least(m, n):
    return not isinstance(m, int) or m >= n


def before(m, n):
    return not isinstance(m, int) or m < n


def wait_apart(eng, passed, *waits):
    for semaphore, value in waits:
        eng.wait_ge(semaphore, value)
    eng.sem_inc(passed, 1)


def steps(eng, step, head, tail, total, unroll):
    for m in range(head):
        step(m, m % unroll, m // unroll)
    with eng.Fori(head // unroll, tail // unroll) as i:
        for u in range(unroll):
            step(i * unroll + u, u, i)
    for m in range(tail, total):
        step(m, m % unroll, m // unroll)


def gnn_kernel(nc, x, src, dst, etype, basis_w, w_comp, h_bias, enc_w, enc_b, lin_l_w, lin_l_b,
               lin_r_w, out):
    N = x.shape[0]
    E = src.shape[0]
    R, B = w_comp.shape
    ROWS = -(-E // ROW)
    EP = ROWS * ROW
    T = EP // P
    HALVES = T // HALF
    NOWHERE = 2 * N
    BLOCKS = -(-N // BLOCK)
    LAST_BASE = N - BLOCK
    FILLS = -(-N // FILL)
    assert T % (2 * HALF) == 0 and BLOCKS % SLOTS == 0 and ROWS <= P and FILLS < HALVES - 2
    Y = B * P

    ctx = ExitStack()
    with ctx:
        def sb(name, shape, dt=F32):
            return ctx.enter_context(nc.sbuf_tensor(name, shape, dt))

        def sem(name):
            return ctx.enter_context(nc.semaphore(name))

        def dram(name, shape, dt=F32):
            return nc.dram_tensor(name, shape, dt).ap()

        src_s = dram("src_sorted", [EP], I32)
        dst_s = dram("dst_sorted", [EP], I32)
        typ_s = dram("type_sorted", [EP], I32)
        src_u = dram("src_padded", [EP], I32)
        dst_u = dram("dst_padded", [EP], I32)
        typ_u = dram("type_padded", [EP], I32)
        dst_f = dram("dst_float", [EP + 2])
        agg = dram("agg", [N, P])
        x1 = dram("x1", [N, P])
        g0 = dram("g0", [N, P])
        z = [dram(f"z{k}", [N + 2 * HALF * P, P]) for k in range(2)]
        spill = dram("means_by_edge", [HALVES, P, HALF * P])

        ident = sb("ident", [P, P])
        ones = sb("ones", [P, P])
        bias_row = sb("bias_row", [P, P])
        fill_rows = sb("fill_rows", [P, FILL // P * P])
        w_basis = sb("w_basis", [P, B, P])
        w_enc = sb("w_enc", [P, P])
        w_l = sb("w_l", [P, 2, P])
        w_r = sb("w_r", [P, 2, P])
        hb_col = sb("hb_col", [P, 1])
        comp = sb("comp", [P, R * B])
        bias_parts = sb("bias_parts", [P, 3, P], BF16)
        bias_rest = sb("bias_rest", [P, 2, 3, P])
        bias_tmp = sb("bias_tmp", [P, 3, P], BF16)
        ones_bf = sb("ones_bf", [P, P], BF16)
        dst_c = sb("dst_c", [P, T])
        src_c = sb("src_c", [P, T], I32)
        put_c = sb("put_c", [P, T], I32)
        typ_c = sb("typ_c", [P, T])
        inv_c = sb("inv_c", [P, T])
        coef = sb("coef", [P, T, B])

        def rows_of(ap, first):
            return ap[bass.ds(first, BLOCK), :].rearrange("(p j) f -> p (j f)", p=P)

        def fill_of(ap, first):
            return ap[bass.ds(first, FILL), :].rearrange("(p j) f -> p (j f)", p=P)

        def base_of(m):
            return LAST_BASE if isinstance(m, int) and m == BLOCKS - 1 else m * BLOCK

        with ExitStack() as st:
            W = E // 100
            assert W * 100 == E
            cur = st.enter_context(nc.sbuf_tensor("dst_cur", [100, W], I32))
            nxt = st.enter_context(nc.sbuf_tensor("dst_nxt", [100, W], I32))
            down = st.enter_context(nc.sbuf_tensor("down", [100, W], F32))
            downs = st.enter_context(nc.sbuf_tensor("downs", [P, 1], F32))
            unsorted = st.enter_context(nc.sbuf_tensor("unsorted", [1, 1], I32))
            pad = st.enter_context(nc.sbuf_tensor("pad", [1, 2, EP - E], I32))
            ends = st.enter_context(nc.sbuf_tensor("ends", [1, 2], F32))
            total = st.enter_context(nc.psum_tensor("total", [1, 1], F32))
            s_w = sem("weights_loaded")
            s_set = sem("dve_set")
            s_id0, s_id1 = sem("ident_zeroed"), sem("ident_made")
            s_dst = sem("dst_loaded")
            s_pads = sem("pads_set")
            s_padded = sem("pads_stored")
            s_bias = sem("bias_loaded")
            s_downs = sem("downs_counted")
            s_total = sem("downs_totalled")
            with nc.Block() as block:
                @block.sync
                def _(sp):
                    sp.wait_ge(s_set, 1)
                    sp.dma_start(cur[:], dst.rearrange("(p w) -> p w", w=W)).then_inc(s_dst, DMA)
                    sp.dma_start(nxt[0:99, :], dst[1:1 + 99 * W].rearrange("(p w) -> p w", w=W)).then_inc(s_dst, DMA)
                    sp.dma_start(nxt[99:100, 0:W - 1], dst[1 + 99 * W:E].unsqueeze(0)).then_inc(s_dst, DMA)
                    sp.dma_start(bias_row[:], h_bias.partition_broadcast(P)).then_inc(s_bias, DMA)
                    sp.wait_ge(s_set, 2)
                    for r in range(3):
                        for k, b in enumerate((enc_b, lin_l_b[0, :], lin_l_b[1, :])):
                            sp.dma_start(bias_rest[32 * r:32 * r + 1, 0, k, :], b.unsqueeze(0)).then_inc(s_bias, DMA)
                    sp.dma_start(hb_col[:], h_bias.unsqueeze(1)).then_inc(s_w, DMA)
                    sp.dma_start(comp[:], w_comp.rearrange("r b -> (r b)").partition_broadcast(P)).then_inc(s_w, DMA)
                    sp.dma_start(w_basis[:], basis_w.rearrange("b i o -> i b o")).then_inc(s_w, DMA)
                    sp.dma_start(w_enc[:], enc_w).then_inc(s_w, DMA)
                    sp.dma_start(w_l[:], lin_l_w.rearrange("l i o -> i l o")).then_inc(s_w, DMA)
                    sp.dma_start(w_r[:], lin_r_w.rearrange("l i o -> i l o")).then_inc(s_w, DMA)
                    sp.wait_ge(s_pads, 4)
                    for k, arrays in enumerate(((src_s, typ_s, src_u, typ_u), (dst_s, dst_u))):
                        for a in arrays:
                            sp.dma_start(a[E:EP].unsqueeze(0), pad[:, k, :]).then_inc(s_padded, DMA)
                    sp.dma_start(dst_f[0:1].unsqueeze(0), ends[:, 0:1]).then_inc(s_padded, DMA)
                    sp.dma_start(dst_f[EP + 1:EP + 2].unsqueeze(0), ends[:, 1:2]).then_inc(s_padded, DMA)
                    sp.wait_ge(s_w, 6 * DMA)
                    sp.wait_ge(s_padded, 8 * DMA)
                @block.gpsimd
                def _(pool):
                    nc.gpsimd.memset(ident[:], 0.0).then_inc(s_id0, 1)
                    pool.wait_ge(s_id0, 1)
                    nc.gpsimd.affine_select(out=ident[:], in_=ident[:], compare_op=ALU.not_equal, fill=1.0, base=0,
                                            pattern=[[-1, P]], channel_multiplier=1).then_inc(s_id1, 1)

                @block.vector
                def _(dve):
                    chain = [2]

                    def link(ins):
                        chain[0] += 1
                        ins.then_inc(s_set, 1)
                        dve.wait_ge(s_set, chain[0])

                    nc.vector.memset(nxt[:], NOWHERE).then_inc(s_set, 1)
                    nc.vector.memset(bias_rest[:], 0.0).then_inc(s_set, 1)
                    link(nc.vector.memset(ones[:], 1.0))
                    link(nc.vector.memset(ones_bf[:], 1.0))
                    link(nc.vector.memset(downs[:], 0.0))
                    nc.vector.memset(pad[:, 0, :], 0).then_inc(s_pads, 1)
                    nc.vector.memset(pad[:, 1, :], NOWHERE).then_inc(s_pads, 1)
                    nc.vector.memset(ends[:, 0:1], -1.0).then_inc(s_pads, 1)
                    nc.vector.memset(ends[:, 1:2], float(2 * NOWHERE)).then_inc(s_pads, 1)
                    dve.wait_ge(s_dst, 3 * DMA)
                    link(nc.vector.tensor_tensor(down[:], nxt[:], cur[:], ALU.is_lt))
                    nc.vector.reduce_sum(downs[0:100, :], down[:], AX.X).then_inc(s_downs, 1)
                    dve.wait_ge(s_bias, 10 * DMA)
                    link(nc.vector.tensor_copy(fill_rows[:].rearrange("p (j f) -> p j f", f=P),
                                               bias_row[:].unsqueeze(1).to_broadcast([P, FILL // P, P])))
                    link(nc.vector.memset(bias_parts[:], 0.0))
                    for r in range(3):
                        link(nc.vector.tensor_copy(bias_tmp[:], bias_rest[:, r % 2, :, :]))
                        link(nc.vector.tensor_copy(bias_parts[32 * r:32 * r + 1, :, :], bias_tmp[32 * r:32 * r + 1, :, :]))
                        link(nc.vector.tensor_tensor(bias_rest[:, 1 - r % 2, :, :], bias_rest[:, r % 2, :, :], bias_tmp[:],
                                                     ALU.subtract))
                    dve.wait_ge(s_total, 1)
                    link(nc.vector.tensor_copy(unsorted[:], total[:]))

                @block.tensor
                def _(pe):
                    pe.wait_ge(s_downs, 1)
                    nc.tensor.matmul(total[:], downs[:], ones[:, 0:1], start=True, stop=True).then_inc(s_total, 1)

            CH = EP // 8
            GROUP = 8
            row_i = st.enter_context(nc.sbuf_tensor("row_i", [P, CH], I32))
            row_f = st.enter_context(nc.sbuf_tensor("row_f", [P, CH], F32))
            frac = st.enter_context(nc.sbuf_tensor("frac", [P, CH], F32))
            gap = st.enter_context(nc.sbuf_tensor("gap", [P, CH], F32))
            hit = st.enter_context(nc.sbuf_tensor("hit", [P, CH], BF16))
            cols_u = st.enter_context(nc.sbuf_tensor("cols_u", [P, 3, T], I32))
            dcol = st.enter_context(nc.sbuf_tensor("dcol", [P, T], F32))
            thr_i = st.enter_context(nc.sbuf_tensor("thr_i", [P, T], I32))
            thr = st.enter_context(nc.sbuf_tensor("thr", [P, 2, T], F32))
            below = st.enter_context(nc.sbuf_tensor("below", [P, T], F32))
            rank = st.enter_context(nc.sbuf_tensor("rank", [P, 2, T], F32))
            rank_i = st.enter_context(nc.sbuf_tensor("rank_i", [P, T], I32))
            stage = st.enter_context(nc.sbuf_tensor("stage", [P, 4, GROUP], I32))
            s_u = sem("padded_copied")
            s_cols = sem("columns_loaded")
            s_iota = sem("iotas_made")
            s_row = sem("row_loaded")
            s_rowused = sem("row_used")
            s_rk = sem("rank_steps")
            s_ranked = sem("ranked")
            s_staged = sem("staged")
            s_spread = [sem(f"spread{k}") for k in range(3)]
            s_direct = sem("sorted_copied")
            s_passed = sem("waits_passed")
            with nc.Block() as block:
                @block.sync
                def _(sp):
                    flag = sp.value_load(unsorted[0:1, 0:1], min_val=0, max_val=E)
                    with sp.If(flag != 0):
                        for a, b in ((src, src_u), (dst, dst_u), (etype, typ_u)):
                            sp.dma_start(b[0:E], a).then_inc(s_u, DMA)
                        sp.wait_ge(s_u, 3 * DMA)
                        with nc.allow_non_contiguous_dma(reason="edges into columns, in the rare order"):
                            for k, a in enumerate((dst_u, src_u, typ_u)):
                                sp.dma_start(cols_u[:, k, :], a.rearrange("(t p) -> p t", p=P)).then_inc(s_cols, DMA)
                        for c in range(8):
                            if c:
                                sp.wait_ge(s_rowused, c)
                            sp.dma_start(row_i[:], dst_u[c * CH:(c + 1) * CH].partition_broadcast(P)).then_inc(s_row, DMA)
                            sp.wait_ge(s_row, DMA * (c + 1))
                        sp.wait_ge(s_cols, 3 * DMA)
                    with sp.Else():
                        for a, b in ((src, src_s), (dst, dst_s), (etype, typ_s)):
                            sp.dma_start(b[0:E], a).then_inc(s_direct, DMA)
                        sp.wait_ge(s_direct, 3 * DMA)
                    sp.drain()

                @block.vector
                def _(dve):
                    flag = dve.value_load(unsorted[0:1, 0:1], min_val=0, max_val=E)
                    with dve.If(flag != 0):
                        dve.wait_ge(s_iota, 2)
                        nc.vector.tensor_scalar(thr[:, 0, :], thr_i[:], 1.0 / 65536, None, ALU.mult).then_inc(s_rk, 1)
                        nc.vector.tensor_scalar(frac[:], gap[:].bitcast(I32), 1.0 / 65536, None, ALU.mult).then_inc(s_rk, 1)
                        dve.wait_ge(s_cols, 3 * DMA)
                        nc.vector.tensor_copy(dcol[:], cols_u[:, 0, :]).then_inc(s_rk, 1)
                        nc.vector.memset(rank[:, 0, :], 0.0).then_inc(s_rk, 1)
                        done = 4
                        for c in range(8):
                            a, b = c % 2, 1 - c % 2
                            dve.wait_ge(s_rk, done)
                            dve.wait_ge(s_row, DMA * (c + 1))
                            nc.vector.tensor_copy(row_f[:], row_i[:]).then_inc(s_rowused, 1)
                            dve.wait_ge(s_rowused, c + 1)
                            with dve.Fori(0, T) as t:
                                nc.vector.scalar_tensor_tensor(gap[:], row_f[:], dcol[:, bass.ds(t, 1)], frac[:],
                                                               ALU.subtract, ALU.add).then_inc(s_rk, 1)
                                dve.wait_ge(s_rk, t * 2 + (done + 1))
                                nc.vector.tensor_scalar(hit[:], gap[:], thr[:, a, bass.ds(t, 1)], None, ALU.is_lt,
                                                        ALU.add, accum_out=below[:, bass.ds(t, 1)]).then_inc(s_rk, 1)
                                dve.wait_ge(s_rk, t * 2 + (done + 2))
                            done += 2 * T
                            nc.vector.tensor_tensor(rank[:, b, :], rank[:, a, :], below[:], ALU.add).then_inc(s_rk, 1)
                            nc.vector.tensor_scalar(thr[:, b, :], thr[:, a, :], -CH / 65536, None, ALU.add).then_inc(s_rk, 1)
                            done += 2
                        dve.wait_ge(s_rk, done)
                        nc.vector.tensor_copy(rank_i[:], rank[:, 0, :]).then_inc(s_ranked, 1)
                        dve.wait_ge(s_ranked, 1)
                    dve.drain()

                @block.gpsimd
                def _(pool):
                    flag = pool.value_load(unsorted[0:1, 0:1], min_val=0, max_val=E)
                    with pool.If(flag != 0):
                        nc.gpsimd.iota(thr_i[:], [[P, T]], base=0, channel_multiplier=1).then_inc(s_iota, 1)
                        nc.gpsimd.iota(gap[:].bitcast(I32), [[1, CH]], base=0, channel_multiplier=0).then_inc(s_iota, 1)
                        pool.wait_ge(s_ranked, 1)
                        pool.wait_ge(s_cols, 3 * DMA)
                        with pool.Fori(0, T // GROUP) as i:
                            col = bass.ds(i * GROUP, GROUP)
                            nc.gpsimd.tensor_copy(stage[:, 3, :], rank_i[:, col]).then_inc(s_staged, 1)
                            for k in range(3):
                                nc.gpsimd.tensor_copy(stage[:, k, :], cols_u[:, k, col]).then_inc(s_staged, 1)
                            wait_apart(pool, s_passed, (s_staged, i * 4 + 4))
                            for k, a in enumerate((dst_s, src_s, typ_s)):
                                for c in range(GROUP):
                                    nc.gpsimd.indirect_dma_start(
                                        a.unsqueeze(1), bass.IndirectOffsetOnAxis(ap=stage[:, 3, c:c + 1], axis=0),
                                        stage[:, k, c:c + 1], None).then_inc(s_spread[k], DMA)
                            wait_apart(pool, s_passed, *[(s_spread[k], i * (DMA * GROUP) + DMA * GROUP) for k in range(3)])
                    pool.drain()

        with ExitStack() as st:
            def row(name, dt=F32):
                return st.enter_context(nc.sbuf_tensor(name, [P, ROW], dt))

            src_i, dst_i, typ_i = row("src_i", I32), row("dst_i", I32), row("typ_i", I32)
            here, prev, succ = row("here"), row("prev"), row("succ")
            index_i, index = row("index_i", I32), row("index")
            starts, first, first_in = row("starts"), row("first"), row("first_in")
            firsts, degree, inverse = row("firsts"), row("degree"), row("inverse")
            ends_run, is_node = row("ends_run"), row("is_node")
            src_r, typ_r, kept = row("src_r"), row("typ_r"), row("kept")
            carry = st.enter_context(nc.sbuf_tensor("carry", [1, 2, P], F32))
            carry_col = st.enter_context(nc.sbuf_tensor("carry_col", [P, 1], F32))
            aside_i = st.enter_context(nc.sbuf_tensor("aside_i", [P, T], I32))
            aside = st.enter_context(nc.sbuf_tensor("aside", [P, T], F32))
            kept_c = st.enter_context(nc.sbuf_tensor("kept_c", [P, T], F32))
            ahead = st.enter_context(nc.sbuf_tensor("ahead", [P, T], F32))
            moved = st.enter_context(nc.sbuf_tensor("moved", [P, T], F32))
            zeros = st.enter_context(nc.sbuf_tensor("zeros", [P, 2 * HALF * P], F32))
            onehot = st.enter_context(nc.sbuf_tensor("onehot", [P, R, T], F32))
            turned = [st.enter_context(nc.psum_tensor(f"turned{k}", [P, 4, P], F32)) for k in range(5)]
            carry_ps = st.enter_context(nc.psum_tensor("carry_ps", [1, P], F32))
            carry_back = st.enter_context(nc.psum_tensor("carry_back", [P, 1], F32))
            s_rows = sem("rows_loaded")
            s_filled = sem("agg_filled")
            s_zero = sem("rows_zeroed")
            s_index = sem("index_made")
            s_here = sem("here_made")
            s_dstf = sem("dst_float_stored")
            s_shift = sem("shifts_loaded")
            s_v = sem("row_steps")
            s_lastcol = sem("last_column")
            s_carry = sem("carry_turned")
            s_scan = sem("carry_scanned")
            s_back = sem("carry_back_turned")
            s_ready = sem("row_ready")
            s_turned = sem("row_turned")
            s_col = sem("columns_made")
            s_one = sem("onehots")
            s_coef = sem("coef_steps")
            s_aside = sem("aside_stored")
            order = [src_r, here, kept, typ_r, inverse]

            with nc.Block() as block:
                @block.scalar
                def _(act):
                    with act.Fori(0, FILLS - 1) as m:
                        act.dma_start(fill_of(agg, m * FILL), fill_rows[:]).then_inc(s_filled, DMA)
                    act.wait_ge(s_filled, DMA * (FILLS - 1))
                    act.dma_start(fill_of(agg, N - FILL), fill_rows[:]).then_inc(s_filled, DMA)
                    act.wait_ge(s_filled, DMA * FILLS)

                @block.sync
                def _(sp):
                    sp.wait_ge(s_zero, 3)
                    for a, b in ((dst_s, dst_i), (src_s, src_i), (typ_s, typ_i)):
                        sp.dma_start(b[0:ROWS, :], a.rearrange("(r k) -> r k", k=ROW)).then_inc(s_rows, DMA)
                    sp.wait_ge(s_here, 1)
                    sp.dma_start(dst_f[1:1 + EP].rearrange("(r k) -> r k", k=ROW), here[0:ROWS, :]).then_inc(s_dstf, DMA)
                    sp.wait_ge(s_dstf, DMA)
                    sp.wait_ge(s_zero, 5)
                    sp.dma_start(prev[0:ROWS, :], dst_f[0:EP].rearrange("(r k) -> r k", k=ROW)).then_inc(s_shift, DMA)
                    sp.dma_start(succ[0:ROWS, :], dst_f[2:2 + EP].rearrange("(r k) -> r k", k=ROW)).then_inc(s_shift, DMA)
                    sp.wait_ge(s_zero, 6)
                    for a in z:
                        sp.dma_start(a[N:N + 2 * HALF * P, :].rearrange("(p s) f -> p (s f)", p=P), zeros[:]).then_inc(s_aside, DMA)
                    sp.wait_ge(s_aside, 2 * DMA)

                @block.gpsimd
                def _(pool):
                    nc.gpsimd.iota(aside_i[:], [[0, T // (2 * HALF)], [P, 2 * HALF]], base=N,
                                   channel_multiplier=1).then_inc(s_index, 1)
                    nc.gpsimd.iota(index_i[:], [[1, ROW]], base=0, channel_multiplier=ROW).then_inc(s_index, 1)

                @block.vector
                def _(dve):
                    chain = [0]

                    def link(ins):
                        chain[0] += 1
                        ins.then_inc(s_v, 1)
                        dve.wait_ge(s_v, chain[0])

                    for a in (dst_i, src_i, typ_i, prev, succ, zeros):
                        nc.vector.memset(a[:], 0).then_inc(s_zero, 1)
                    dve.wait_ge(s_zero, 6)
                    dve.wait_ge(s_rows, 3 * DMA)
                    nc.vector.tensor_copy(here[:], dst_i[:]).then_inc(s_here, 1)
                    dve.wait_ge(s_here, 1)
                    link(nc.vector.tensor_copy(src_r[:], src_i[:]))
                    link(nc.vector.tensor_copy(typ_r[:], typ_i[:]))
                    dve.wait_ge(s_index, 2)
                    link(nc.vector.tensor_copy(index[:], index_i[:]))
                    dve.wait_ge(s_shift, 2 * DMA)
                    link(nc.vector.tensor_tensor(starts[:], here[:], prev[:], ALU.not_equal))
                    link(nc.vector.tensor_tensor(first_in[:], starts[:], index[:], ALU.mult))
                    link(nc.vector.tensor_tensor_scan(first[:], first_in[:], first_in[:], 0.0, ALU.max, ALU.max))
                    dve.wait_ge(s_v, chain[0])
                    nc.vector.tensor_copy(carry_col[:], first[:, ROW - 1:ROW]).then_inc(s_lastcol, 1)
                    dve.wait_ge(s_carry, 1)
                    link(nc.vector.memset(carry[:, 1, 0:1], 0.0))
                    link(nc.vector.tensor_copy(carry[:, 0, :], carry_ps[:]))
                    link(nc.vector.tensor_tensor_scan(carry[:, 1, 1:P], carry[:, 0, 0:P - 1], carry[:, 0, 0:P - 1], 0.0,
                                                      ALU.max, ALU.max))
                    nc.vector.drain().then_inc(s_scan, 1)
                    dve.wait_ge(s_back, 1)
                    link(nc.vector.tensor_copy(carry_col[:], carry_back[:]))
                    link(nc.vector.tensor_scalar(firsts[:], first[:], carry_col[:], None, ALU.max))
                    link(nc.vector.tensor_tensor(degree[:], index[:], firsts[:], ALU.subtract))
                    link(nc.vector.tensor_scalar(degree[:], degree[:], 1.0, None, ALU.add))
                    link(nc.vector.reciprocal(inverse[:], degree[:]))
                    link(nc.vector.tensor_tensor(ends_run[:], here[:], succ[:], ALU.not_equal))
                    link(nc.vector.tensor_scalar(is_node[:], here[:], float(N), None, ALU.is_lt))
                    link(nc.vector.tensor_tensor(kept[:], ends_run[:], is_node[:], ALU.mult))
                    nc.vector.drain().then_inc(s_ready, 1)
                    for k, col in enumerate((src_c, dst_c, kept_c, typ_c, inv_c)):
                        dve.wait_ge(s_turned, k + 1)
                        nc.vector.tensor_copy(col[:].rearrange("p (r c) -> p c r", c=4),
                                              turned[k][:, :, 0:ROWS]).then_inc(s_col, 1)
                    dve.wait_ge(s_col, 5)
                    link(nc.vector.tensor_copy(aside[:], aside_i[:]))
                    link(nc.vector.tensor_tensor(ahead[:], dst_c[:], aside[:], ALU.subtract))
                    link(nc.vector.tensor_tensor(moved[:], ahead[:], kept_c[:], ALU.mult))
                    link(nc.vector.tensor_tensor(put_c[:], moved[:], aside[:], ALU.add))
                    for r in range(R):
                        nc.vector.tensor_scalar(onehot[:, r, :], typ_c[:], float(r), None, ALU.is_equal).then_inc(s_one, 1)
                    for r in range(R):
                        dve.wait_ge(s_one, r + 1)
                        for b in range(B):
                            w = comp[:, r * B + b:r * B + b + 1]
                            if r == 0:
                                nc.vector.tensor_scalar(coef[:, :, b], onehot[:, r, :], w, None, ALU.mult).then_inc(s_coef, 1)
                            else:
                                dve.wait_ge(s_coef, B * (r - 1) + b + 1)
                                nc.vector.scalar_tensor_tensor(coef[:, :, b], onehot[:, r, :], w, coef[:, :, b],
                                                               ALU.mult, ALU.add).then_inc(s_coef, 1)

                @block.tensor
                def _(pe):
                    pe.wait_ge(s_lastcol, 1)
                    nc.tensor.matmul(carry_ps[:], carry_col[:], ident[:], start=True, stop=True).then_inc(s_carry, 1)
                    pe.wait_ge(s_scan, 1)
                    nc.tensor.matmul(carry_back[:], carry[:, 1, :], ones[0:1, 0:1], start=True, stop=True).then_inc(s_back, 1)
                    pe.wait_ge(s_ready, 1)
                    for k, a in enumerate(order):
                        for c in range(4):
                            last = nc.tensor.transpose(turned[k][:, c, :], a[:, c * P:(c + 1) * P], ident[:])
                        last.then_inc(s_turned, 1)

        def clear(held):
            nc.clear_and_free_semaphores(held)
            nc.all_engine_barrier()

        def relational_pass():
            held = []
            lag = 3
            with ExitStack() as st:
                def buf(name, shape, dt=F32):
                    return st.enter_context(nc.sbuf_tensor(f"{name}_rel", shape, dt))

                def bank(name, shape):
                    return st.enter_context(nc.psum_tensor(f"{name}_rel", shape, F32))

                def psem(name):
                    held.append(nc.alloc_semaphore(f"{name}_rel"))
                    return held[-1]

                gat = buf("gat", [P, 2, HALF, P])
                rows = buf("rows", [P, 2, HALF, P])
                gidx = buf("gidx", [P, 2, HALF], I32)
                pidx = buf("pidx", [P, 2, HALF], I32)
                dst_b = buf("dst_b", [P, 2, HALF * P + 1])
                same = buf("same", [P, 2, HALF, P])
                open_ = buf("open", [P, 2, HALF, P])
                sums = buf("sums", [P, HALF, P])
                sum_ps = [bank(f"sum_ps{i}", [P, 512]) for i in range(2)]
                row_ps = bank("row_ps", [P, 512])
                s_gathered = [[psem(f"gathered{q}{j}") for j in range(HALF)] for q in range(2)]
                s_scattered = [[psem(f"scattered{q}{j}") for j in range(HALF)] for q in range(2)]
                s_gidx, s_pidx = psem("gather_index"), psem("scatter_index")
                s_dstb = [psem(f"dst_b{q}") for q in range(2)]
                s_same, s_open = psem("same_made"), psem("open_made")
                s_summed = psem("summed")
                s_carried = psem("carried")
                s_rowed = psem("rowed")
                s_rows = psem("rows_ready")
                s_start = psem("carry_zeroed")
                s_passed, s_dve_passed = psem("pool_passed"), psem("dve_passed")
                st6 = buf("st6", [P, 2, HALF, 6])
                mv = buf("mv", [P, 2, HALF, 2])
                var = buf("var", [P, 2, HALF])
                std = buf("std", [P, 2, HALF])
                rstd = buf("rstd", [P, 2, HALF])
                shift = buf("shift", [P, 2, HALF])
                h = buf("h", [P, 2, HALF, P])
                ht = buf("ht", [P, 2, HALF, P])
                part = buf("part", [P, 2, BASES_ON_ACT, P])
                two = buf("two", [P, HALF, 2, P])
                sums_b = buf("sums_b", [P, HALF, P])
                y_ps = [bank(f"y_ps{i}", [P, Y]) for i in range(2)]
                ht_ps = bank("ht_ps", [P, 512])
                s_stat, s_mv, s_var = psem("stats"), psem("mean_var"), psem("var_eps")
                s_std, s_rstd, s_shift = psem("std"), psem("rstd"), psem("shift")
                s_h, s_turn, s_ht = psem("h"), psem("turned"), psem("ht")
                s_y_high, s_y, s_part, s_acc = psem("y_high"), psem("y"), psem("part"), psem("acc")
                s_biased = psem("biased")

                def tile(m, j):
                    return m * HALF + (j + 1)

                def use(m, q):
                    return (m // 2 + 1) * DMA if isinstance(m, int) else (m - q) * (DMA // 2) + DMA

                def group(m, a):
                    return m * 2 + (a + 1)

                def ago(m, q, j, n, what):
                    if j >= n:
                        what(m, q, j - n)
                    elif at_least(m, 1):
                        what(m - 1, 1 - q, HALF + j - n)

                with nc.Block() as block:
                    @block.gpsimd
                    def _(pool):
                        def step(m, q, i):
                            if before(m, HALVES):
                                if at_least(m, 2):
                                    pool.wait_ge(s_h, tile(m - 2, HALF - 1))
                                nc.gpsimd.tensor_copy(gidx[:, q, :], src_c[:, bass.ds(m * HALF, HALF)]).then_inc(s_gidx, 1)
                            if at_least(m, lag):
                                o, oq = m - lag, (q - lag) % 2
                                if at_least(m, lag + 2):
                                    for j in range(HALF):
                                        pool.wait_ge(s_scattered[oq][j], use(o - 2, oq))
                                nc.gpsimd.tensor_copy(pidx[:, oq, :], put_c[:, bass.ds(o * HALF, HALF)]).then_inc(s_pidx, 1)
                            wait_apart(pool, s_passed, *[(s_gidx, m + 1)] * before(m, HALVES),
                                       *[(s_pidx, m + (1 - lag))] * at_least(m, lag))
                            for j in range(HALF):
                                if before(m, HALVES):
                                    nc.gpsimd.indirect_dma_start(
                                        gat[:, q, j, :], None, x,
                                        bass.IndirectOffsetOnAxis(ap=gidx[:, q, j:j + 1], axis=0)).then_inc(s_gathered[q][j], DMA)
                                if at_least(m, lag):
                                    wait_apart(pool, s_passed, (s_rows, tile(o, j)))
                                    nc.gpsimd.indirect_dma_start(
                                        agg, bass.IndirectOffsetOnAxis(ap=pidx[:, oq, j:j + 1], axis=0),
                                        rows[:, oq, j, :], None, bounds_check=N - 1,
                                        oob_is_err=False).then_inc(s_scattered[oq][j], DMA)

                        steps(pool, step, 6, HALVES, HALVES + lag, 2)
                        for q in range(2):
                            for j in range(HALF):
                                pool.wait_ge(s_scattered[q][j], DMA * HALVES // 2)

                    @block.sync
                    def _(sp):
                        def step(m, q, i):
                            if at_least(m, 2):
                                sp.wait_ge(s_same, m - 1)
                                sp.wait_ge(s_open, m - 1)
                            sp.dma_start(dst_b[:, q, :], dst_f[bass.ds(m * (HALF * P), HALF * P + 1)]
                                         .partition_broadcast(P)).then_inc(s_dstb[q], DMA)

                        steps(sp, step, 4, HALVES, HALVES, 2)

                    @block.vector
                    def _(dve):
                        nc.vector.memset(sums[:, HALF - 1, :], 0.0).then_inc(s_start, 1)
                        dve.wait_ge(s_start, 1)

                        def columns(q):
                            return dst_b[:, q, 1:HALF * P + 1].rearrange("p (t e) -> p t e", e=P)

                        def select(m, q):
                            dve.wait_ge(s_dstb[q], use(m, q))
                            if at_least(m, 2):
                                dve.wait_ge(s_summed, tile(m - 2, HALF - 1))
                            nc.vector.tensor_tensor(same[:, q, :, :], columns(q),
                                                    dst_c[:, bass.ds(m * HALF, HALF)].unsqueeze(2).to_broadcast([P, HALF, P]),
                                                    ALU.is_equal).then_inc(s_same, 1)

                        def find_open(m, q):
                            dve.wait_ge(s_dstb[q], use(m, q))
                            if at_least(m, 2):
                                dve.wait_ge(s_carried, tile(m - 2, HALF - 1))
                            before_ = dst_b[:, q, 0:HALF * P].rearrange("p (t e) -> p t e", e=P)[:, :, 0:1]
                            nc.vector.tensor_tensor(open_[:, q, :, :], columns(q), before_.to_broadcast([P, HALF, P]),
                                                    ALU.is_equal).then_inc(s_open, 1)

                        def stats(m, q, lo, hi):
                            for j in range(lo, hi):
                                dve.wait_ge(s_gathered[q][j], use(m, q))
                                nc.vector.bn_stats(st6[:, q, j, :], gat[:, q, j, :]).then_inc(s_stat, 1)

                        def mean_var(m, q):
                            for j in range(HALF):
                                wait_apart(dve, s_dve_passed, (s_stat, tile(m, j)))
                                nc.vector.bn_aggr(mv[:, q, j, :], st6[:, q, j, :]).then_inc(s_mv, 1)
                            dve.wait_ge(s_mv, tile(m, HALF - 1))
                            nc.vector.tensor_scalar(var[:, q, :], mv[:, q, :, 1], EPS, None, ALU.add).then_inc(s_var, 1)

                        def scales(m, q):
                            dve.wait_ge(s_std, m + 1)
                            if at_least(m, 2):
                                dve.wait_ge(s_h, tile(m - 2, HALF - 1))
                            nc.vector.reciprocal(rstd[:, q, :], std[:, q, :]).then_inc(s_rstd, 1)
                            dve.wait_ge(s_rstd, m + 1)
                            nc.vector.scalar_tensor_tensor(shift[:, q, :], mv[:, q, :, 0], -1.0, rstd[:, q, :],
                                                           ALU.mult, ALU.mult).then_inc(s_shift, 1)

                        def message(m, q, j):
                            y = y_ps[(q + j) % 2]
                            acc = two[:, j, :, :]
                            dve.wait_ge(s_part, tile(m, j))
                            if at_least(m, 1):
                                dve.wait_ge(s_summed, tile(m, j) - HALF)
                            for n, b in enumerate((4, 5, 0, 1, 2, 3)):
                                a = n % 2
                                c = coef[:, bass.ds(m * HALF + j, 1), b]
                                prior = part[:, (q + j) % 2, a, :] if n < 2 else acc[:, a, :]
                                if n == 2:
                                    dve.wait_ge(s_y, tile(m, j))
                                if n >= 2:
                                    dve.wait_ge(s_acc, (m * HALF + j) * 6 + (n - 1))
                                nc.vector.scalar_tensor_tensor(acc[:, a, :], y[:, b * P:(b + 1) * P], c, prior,
                                                               ALU.mult, ALU.add).then_inc(s_acc, 1)

                        def carry_on(m, q, j):
                            dve.wait_ge(s_summed, tile(m, j))
                            if at_least(m, 1) or j >= 1:
                                dve.wait_ge(s_carried, tile(m, j) - 1)
                            if j == 0:
                                dve.wait_ge(s_open, m + 1)
                            if at_least(m, 1):
                                dve.wait_ge(s_biased, tile(m, j) - HALF)
                            nc.vector.scalar_tensor_tensor(sums[:, j, :], open_[:, q, j, :],
                                                           sums[:, (j - 1) % HALF, P - 1:P], sum_ps[(q + j) % 2][:, 0:P],
                                                           ALU.mult, ALU.add).then_inc(s_carried, 1)

                        def step(m, q, i):
                            more = before(m, HALVES - 1)
                            for j in range(HALF):
                                message(m, q, j)
                                ago(m, q, j, 2, carry_on)
                                if more and j == 0:
                                    stats(m + 1, 1 - q, 0, 4)
                                if more and j == 1:
                                    stats(m + 1, 1 - q, 4, HALF)
                                    mean_var(m + 1, 1 - q)
                                if more and j == 2:
                                    scales(m + 1, 1 - q)
                                if more and j == 4:
                                    select(m + 1, 1 - q)
                                if more and j == 5:
                                    find_open(m + 1, 1 - q)

                        stats(0, 0, 0, HALF)
                        mean_var(0, 0)
                        scales(0, 0)
                        select(0, 0)
                        find_open(0, 0)
                        steps(dve, step, 4, HALVES - 2, HALVES, 2)
                        for j in range(2):
                            ago(HALVES, 0, j, 2, carry_on)

                    @block.scalar
                    def _(act):
                        def deviation(m, q):
                            act.wait_ge(s_var, m + 1)
                            nc.scalar.activation(std[:, q, :], var[:, q, :], ACT.Sqrt).then_inc(s_std, 1)

                        def normalize(m, q, j):
                            act.wait_ge(s_shift, m + 1)
                            if at_least(m, 2):
                                act.wait_ge(s_turn, group(m - 2, 1))
                            nc.scalar.activation(h[:, q, j, :], gat[:, q, j, :], ACT.Relu, bias=shift[:, q, j:j + 1],
                                                 scale=rstd[:, q, j:j + 1]).then_inc(s_h, 1)

                        def keep_turned(m, q, a):
                            lo, hi = (0, 4) if a == 0 else (4, HALF)
                            act.wait_ge(s_turn, group(m, a))
                            if at_least(m, 2):
                                act.wait_ge(s_y, tile(m - 2, HALF - 1))
                            nc.scalar.activation(ht[:, q, lo:hi, :], ht_ps[:, 0:(hi - lo) * P]
                                                 .rearrange("p (t e) -> p t e", e=P), ACT.Copy).then_inc(s_ht, 1)

                        def begin(m, q, j):
                            s = (q + j) % 2
                            act.wait_ge(s_y_high, tile(m, j))
                            if at_least(m, 1) or j >= 2:
                                act.wait_ge(s_acc, (m * HALF + j) * 6 - 10)
                            for a in range(BASES_ON_ACT):
                                b = B - BASES_ON_ACT + a
                                last = nc.scalar.activation(part[:, s, a, :], y_ps[s][:, b * P:(b + 1) * P], ACT.Copy,
                                                            scale=coef[:, bass.ds(m * HALF + j, 1), b])
                            last.then_inc(s_part, 1)

                        def add_bias(m, q, j):
                            act.wait_ge(s_carried, tile(m, j))
                            if at_least(m, 1):
                                act.wait_ge(s_rowed, tile(m, j) - HALF)
                            nc.scalar.activation(sums_b[:, j, :], sums[:, j, :], ACT.Identity,
                                                 bias=hb_col[:]).then_inc(s_biased, 1)

                        def keep_rows(m, q, j):
                            act.wait_ge(s_rowed, tile(m, j))
                            if at_least(m, 2):
                                act.wait_ge(s_scattered[q][j], use(m - 2, q))
                            nc.scalar.activation(rows[:, q, j, :], row_ps[:, 0:P], ACT.Copy).then_inc(s_rows, 1)

                        def step(m, q, i):
                            more = before(m, HALVES - 1)
                            for j in range(HALF):
                                ago(m, q, j, 4, add_bias)
                                ago(m, q, j, 6, keep_rows)
                                begin(m, q, j)
                                if j == 0 and at_least(m, 1):
                                    keep_turned(m, q, 1)
                                if more and j == 2:
                                    deviation(m + 1, 1 - q)
                                if more and j >= 3:
                                    for t in ((0, 1), (2, 3), (4, 5), (6,))[j - 3]:
                                        normalize(m + 1, 1 - q, t)
                                if more and j == 5:
                                    keep_turned(m + 1, 1 - q, 0)

                        deviation(0, 0)
                        for j in range(HALF):
                            normalize(0, 0, j)
                        keep_turned(0, 0, 0)
                        keep_turned(0, 0, 1)
                        steps(act, step, 4, HALVES - 2, HALVES, 2)
                        for j in range(6):
                            if j < 4:
                                ago(HALVES, 0, j, 4, add_bias)
                            ago(HALVES, 0, j, 6, keep_rows)

                    @block.tensor
                    def _(pe):
                        def turn(m, q, a):
                            lo, hi = (0, 4) if a == 0 else (4, HALF)
                            pe.wait_ge(s_h, tile(m, hi - 1))
                            if at_least(m, 1) or a:
                                pe.wait_ge(s_ht, group(m, a) - 1)
                            for t in range(lo, hi):
                                last = nc.tensor.transpose(ht_ps[:, (t - lo) * P:(t - lo + 1) * P], h[:, q, t, :], ident[:])
                            last.then_inc(s_turn, 1)

                        def products(m, q, j):
                            pe.wait_ge(s_ht, group(m, 0 if j < 4 else 1))
                            for c, done in ((1, s_y_high), (0, s_y)):
                                if at_least(m, 1) or j >= 2:
                                    pe.wait_ge(s_acc, (m * HALF + j) * 6 - (10 if c else 6))
                                nc.tensor.matmul(y_ps[(q + j) % 2][:, c * 512:(c + 1) * 512], ht[:, q, j, :],
                                                 w_basis[:, 4 * c:4 * c + 4, :], start=True, stop=True).then_inc(done, 1)

                        def sum_runs(m, q, j):
                            pe.wait_ge(s_acc, (m * HALF + j) * 6 + 6)
                            if j == 0:
                                pe.wait_ge(s_same, m + 1)
                            if at_least(m, 1) or j >= 2:
                                pe.wait_ge(s_carried, tile(m, j) - 2)
                            s = (q + j) % 2
                            for a in range(2):
                                last = nc.tensor.matmul(sum_ps[s][:, 0:P], two[:, j, a, :], same[:, q, j, :],
                                                        start=(a == 0), stop=(a == 1))
                            last.then_inc(s_summed, 1)

                        def to_rows(m, q, j):
                            pe.wait_ge(s_biased, tile(m, j))
                            if at_least(m, 1) or j >= 1:
                                pe.wait_ge(s_rows, tile(m, j) - 1)
                            nc.tensor.transpose(row_ps[:, 0:P], sums_b[:, j, :], ident[:]).then_inc(s_rowed, 1)

                        def step(m, q, i):
                            for j in range(HALF):
                                products(m, q, j)
                                ago(m, q, j, 2, sum_runs)
                                ago(m, q, j, 5, to_rows)
                                if before(m, HALVES - 1) and j in (5, 6):
                                    turn(m + 1, 1 - q, j - 5)

                        turn(0, 0, 0)
                        turn(0, 0, 1)
                        steps(pe, step, 4, HALVES - 2, HALVES, 2)
                        for j in range(5):
                            if j < 2:
                                ago(HALVES, 0, j, 2, sum_runs)
                            ago(HALVES, 0, j, 5, to_rows)
            clear(held)

        def norm_pass():
            held = []
            with ExitStack() as st:
                def buf(name, shape, dt=F32):
                    return st.enter_context(nc.sbuf_tensor(f"{name}_norm", shape, dt))

                def bank(name):
                    return st.enter_context(nc.psum_tensor(f"{name}_norm", [P, BLOCK], F32))

                def psem(name):
                    held.append(nc.alloc_semaphore(f"{name}_norm"))
                    return held[-1]

                node = buf("node", [P, SLOTS, BLOCK])
                term = buf("term", [P, SLOTS, BLOCK])
                base = buf("base", [P, SLOTS, BLOCK])
                done = buf("done", [P, SLOTS, BLOCK])
                st6 = buf("st6", [P, SLOTS, NB, 6])
                mv = buf("mv", [P, SLOTS, NB, 2])
                var = buf("var", [P, SLOTS, NB])
                std = buf("std", [P, SLOTS, NB])
                rstd = buf("rstd", [P, SLOTS, NB])
                shift = buf("shift", [P, SLOTS, NB])
                h = buf("h", [P, 2, BLOCK])
                ht = buf("ht", [P, 2, BLOCK])
                tmp = buf("tmp", [P, 2, BLOCK])
                ht_ps = [bank(f"ht_ps{i}") for i in range(2)]
                z_ps = [bank(f"z_ps{i}") for i in range(2)]
                s_node = [psem(f"node{q}") for q in range(SLOTS)]
                s_x1 = [psem(f"x1_{q}") for q in range(SLOTS)]
                s_kept = [psem(f"stored{q}") for q in range(SLOTS)]
                s_base, s_stat, s_mv, s_var = psem("base"), psem("stats"), psem("mean_var"), psem("var_eps")
                s_std, s_rstd, s_shift, s_h = psem("std"), psem("rstd"), psem("shift"), psem("h")
                s_turn, s_ht, s_z = psem("turned"), psem("ht"), psem("z")
                s_tenth, s_done, s_passed = psem("tenth"), psem("done"), psem("dve_passed")

                def use(i, n=1):
                    return i * (n * DMA) + n * DMA

                def earlier(m, q, i, n, what):
                    what(m - n, (q - n) % SLOTS, i if q >= n else i - 1)

                with nc.Block() as block:
                    @block.sync
                    def _(sp):
                        def load(m, q, i):
                            if at_least(m, SLOTS):
                                sp.wait_ge(s_base, m - (SLOTS - 1))
                            sp.dma_start(node[:, q, :], rows_of(x, base_of(m))).then_inc(s_node[q], DMA)
                            sp.dma_start(term[:, q, :], rows_of(agg, base_of(m))).then_inc(s_node[q], DMA)

                        def store(m, q, i):
                            sp.wait_ge(s_done, m + 1)
                            if isinstance(m, int) and m == BLOCKS - 1:
                                sp.wait_ge(s_kept[(q - 1) % SLOTS], use(i))
                            sp.dma_start(rows_of(g0, base_of(m)), done[:, q, :]).then_inc(s_kept[q], DMA)

                        def step(m, q, i):
                            if before(m, BLOCKS):
                                load(m, q, i)
                            if at_least(m, 6):
                                store(m - 6, (q - 6) % SLOTS, i - 1 if q >= 2 else i - 2)

                        steps(sp, step, 2 * SLOTS, BLOCKS - SLOTS, BLOCKS + 6, SLOTS)
                        for q in range(SLOTS):
                            sp.wait_ge(s_kept[q], DMA * BLOCKS // SLOTS)
                            sp.wait_ge(s_x1[q], DMA * BLOCKS // SLOTS)

                    @block.tensor
                    def _(pe):
                        def turn(m, q, i):
                            pe.wait_ge(s_h, m + 1)
                            if at_least(m, 2):
                                pe.wait_ge(s_ht, m - 1)
                            for j in range(NB):
                                last = nc.tensor.transpose(ht_ps[q % 2][:, j * P:(j + 1) * P],
                                                           h[:, q % 2, j * P:(j + 1) * P], ident[:])
                            last.then_inc(s_turn, 1)

                        def product(m, q, i):
                            pe.wait_ge(s_ht, m + 1)
                            if at_least(m, 2):
                                pe.wait_ge(s_done, m - 1)
                            nc.tensor.matmul(z_ps[q % 2][:], ones_bf[0:96, :],
                                             bias_parts[0:96, 0, :].unsqueeze(1).to_broadcast([96, NB, P]),
                                             start=True, stop=False)
                            for j in range(NB):
                                last = nc.tensor.matmul(z_ps[q % 2][:, j * P:(j + 1) * P], ht[:, q % 2, j * P:(j + 1) * P],
                                                        w_enc[:], start=False, stop=(j == NB - 1))
                            last.then_inc(s_z, 1)

                        def step(m, q, i):
                            if before(m, BLOCKS):
                                turn(m, q, i)
                            if at_least(m, 1):
                                earlier(m, q, i, 1, product)

                        steps(pe, step, SLOTS, BLOCKS, BLOCKS + 1, SLOTS)

                    @block.scalar
                    def _(act):
                        def deviation(m, q):
                            act.wait_ge(s_var, m + 1)
                            nc.scalar.activation(std[:, q, :], var[:, q, :], ACT.Sqrt).then_inc(s_std, 1)

                        def normalize(m, q, i):
                            s = q % 2
                            act.wait_ge(s_shift, m + 1)
                            if at_least(m, 2):
                                act.wait_ge(s_turn, m - 1)
                            for j in range(NB):
                                last = nc.scalar.activation(h[:, s, j * P:(j + 1) * P], base[:, q, j * P:(j + 1) * P],
                                                            ACT.Relu, bias=shift[:, q, j:j + 1], scale=rstd[:, q, j:j + 1])
                            last.then_inc(s_h, 1)
                            if isinstance(m, int) and m == BLOCKS - 1:
                                act.wait_ge(s_x1[(q - 1) % SLOTS], use(i))
                            act.dma_start(rows_of(x1, base_of(m)), base[:, q, :]).then_inc(s_x1[q], DMA)

                        def tenth(m, q, i):
                            act.wait_ge(s_z, m + 1)
                            if at_least(m, 2):
                                act.wait_ge(s_done, m - 1)
                            nc.scalar.activation(tmp[:, q % 2, :], z_ps[q % 2][:], ACT.Copy, scale=SLOPE).then_inc(s_tenth, 1)

                        def keep_turned(m, q, i):
                            act.wait_ge(s_turn, m + 1)
                            if at_least(m, 2):
                                act.wait_ge(s_z, m - 1)
                            nc.scalar.activation(ht[:, q % 2, :], ht_ps[q % 2][:], ACT.Copy).then_inc(s_ht, 1)

                        def step(m, q, i):
                            if before(m, BLOCKS):
                                normalize(m, q, i)
                            if at_least(m, 2):
                                earlier(m, q, i, 2, tenth)
                            if at_least(m, 1) and before(m, BLOCKS + 1):
                                earlier(m, q, i, 1, keep_turned)
                            if before(m, BLOCKS - 2):
                                deviation(m + 2, (q + 2) % SLOTS)

                        deviation(0, 0)
                        deviation(1, 1)
                        steps(act, step, SLOTS, BLOCKS - SLOTS, BLOCKS + 2, SLOTS)

                    @block.vector
                    def _(dve):
                        def prepare(m, q, i):
                            dve.wait_ge(s_node[q], use(i, 2))
                            if at_least(m, SLOTS):
                                dve.wait_ge(s_h, m - (SLOTS - 1))
                                dve.wait_ge(s_x1[q], use(i - 1))
                            nc.vector.tensor_tensor(base[:, q, :], node[:, q, :], term[:, q, :], ALU.add).then_inc(s_base, 1)
                            dve.wait_ge(s_base, m + 1)
                            for j in range(NB):
                                nc.vector.bn_stats(st6[:, q, j, :], base[:, q, j * P:(j + 1) * P]).then_inc(s_stat, 1)
                            for j in range(NB):
                                wait_apart(dve, s_passed, (s_stat, m * NB + (j + 1)))
                                nc.vector.bn_aggr(mv[:, q, j, :], st6[:, q, j, :]).then_inc(s_mv, 1)
                            dve.wait_ge(s_mv, m * NB + NB)
                            nc.vector.tensor_scalar(var[:, q, :], mv[:, q, :, 1], EPS, None, ALU.add).then_inc(s_var, 1)

                        def scales(m, q):
                            dve.wait_ge(s_std, m + 1)
                            nc.vector.reciprocal(rstd[:, q, :], std[:, q, :]).then_inc(s_rstd, 1)
                            dve.wait_ge(s_rstd, m + 1)
                            nc.vector.scalar_tensor_tensor(shift[:, q, :], mv[:, q, :, 0], -1.0, rstd[:, q, :],
                                                           ALU.mult, ALU.mult).then_inc(s_shift, 1)

                        def leaky(m, q, i):
                            dve.wait_ge(s_tenth, m + 1)
                            if at_least(m, SLOTS):
                                dve.wait_ge(s_kept[q], use(i - 1))
                            nc.vector.tensor_tensor(done[:, q, :], z_ps[q % 2][:], tmp[:, q % 2, :],
                                                    ALU.max).then_inc(s_done, 1)

                        def step(m, q, i):
                            if before(m, BLOCKS - 1):
                                scales(m + 1, (q + 1) % SLOTS)
                            if before(m, BLOCKS - 2):
                                prepare(m + 2, (q + 2) % SLOTS, i if q < SLOTS - 2 else i + 1)
                            if at_least(m, 3):
                                earlier(m, q, i, 3, leaky)

                        prepare(0, 0, 0)
                        prepare(1, 1, 0)
                        scales(0, 0)
                        steps(dve, step, 2 * SLOTS, BLOCKS - SLOTS, BLOCKS + 3, SLOTS)
            clear(held)

        def layer_pass(l, source, result):
            held = []
            with ExitStack() as st:
                def buf(name, shape, dt=F32):
                    return st.enter_context(nc.sbuf_tensor(f"{name}_l{l}", shape, dt))

                def bank(name):
                    return st.enter_context(nc.psum_tensor(f"{name}_l{l}", [P, 512], F32))

                def psem(name):
                    held.append(nc.alloc_semaphore(f"{name}_l{l}"))
                    return held[-1]

                gat = buf("gat", [P, 2, HALF, P])
                act_gat = buf("act_gat", [P, 2, HALF, P]) if l else gat
                rows = buf("rows", [P, 2, HALF, P])
                gidx = buf("gidx", [P, 2, HALF], I32)
                pidx = buf("pidx", [P, 2, HALF], I32)
                dst_b = buf("dst_b", [P, 2, HALF * P + 1])
                same = buf("same", [P, 2, HALF, P])
                open_ = buf("open", [P, 2, HALF, P])
                sums = buf("sums", [P, HALF, P])
                sum_ps = [bank(f"sum_ps{i}") for i in range(2)]
                row_ps = [bank(f"row_ps{i}") for i in range(2)]
                s_gathered = [[psem(f"gathered{q}{j}") for j in range(HALF)] for q in range(2)]
                s_added = [[psem(f"added{q}{j}") for j in range(HALF)] for q in range(2)]
                s_gidx, s_pidx, s_passed = psem("gather_index"), psem("scatter_index"), psem("pool_passed")
                s_dstb = [psem(f"dst_b{q}") for q in range(2)]
                s_same, s_open, s_leaked = psem("same_made"), psem("open_made"), psem("leaked")
                s_summed, s_carried, s_rowed = psem("summed"), psem("carried"), psem("rowed")
                s_rows, s_start = psem("rows_ready"), psem("carry_zeroed")
                s_spilled = [psem(f"spilled{q}") for q in range(2)]
                s_back = [psem(f"back{q}") for q in range(2)]
                node = buf("node", [P, WALK, BLOCK])
                ht = buf("ht", [P, 2, BLOCK])
                done = buf("done", [P, WALK, BLOCK])
                ht_ps = [bank(f"ht_ps{i}") for i in range(2)]
                z_ps = [bank(f"z_ps{i}") for i in range(2)]
                s_node = [psem(f"node{c}") for c in range(WALK)]
                s_stored = [psem(f"stored{c}") for c in range(WALK)]
                s_node_leaky, s_turn, s_ht, s_z, s_done = (psem("node_leaky"), psem("turned"), psem("ht"), psem("z"),
                                                           psem("done"))

                def tile(m, j):
                    return m * HALF + (j + 1)

                def use(m, q):
                    return (m // 2 + 1) * DMA if isinstance(m, int) else (m - q) * (DMA // 2) + DMA

                def turn_of(i):
                    return (i + 1) * DMA

                def blocks(q):
                    return [(0, 0), (2, 1), (4, 2), (6, 3)] if q == 0 else [(1, 4), (3, 5), (5, 6)]

                def earlier(i, c, n, what):
                    if c >= n:
                        what(i, c - n)
                    elif at_least(i, 1):
                        what(i - 1, WALK + c - n)

                def bank_used(i, c):
                    return i * WALK + (c if c == 0 else c - 1)

                def ago(m, q, i, j, n, what):
                    if j >= n:
                        what(m, q, j - n)
                    elif at_least(m, 1):
                        what(m - 1, 1 - q, HALF + j - n)

                if l:
                    COUNT = -(-N // LAST)
                    assert COUNT % WALK == 0
                    last_z = buf("last_z", [P, WALK, LAST // P * P])
                    last_x1 = buf("last_x1", [P, WALK, LAST // P * P])
                    limit_i = buf("limit_i", [1, COUNT], I32)
                    limit = buf("limit", [1, COUNT])
                    count = buf("count", [1, 2, COUNT])
                    need = buf("need", [1, COUNT], I32)
                    s_final, s_limits, s_need = psem("half_steps_added"), psem("limits_made"), psem("need_made")
                    s_count = psem("counting")
                    s_in = [psem(f"last_loaded{c}") for c in range(WALK)]
                    s_out = [psem(f"out_stored{c}") for c in range(WALK)]
                    s_leaky, s_sum = psem("leaky"), psem("sum")

                def part(ap, k):
                    first = N - LAST if isinstance(k, int) and k == COUNT - 1 else k * LAST
                    return ap[bass.ds(first, LAST), :].rearrange("(p j) f -> p (j f)", p=P)

                def count_needed(dve):
                    dve.wait_ge(s_limits, 1)
                    nc.vector.tensor_copy(limit[:], limit_i[:]).then_inc(s_count, 1)
                    dve.wait_ge(s_count, 1)
                    below = last_z[0:1].rearrange("o c f -> o (c f)")[:, 0:COUNT * HALVES].rearrange("o (k m) -> o k m",
                                                                                                 m=HALVES)
                    firsts = dst_c[0:1, :].rearrange("o (m j) -> o m j", j=HALF)[:, :, 0]
                    nc.vector.tensor_tensor(below, firsts.unsqueeze(1).to_broadcast([1, COUNT, HALVES]),
                                            limit[:].unsqueeze(2).to_broadcast([1, COUNT, HALVES]),
                                            ALU.is_lt).then_inc(s_count, 1)
                    dve.wait_ge(s_count, 2)
                    nc.vector.reduce_sum(count[:, 0, :], below, AX.X).then_inc(s_count, 1)
                    dve.wait_ge(s_count, 3)
                    nc.vector.tensor_scalar(count[:, 1, :], count[:, 0, :], 1.0, None, ALU.max).then_inc(s_count, 1)
                    dve.wait_ge(s_count, 4)
                    nc.vector.tensor_copy(need[:], count[:, 1, :]).then_inc(s_need, 1)

                def add_up(dve):
                    def combine(k, c, i):
                        dve.wait_ge(s_in[c], i * (2 * DMA) + 2 * DMA)
                        nc.vector.scalar_tensor_tensor(last_z[:, c, :], last_z[:, c, :], SLOPE, last_z[:, c, :],
                                                       ALU.mult, ALU.max).then_inc(s_leaky, 1)
                        dve.wait_ge(s_leaky, k + 1)
                        nc.vector.tensor_tensor(last_z[:, c, :], last_z[:, c, :], last_x1[:, c, :],
                                                ALU.add).then_inc(s_sum, 1)

                    steps(dve, combine, 0, COUNT, COUNT, WALK)

                def write_out(act):
                    LATE = 4

                    def load(k, c, i):
                        if at_least(k, WALK):
                            act.wait_ge(s_out[c], i * DMA)
                        act.dma_start(last_x1[:, c, :], part(x1, k)).then_inc(s_in[c], DMA)
                        act.wait_ge(s_final, act.value_load(need[0:1, bass.ds(k, 1)], min_val=1, max_val=HALVES))
                        act.dma_start(last_z[:, c, :], part(result, k)).then_inc(s_in[c], DMA)

                    def store(k, c, i):
                        act.wait_ge(s_sum, k + 1)
                        if isinstance(k, int) and k == COUNT - 1:
                            act.wait_ge(s_out[c - 1], (i + 1) * DMA)
                        act.dma_start(part(out, k), last_z[:, c, :]).then_inc(s_out[c], DMA)

                    def step(k, c, i):
                        load(k, c, i)
                        if at_least(k, LATE):
                            store(k - LATE, (c - LATE) % WALK, i if c >= LATE else i - 1)

                    act.wait_ge(s_need, 1)
                    for c in range(WALK):
                        act.wait_ge(s_stored[c], DMA * BLOCKS // WALK)
                    steps(act, step, WALK, COUNT - WALK, COUNT, WALK)
                    for k in range(COUNT - LATE, COUNT):
                        store(k, k % WALK, k // WALK)
                    for c in range(WALK):
                        act.wait_ge(s_out[c], DMA * COUNT // WALK)

                with nc.Block() as block:
                    @block.gpsimd
                    def _(pool):
                        if l:
                            nc.gpsimd.iota(limit_i[:], pattern=[[LAST, COUNT]], base=LAST,
                                           channel_multiplier=0).then_inc(s_limits, 1)

                        def gather(m, q, i):
                            if at_least(m, 2):
                                if l:
                                    pool.wait_ge(s_leaked, m - 1)
                                else:
                                    pool.wait_ge(s_summed, tile(m - 2, HALF - 1))
                            nc.gpsimd.tensor_copy(gidx[:, q, :], src_c[:, bass.ds(m * HALF, HALF)]).then_inc(s_gidx, 1)
                            wait_apart(pool, s_passed, (s_gidx, m + 1))
                            for j in range(HALF):
                                nc.gpsimd.indirect_dma_start(
                                    gat[:, q, j, :], None, source[0:N, :],
                                    bass.IndirectOffsetOnAxis(ap=gidx[:, q, j:j + 1], axis=0)).then_inc(s_gathered[q][j], DMA)

                        def add(m, q, i):
                            if at_least(m, 2):
                                for j in range(HALF):
                                    pool.wait_ge(s_added[q][j], use(m - 2, q))
                                if l:
                                    pool.sem_inc(s_final, 1)
                            nc.gpsimd.tensor_copy(pidx[:, q, :], put_c[:, bass.ds(m * HALF, HALF)]).then_inc(s_pidx, 1)
                            wait_apart(pool, s_passed, (s_pidx, m + 1), (s_back[q], use(m, q)))
                            for j in range(HALF):
                                nc.gpsimd.indirect_dma_start(
                                    result, bass.IndirectOffsetOnAxis(ap=pidx[:, q, j:j + 1], axis=0),
                                    rows[:, q, j, :], None, compute_op=ALU.add).then_inc(s_added[q][j], DMA)

                        steps(pool, gather, 4, HALVES, HALVES, 2)
                        for c in range(WALK):
                            pool.wait_ge(s_stored[c], DMA * BLOCKS // WALK)
                        steps(pool, add, 4, HALVES, HALVES, 2)
                        for q in range(2):
                            for j in range(HALF):
                                pool.wait_ge(s_added[q][j], DMA * HALVES // 2)
                            if l:
                                pool.sem_inc(s_final, 1)

                    @block.sync
                    def _(sp):
                        def load(m, q, i):
                            if at_least(m, 2):
                                sp.wait_ge(s_same, m - 1)
                                sp.wait_ge(s_open, m - 1)
                            sp.dma_start(dst_b[:, q, :], dst_f[bass.ds(m * (HALF * P), HALF * P + 1)]
                                         .partition_broadcast(P)).then_inc(s_dstb[q], DMA)
                            for _, c in blocks(q):
                                if at_least(i, 1):
                                    sp.wait_ge(s_turn, i * WALK + (c - WALK + 1))
                                sp.dma_start(node[:, c, :], rows_of(source, base_of(i * WALK + c))).then_inc(s_node[c], DMA)

                        def back(m, q, i):
                            if at_least(m, 2):
                                for j in range(HALF):
                                    sp.wait_ge(s_added[q][j], use(m - 2, q))
                            sp.dma_start(rows[:, q, :, :], spill[bass.ds(m, 1), :, :]
                                         .rearrange("o p (j f) -> (o p) j f", f=P)).then_inc(s_back[q], DMA)

                        steps(sp, load, 4, HALVES - 2, HALVES, 2)
                        for q in range(2):
                            sp.wait_ge(s_spilled[q], DMA * HALVES // 2)
                        steps(sp, back, 4, HALVES, HALVES, 2)

                    @block.vector
                    def _(dve):
                        nc.vector.memset(sums[:, HALF - 1, :], 0.0).then_inc(s_start, 1)
                        dve.wait_ge(s_start, 1)
                        if l:
                            count_needed(dve)

                        def columns(q):
                            return dst_b[:, q, 1:HALF * P + 1].rearrange("p (t e) -> p t e", e=P)

                        def select(m, q):
                            dve.wait_ge(s_dstb[q], use(m, q))
                            if at_least(m, 2):
                                dve.wait_ge(s_summed, tile(m - 2, HALF - 1))
                            nc.vector.tensor_tensor(same[:, q, :, :], columns(q),
                                                    dst_c[:, bass.ds(m * HALF, HALF)].unsqueeze(2).to_broadcast([P, HALF, P]),
                                                    ALU.is_equal).then_inc(s_same, 1)

                        def find_open(m, q):
                            dve.wait_ge(s_dstb[q], use(m, q))
                            if at_least(m, 2):
                                dve.wait_ge(s_carried, tile(m - 2, HALF - 1))
                            last_before = dst_b[:, q, 0:HALF * P].rearrange("p (t e) -> p t e", e=P)[:, :, 0:1]
                            nc.vector.tensor_tensor(open_[:, q, :, :], columns(q), last_before.to_broadcast([P, HALF, P]),
                                                    ALU.is_equal).then_inc(s_open, 1)

                        def leak(m, q):
                            for j in range(HALF):
                                dve.wait_ge(s_gathered[q][j], use(m, q))
                            nc.vector.scalar_tensor_tensor(act_gat[:, q, :, :], gat[:, q, :, :], SLOPE, gat[:, q, :, :],
                                                           ALU.mult, ALU.max).then_inc(s_leaked, 1)

                        def leak_node(i, c):
                            dve.wait_ge(s_node[c], turn_of(i))
                            nc.vector.scalar_tensor_tensor(node[:, c, :], node[:, c, :], SLOPE, node[:, c, :],
                                                           ALU.mult, ALU.max).then_inc(s_node_leaky, 1)

                        def carry_on(m, q, j):
                            dve.wait_ge(s_summed, tile(m, j))
                            if at_least(m, 1) or j >= 1:
                                dve.wait_ge(s_carried, tile(m, j) - 1)
                            if j == 0:
                                dve.wait_ge(s_open, m + 1)
                            if at_least(m, 1):
                                dve.wait_ge(s_rowed, tile(m, j) - HALF)
                            nc.vector.scalar_tensor_tensor(sums[:, j, :], open_[:, q, j, :],
                                                           sums[:, (j - 1) % HALF, P - 1:P], sum_ps[(q + j) % 2][:, 0:P],
                                                           ALU.mult, ALU.add).then_inc(s_carried, 1)

                        def step(m, q, i):
                            more = before(m, HALVES - 1)
                            for j in range(HALF):
                                if l:
                                    for after, c in blocks(q):
                                        if after == j:
                                            leak_node(i, c)
                                carry_on(m, q, j)
                                if more and j == 2:
                                    select(m + 1, 1 - q)
                                if more and j == 3:
                                    find_open(m + 1, 1 - q)
                                if more and j == 5 and l:
                                    leak(m + 1, 1 - q)

                        select(0, 0)
                        find_open(0, 0)
                        if l:
                            leak(0, 0)
                        steps(dve, step, 4, HALVES - 2, HALVES, 2)
                        if l:
                            add_up(dve)

                    @block.scalar
                    def _(act):
                        def finish(m, q, j):
                            act.wait_ge(s_rowed, tile(m, j))
                            if at_least(m, 2) and j == 0:
                                act.wait_ge(s_spilled[q], use(m - 2, q))
                            nc.scalar.activation(rows[:, q, j, :], row_ps[(q + j) % 2][:, 0:P], ACT.Copy,
                                                 scale=inv_c[:, bass.ds(m * HALF + j, 1)]).then_inc(s_rows, 1)
                            if j == HALF - 1:
                                act.wait_ge(s_rows, tile(m, j))
                                act.dma_start(spill[bass.ds(m, 1), :, :].rearrange("o p (j f) -> (o p) j f", f=P),
                                              rows[:, q, :, :]).then_inc(s_spilled[q], DMA)

                        def keep_turned(i, c):
                            act.wait_ge(s_turn, i * WALK + (c + 1))
                            if at_least(i, 1) or c >= 2:
                                act.wait_ge(s_z, bank_used(i, c))
                            nc.scalar.activation(ht[:, c % 2, :], ht_ps[c % 2][:], ACT.Copy).then_inc(s_ht, 1)

                        def keep_product(i, c):
                            act.wait_ge(s_z, i * WALK + (c + 1))
                            if at_least(i, 1):
                                act.wait_ge(s_stored[c], turn_of(i - 1))
                            nc.scalar.activation(done[:, c, :], z_ps[c % 2][:], ACT.Copy).then_inc(s_done, 1)

                        def store(i, c):
                            act.wait_ge(s_done, i * WALK + (c + 1))
                            if isinstance(i, int) and i * WALK + c == BLOCKS - 1:
                                act.wait_ge(s_stored[c - 1], turn_of(i))
                            act.dma_start(rows_of(result, base_of(i * WALK + c)), done[:, c, :]).then_inc(s_stored[c], DMA)

                        def step(m, q, i):
                            for j in range(HALF):
                                for after, c in blocks(q):
                                    if after == j:
                                        earlier(i, c, 3, keep_product)
                                        earlier(i, c, 1, keep_turned)
                                        earlier(i, c, 4, store)
                                ago(m, q, i, j, 3, finish)

                        steps(act, step, 4, HALVES - 2, HALVES, 2)
                        keep_product(BLOCKS // WALK - 1, WALK - 3)
                        keep_turned(BLOCKS // WALK - 1, WALK - 1)
                        for c in (WALK - 2, WALK - 1):
                            keep_product(BLOCKS // WALK - 1, c)
                        for c in range(WALK - 4, WALK):
                            store(BLOCKS // WALK - 1, c)
                        for j in range(3):
                            ago(HALVES, 0, 0, j, 3, finish)
                        if l:
                            write_out(act)

                    @block.tensor
                    def _(pe):
                        def sum_runs(m, q, j):
                            if l:
                                if j == 0:
                                    pe.wait_ge(s_leaked, m + 1)
                            else:
                                pe.wait_ge(s_gathered[q][j], use(m, q))
                            if j == 0:
                                pe.wait_ge(s_same, m + 1)
                            if at_least(m, 1) or j >= 2:
                                pe.wait_ge(s_carried, tile(m, j) - 2)
                            nc.tensor.matmul(sum_ps[(q + j) % 2][:, 0:P], act_gat[:, q, j, :], same[:, q, j, :],
                                             start=True, stop=True).then_inc(s_summed, 1)

                        def to_rows(m, q, j):
                            s = (q + j) % 2
                            pe.wait_ge(s_carried, tile(m, j))
                            if at_least(m, 1) or j >= 2:
                                pe.wait_ge(s_rows, tile(m, j) - 2)
                            nc.tensor.matmul(row_ps[s][:, 0:P], sums[:, j, :], w_l[:, l, :],
                                             start=True, stop=True).then_inc(s_rowed, 1)

                        def turn(i, c):
                            if l:
                                pe.wait_ge(s_node_leaky, i * WALK + (c + 1))
                            else:
                                pe.wait_ge(s_node[c], turn_of(i))
                            if at_least(i, 1) or c >= 2:
                                pe.wait_ge(s_ht, bank_used(i, c))
                            for j in range(NB):
                                last = nc.tensor.transpose(ht_ps[c % 2][:, j * P:(j + 1) * P],
                                                           node[:, c, j * P:(j + 1) * P], ident[:])
                            last.then_inc(s_turn, 1)

                        def product(i, c):
                            pe.wait_ge(s_ht, i * WALK + (c + 1))
                            if at_least(i, 1) or c >= 2:
                                pe.wait_ge(s_done, bank_used(i, c))
                            nc.tensor.matmul(z_ps[c % 2][:], ones_bf[0:96, :],
                                             bias_parts[0:96, 1 + l, :].unsqueeze(1).to_broadcast([96, NB, P]),
                                             start=True, stop=False)
                            for j in range(NB):
                                last = nc.tensor.matmul(z_ps[c % 2][:, j * P:(j + 1) * P], ht[:, c % 2, j * P:(j + 1) * P],
                                                        w_r[:, l, :], start=False, stop=(j == NB - 1))
                            last.then_inc(s_z, 1)

                        def step(m, q, i):
                            for j in range(HALF):
                                sum_runs(m, q, j)
                                for after, c in blocks(q):
                                    if after == j:
                                        earlier(i, c, 1, turn)
                                        earlier(i, c, 2, product)
                                ago(m, q, i, j, 2, to_rows)

                        steps(pe, step, 4, HALVES - 2, HALVES, 2)
                        turn(BLOCKS // WALK - 1, WALK - 1)
                        product(BLOCKS // WALK - 1, WALK - 2)
                        product(BLOCKS // WALK - 1, WALK - 1)
                        ago(HALVES, 0, 0, 0, 2, to_rows)
                        ago(HALVES, 0, 0, 1, 2, to_rows)
            clear(held)

        relational_pass()
        norm_pass()
        layer_pass(0, g0, z[0])
        layer_pass(1, z[0], z[1])


_INS = ['x', 'src', 'dst', 'edge_type_16', 'L0_gnn_weight', 'L0_gnn_w_comp', 'L0_gnn_h_bias', 'L1_gnn_enc_w',
        'L1_gnn_enc_b', 'L1_gnn_lin_l_w', 'L1_gnn_lin_l_b', 'L1_gnn_lin_r_w']
_OUTS = [((100000, 128), 'float32')]


def kernel(**inputs):
    import numpy as _np
    import concourse.bacc as _bacc
    from concourse import mybir as _mybir
    from concourse.bass_utils import run_bass_kernel_spmd as _run

    nc = _bacc.Bacc("TRN2", target_bir_lowering=False, num_devices=1)
    arrays, args = {}, []
    for name in _INS:
        a = _np.ascontiguousarray(inputs[name])
        arrays[f"in_{name}_dram"] = a
        args.append(nc.dram_tensor(f"in_{name}_dram", a.shape, _mybir.dt.from_np(a.dtype), kind="ExternalInput").ap())
    for i, (shape, dtype) in enumerate(_OUTS):
        dt = _mybir.dt.from_np(_np.dtype(dtype))
        args.append(nc.dram_tensor(f"out_{i}_dram", shape, dt, kind="ExternalOutput").ap())
    gnn_kernel(nc, *args)
    r = _run(nc, [arrays], core_ids=[0])
    got = tuple(r.results[0][f"out_{i}_dram"] for i in range(len(_OUTS)))
    return got[0]
```

```python
import concourse.bass as bass
from concourse import mybir
from contextlib import ExitStack

F32 = mybir.dt.float32
BF16 = mybir.dt.bfloat16
I32 = mybir.dt.int32
ALU = mybir.AluOpType
ACT = mybir.ActivationFunctionType
AX = mybir.AxisListType

P = 128
EPS = 1e-5
SLOPE = 0.1
DMA = 16

HALF = 7
ROW = 4 * P
NB = 4
BLOCK = NB * P
SLOTS = 8
WALK = 7
LAST = 8 * P
FILL = 16 * P
BASES_ON_ACT = 2


def at_least(m, n):
    return not isinstance(m, int) or m >= n


def before(m, n):
    return not isinstance(m, int) or m < n


def wait_apart(eng, passed, *waits):
    for semaphore, value in waits:
        eng.wait_ge(semaphore, value)
    eng.sem_inc(passed, 1)


def steps(eng, step, head, tail, total, unroll):
    for m in range(head):
        step(m, m % unroll, m // unroll)
    with eng.Fori(head // unroll, tail // unroll) as i:
        for u in range(unroll):
            step(i * unroll + u, u, i)
    for m in range(tail, total):
        step(m, m % unroll, m // unroll)


def gnn_kernel(nc, x, src, dst, etype, basis_w, w_comp, h_bias, enc_w, enc_b, lin_l_w, lin_l_b,
               lin_r_w, out):
    N = x.shape[0]
    E = src.shape[0]
    R, B = w_comp.shape
    ROWS = -(-E // ROW)
    EP = ROWS * ROW
    T = EP // P
    HALVES = T // HALF
    NOWHERE = 2 * N
    BLOCKS = -(-N // BLOCK)
    LAST_BASE = N - BLOCK
    FILLS = -(-N // FILL)
    FILLS_EARLY = 12
    FILLS_MIDDLE = 22
    GROUPS = P // R
    assert T % (4 * HALF) == 0 and BLOCKS == HALVES // 2 * WALK and BLOCKS % SLOTS >= 2
    assert ROWS <= P and T % GROUPS == 0 and N % (FILL // P) == 0
    AHEAD = BLOCKS - 6 * HALVES // 4
    assert AHEAD > 0 and AHEAD % WALK == 0
    Y = B * P

    ctx = ExitStack()
    with ctx:
        def sb(name, shape, dt=F32):
            return ctx.enter_context(nc.sbuf_tensor(name, shape, dt))

        def sem(name):
            return ctx.enter_context(nc.semaphore(name))

        def dram(name, shape, dt=F32):
            return nc.dram_tensor(name, shape, dt).ap()

        src_s = dram("src_sorted", [EP], I32)
        dst_s = dram("dst_sorted", [EP], I32)
        typ_s = dram("type_sorted", [EP], I32)
        src_u = dram("src_padded", [EP], I32)
        dst_u = dram("dst_padded", [EP], I32)
        typ_u = dram("type_padded", [EP], I32)
        dst_f = dram("dst_float", [EP + 2])
        agg = dram("agg", [N, P])
        x1 = dram("x1", [N, P])
        g0 = dram("g0", [N, P])
        z = [dram(f"z{k}", [N + 2 * HALF * P, P]) for k in range(2)]
        spill = dram("means_by_edge", [HALVES, P, HALF * P])

        ident = sb("ident", [P, P])
        ones = sb("ones", [P, P])
        bias_row = sb("bias_row", [P, P])
        fill_rows = sb("fill_rows", [P, FILL // P * P])
        w_basis = sb("w_basis", [P, B, P])
        w_enc = sb("w_enc", [P, P])
        w_l = sb("w_l", [P, 2, P])
        w_r = sb("w_r", [P, 2, P])
        hb_col = sb("hb_col", [P, 1])
        comp = sb("comp", [P, GROUPS * B])
        bias_parts = sb("bias_parts", [P, 3, P], BF16)
        bias_rest = sb("bias_rest", [P, 2, 3, P])
        bias_tmp = sb("bias_tmp", [P, 3, P], BF16)
        ones_bf = sb("ones_bf", [P, P], BF16)
        dst_c = sb("dst_c", [P, T])
        src_c = sb("src_c", [P, T], I32)
        put_c = sb("put_c", [P, T], I32)
        inv_c = sb("inv_c", [P, T])
        coef = sb("coef", [P, T, B])

        def rows_of(ap, first):
            return ap[bass.ds(first, BLOCK), :].rearrange("(p j) f -> p (j f)", p=P)

        s_filled = [sem(f"agg_filled{k}") for k in range(2)]

        def wait_filled(eng, m):
            eng.wait_ge(s_filled[m % 2], DMA * (m // 2 + 1))

        def fill(eng, lo, hi, flying):
            for m in range(lo, hi):
                if m - flying >= lo:
                    wait_filled(eng, m - flying)
                rows = min(FILL, N - m * FILL)
                eng.dma_start(agg[m * FILL:m * FILL + rows, :].rearrange("(p j) f -> p (j f)", j=FILL // P),
                              fill_rows[0:rows * P // FILL, :]).then_inc(s_filled[m % 2], DMA)

        def base_of(m):
            return LAST_BASE if isinstance(m, int) and m == BLOCKS - 1 else m * BLOCK

        with ExitStack() as st:
            W = E // 100
            assert W * 100 == E
            cur = st.enter_context(nc.sbuf_tensor("dst_cur", [100, W], I32))
            nxt = st.enter_context(nc.sbuf_tensor("dst_nxt", [100, W], I32))
            down = st.enter_context(nc.sbuf_tensor("down", [100, W], F32))
            downs = st.enter_context(nc.sbuf_tensor("downs", [P, 1], F32))
            unsorted = st.enter_context(nc.sbuf_tensor("unsorted", [1, 1], I32))
            pad = st.enter_context(nc.sbuf_tensor("pad", [1, 2, EP - E], I32))
            ends = st.enter_context(nc.sbuf_tensor("ends", [1, 2], F32))
            total = st.enter_context(nc.psum_tensor("total", [1, 1], F32))
            s_w = sem("weights_loaded")
            s_set = sem("dve_set")
            s_id0, s_id1 = sem("ident_zeroed"), sem("ident_made")
            s_comp_zero = sem("comp_zeroed")
            s_dst = sem("dst_loaded")
            s_pads = sem("pads_set")
            s_padded = sem("pads_stored")
            s_bias = sem("bias_loaded")
            s_bias_row, s_filler = sem("bias_row_loaded"), sem("filler_made")
            s_downs = sem("downs_counted")
            s_total = sem("downs_totalled")
            with nc.Block() as block:
                @block.sync
                def _(sp):
                    sp.dma_start(bias_row[:], h_bias.partition_broadcast(P)).then_inc(s_bias_row, DMA)
                    sp.wait_ge(s_set, 1)
                    sp.dma_start(cur[:], dst.rearrange("(p w) -> p w", w=W)).then_inc(s_dst, DMA)
                    sp.dma_start(nxt[0:99, :], dst[1:1 + 99 * W].rearrange("(p w) -> p w", w=W)).then_inc(s_dst, DMA)
                    sp.dma_start(nxt[99:100, 0:W - 1], dst[1 + 99 * W:E].unsqueeze(0)).then_inc(s_dst, DMA)
                    sp.wait_ge(s_set, 2)
                    for r in range(3):
                        for k, b in enumerate((enc_b, lin_l_b[0, :], lin_l_b[1, :])):
                            sp.dma_start(bias_rest[32 * r:32 * r + 1, 0, k, :], b.unsqueeze(0)).then_inc(s_bias, DMA)
                    sp.dma_start(hb_col[:], h_bias.unsqueeze(1)).then_inc(s_w, DMA)
                    sp.wait_ge(s_comp_zero, 1)
                    for g in range(GROUPS):
                        sp.dma_start(comp[g * R:(g + 1) * R, g * B:(g + 1) * B], w_comp).then_inc(s_w, DMA)
                    sp.dma_start(w_basis[:], basis_w.rearrange("b i o -> i b o")).then_inc(s_w, DMA)
                    sp.dma_start(w_enc[:], enc_w).then_inc(s_w, DMA)
                    sp.dma_start(w_l[:], lin_l_w.rearrange("l i o -> i l o")).then_inc(s_w, DMA)
                    sp.dma_start(w_r[:], lin_r_w.rearrange("l i o -> i l o")).then_inc(s_w, DMA)
                    sp.wait_ge(s_pads, 4)
                    for k, arrays in enumerate(((src_s, typ_s, src_u, typ_u), (dst_s, dst_u))):
                        for a in arrays:
                            sp.dma_start(a[E:EP].unsqueeze(0), pad[:, k, :]).then_inc(s_padded, DMA)
                    sp.dma_start(dst_f[0:1].unsqueeze(0), ends[:, 0:1]).then_inc(s_padded, DMA)
                    sp.dma_start(dst_f[EP + 1:EP + 2].unsqueeze(0), ends[:, 1:2]).then_inc(s_padded, DMA)
                    sp.wait_ge(s_w, (5 + GROUPS) * DMA)
                    sp.wait_ge(s_padded, 8 * DMA)
                @block.gpsimd
                def _(pool):
                    nc.gpsimd.memset(ident[:], 0.0).then_inc(s_id0, 1)
                    pool.wait_ge(s_id0, 1)
                    nc.gpsimd.affine_select(out=ident[:], in_=ident[:], compare_op=ALU.not_equal, fill=1.0, base=0,
                                            pattern=[[-1, P]], channel_multiplier=1).then_inc(s_id1, 1)

                @block.vector
                def _(dve):
                    chain = [2]

                    def link(ins):
                        chain[0] += 1
                        ins.then_inc(s_set, 1)
                        dve.wait_ge(s_set, chain[0])

                    nc.vector.memset(nxt[:], NOWHERE).then_inc(s_set, 1)
                    nc.vector.memset(bias_rest[:], 0.0).then_inc(s_set, 1)
                    nc.vector.memset(comp[:], 0.0).then_inc(s_comp_zero, 1)
                    link(nc.vector.memset(ones[:], 1.0))
                    link(nc.vector.memset(ones_bf[:], 1.0))
                    link(nc.vector.memset(downs[:], 0.0))
                    nc.vector.memset(pad[:, 0, :], 0).then_inc(s_pads, 1)
                    nc.vector.memset(pad[:, 1, :], NOWHERE).then_inc(s_pads, 1)
                    nc.vector.memset(ends[:, 0:1], -1.0).then_inc(s_pads, 1)
                    nc.vector.memset(ends[:, 1:2], float(2 * NOWHERE)).then_inc(s_pads, 1)
                    dve.wait_ge(s_bias_row, DMA)
                    nc.vector.tensor_copy(fill_rows[:].rearrange("p (j f) -> p j f", f=P),
                                          bias_row[:].unsqueeze(1).to_broadcast([P, FILL // P, P])).then_inc(s_filler, 1)
                    dve.wait_ge(s_dst, 3 * DMA)
                    link(nc.vector.tensor_tensor(down[:], nxt[:], cur[:], ALU.is_lt))
                    nc.vector.reduce_sum(downs[0:100, :], down[:], AX.X).then_inc(s_downs, 1)
                    dve.wait_ge(s_bias, 9 * DMA)
                    link(nc.vector.memset(bias_parts[:], 0.0))
                    for r in range(3):
                        link(nc.vector.tensor_copy(bias_tmp[:], bias_rest[:, r % 2, :, :]))
                        link(nc.vector.tensor_copy(bias_parts[32 * r:32 * r + 1, :, :], bias_tmp[32 * r:32 * r + 1, :, :]))
                        link(nc.vector.tensor_tensor(bias_rest[:, 1 - r % 2, :, :], bias_rest[:, r % 2, :, :], bias_tmp[:],
                                                     ALU.subtract))
                    dve.wait_ge(s_total, 1)
                    link(nc.vector.tensor_copy(unsorted[:], total[:]))

                @block.scalar
                def _(act):
                    act.wait_ge(s_filler, 1)
                    fill(act, 0, FILLS_EARLY, FILLS_EARLY)

                @block.tensor
                def _(pe):
                    pe.wait_ge(s_downs, 1)
                    nc.tensor.matmul(total[:], downs[:], ones[:, 0:1], start=True, stop=True).then_inc(s_total, 1)

            CH = EP // 8
            GROUP = 8
            row_i = st.enter_context(nc.sbuf_tensor("row_i", [P, CH], I32))
            row_f = st.enter_context(nc.sbuf_tensor("row_f", [P, CH], F32))
            frac = st.enter_context(nc.sbuf_tensor("frac", [P, CH], F32))
            gap = st.enter_context(nc.sbuf_tensor("gap", [P, CH], F32))
            hit = st.enter_context(nc.sbuf_tensor("hit", [P, CH], BF16))
            cols_u = st.enter_context(nc.sbuf_tensor("cols_u", [P, 3, T], I32))
            dcol = st.enter_context(nc.sbuf_tensor("dcol", [P, T], F32))
            thr_i = st.enter_context(nc.sbuf_tensor("thr_i", [P, T], I32))
            thr = st.enter_context(nc.sbuf_tensor("thr", [P, 2, T], F32))
            below = st.enter_context(nc.sbuf_tensor("below", [P, T], F32))
            rank = st.enter_context(nc.sbuf_tensor("rank", [P, 2, T], F32))
            rank_i = st.enter_context(nc.sbuf_tensor("rank_i", [P, T], I32))
            stage = st.enter_context(nc.sbuf_tensor("stage", [P, 4, GROUP], I32))
            s_u = sem("padded_copied")
            s_cols = sem("columns_loaded")
            s_iota = sem("iotas_made")
            s_row = sem("row_loaded")
            s_rowused = sem("row_used")
            s_rk = sem("rank_steps")
            s_ranked = sem("ranked")
            s_staged = sem("staged")
            s_spread = [sem(f"spread{k}") for k in range(3)]
            s_direct = sem("sorted_copied")
            s_passed = sem("waits_passed")
            with nc.Block() as block:
                @block.sync
                def _(sp):
                    flag = sp.value_load(unsorted[0:1, 0:1], min_val=0, max_val=E)
                    with sp.If(flag != 0):
                        for a, b in ((src, src_u), (dst, dst_u), (etype, typ_u)):
                            sp.dma_start(b[0:E], a).then_inc(s_u, DMA)
                        sp.wait_ge(s_u, 3 * DMA)
                        with nc.allow_non_contiguous_dma(reason="edges into columns, in the rare order"):
                            for k, a in enumerate((dst_u, src_u, typ_u)):
                                sp.dma_start(cols_u[:, k, :], a.rearrange("(t p) -> p t", p=P)).then_inc(s_cols, DMA)
                        for c in range(8):
                            if c:
                                sp.wait_ge(s_rowused, c)
                            sp.dma_start(row_i[:], dst_u[c * CH:(c + 1) * CH].partition_broadcast(P)).then_inc(s_row, DMA)
                            sp.wait_ge(s_row, DMA * (c + 1))
                        sp.wait_ge(s_cols, 3 * DMA)
                    with sp.Else():
                        for a, b in ((src, src_s), (dst, dst_s), (etype, typ_s)):
                            sp.dma_start(b[0:E], a).then_inc(s_direct, DMA)
                        sp.wait_ge(s_direct, 3 * DMA)
                    sp.drain()

                @block.vector
                def _(dve):
                    flag = dve.value_load(unsorted[0:1, 0:1], min_val=0, max_val=E)
                    with dve.If(flag != 0):
                        dve.wait_ge(s_iota, 2)
                        nc.vector.tensor_scalar(thr[:, 0, :], thr_i[:], 1.0 / 65536, None, ALU.mult).then_inc(s_rk, 1)
                        nc.vector.tensor_scalar(frac[:], gap[:].bitcast(I32), 1.0 / 65536, None, ALU.mult).then_inc(s_rk, 1)
                        dve.wait_ge(s_cols, 3 * DMA)
                        nc.vector.tensor_copy(dcol[:], cols_u[:, 0, :]).then_inc(s_rk, 1)
                        nc.vector.memset(rank[:, 0, :], 0.0).then_inc(s_rk, 1)
                        done = 4
                        for c in range(8):
                            a, b = c % 2, 1 - c % 2
                            dve.wait_ge(s_rk, done)
                            dve.wait_ge(s_row, DMA * (c + 1))
                            nc.vector.tensor_copy(row_f[:], row_i[:]).then_inc(s_rowused, 1)
                            dve.wait_ge(s_rowused, c + 1)
                            with dve.Fori(0, T) as t:
                                nc.vector.scalar_tensor_tensor(gap[:], row_f[:], dcol[:, bass.ds(t, 1)], frac[:],
                                                               ALU.subtract, ALU.add).then_inc(s_rk, 1)
                                dve.wait_ge(s_rk, t * 2 + (done + 1))
                                nc.vector.tensor_scalar(hit[:], gap[:], thr[:, a, bass.ds(t, 1)], None, ALU.is_lt,
                                                        ALU.add, accum_out=below[:, bass.ds(t, 1)]).then_inc(s_rk, 1)
                                dve.wait_ge(s_rk, t * 2 + (done + 2))
                            done += 2 * T
                            nc.vector.tensor_tensor(rank[:, b, :], rank[:, a, :], below[:], ALU.add).then_inc(s_rk, 1)
                            nc.vector.tensor_scalar(thr[:, b, :], thr[:, a, :], -CH / 65536, None, ALU.add).then_inc(s_rk, 1)
                            done += 2
                        dve.wait_ge(s_rk, done)
                        nc.vector.tensor_copy(rank_i[:], rank[:, 0, :]).then_inc(s_ranked, 1)
                        dve.wait_ge(s_ranked, 1)
                    dve.drain()

                @block.gpsimd
                def _(pool):
                    flag = pool.value_load(unsorted[0:1, 0:1], min_val=0, max_val=E)
                    with pool.If(flag != 0):
                        nc.gpsimd.iota(thr_i[:], [[P, T]], base=0, channel_multiplier=1).then_inc(s_iota, 1)
                        nc.gpsimd.iota(gap[:].bitcast(I32), [[1, CH]], base=0, channel_multiplier=0).then_inc(s_iota, 1)
                        pool.wait_ge(s_ranked, 1)
                        pool.wait_ge(s_cols, 3 * DMA)
                        with pool.Fori(0, T // GROUP) as i:
                            col = bass.ds(i * GROUP, GROUP)
                            nc.gpsimd.tensor_copy(stage[:, 3, :], rank_i[:, col]).then_inc(s_staged, 1)
                            for k in range(3):
                                nc.gpsimd.tensor_copy(stage[:, k, :], cols_u[:, k, col]).then_inc(s_staged, 1)
                            wait_apart(pool, s_passed, (s_staged, i * 4 + 4))
                            for k, a in enumerate((dst_s, src_s, typ_s)):
                                for c in range(GROUP):
                                    nc.gpsimd.indirect_dma_start(
                                        a.unsqueeze(1), bass.IndirectOffsetOnAxis(ap=stage[:, 3, c:c + 1], axis=0),
                                        stage[:, k, c:c + 1], None).then_inc(s_spread[k], DMA)
                            wait_apart(pool, s_passed, *[(s_spread[k], i * (DMA * GROUP) + DMA * GROUP) for k in range(3)])
                    pool.drain()

        with ExitStack() as st:
            def row(name, dt=F32):
                return st.enter_context(nc.sbuf_tensor(name, [P, ROW], dt))

            src_i, dst_i = row("src_i", I32), row("dst_i", I32)
            here, prev, succ = row("here"), row("prev"), row("succ")
            index_i, index = row("index_i", I32), row("index")
            starts, first, first_in = row("starts"), row("first"), row("first_in")
            firsts, degree, inverse = row("firsts"), row("degree"), row("inverse")
            ends_run, is_node = row("ends_run"), row("is_node")
            src_r, kept = row("src_r"), row("kept")
            carry = st.enter_context(nc.sbuf_tensor("carry", [1, 2, P], F32))
            carry_col = st.enter_context(nc.sbuf_tensor("carry_col", [P, 1], F32))
            aside_i = st.enter_context(nc.sbuf_tensor("aside_i", [P, T], I32))
            aside = st.enter_context(nc.sbuf_tensor("aside", [P, T], F32))
            kept_c = st.enter_context(nc.sbuf_tensor("kept_c", [P, T], F32))
            ahead = st.enter_context(nc.sbuf_tensor("ahead", [P, T], F32))
            moved = st.enter_context(nc.sbuf_tensor("moved", [P, T], F32))
            zeros = st.enter_context(nc.sbuf_tensor("zeros", [P, 2 * HALF * P], F32))
            GT = T // GROUPS
            TILES_IN_BANK = 512 // (GROUPS * B)
            typ_b = st.enter_context(nc.sbuf_tensor("typ_b", [P, GT * P], I32))
            onehot = st.enter_context(nc.sbuf_tensor("onehot", [P, GT * P], F32))
            own_i = st.enter_context(nc.sbuf_tensor("own_i", [P, P], I32))
            own = st.enter_context(nc.sbuf_tensor("own", [P, 2, P], F32))
            own_type = st.enter_context(nc.sbuf_tensor("own_type", [P, 1], F32))
            coef_ps = [st.enter_context(nc.psum_tensor(f"coef_ps{k}", [P, 512], F32)) for k in range(2)]
            turned = [st.enter_context(nc.psum_tensor(f"turned{k}", [P, 4, P], F32)) for k in range(4)]
            carry_ps = st.enter_context(nc.psum_tensor("carry_ps", [1, P], F32))
            carry_back = st.enter_context(nc.psum_tensor("carry_back", [P, 1], F32))
            s_rows = sem("rows_loaded")
            s_zero = sem("rows_zeroed")
            s_index = sem("index_made")
            s_here = sem("here_made")
            s_dstf = sem("dst_float_stored")
            s_shift = sem("shifts_loaded")
            s_v = sem("row_steps")
            s_lastcol = sem("last_column")
            s_carry = sem("carry_turned")
            s_scan = sem("carry_scanned")
            s_back = sem("carry_back_turned")
            s_ready = sem("row_ready")
            s_turned = sem("row_turned")
            s_col = sem("columns_made")
            s_typ = sem("types_loaded")
            s_one = sem("onehots")
            s_coef_bank, s_coef = sem("coef_bank"), sem("coef_kept")
            s_aside = sem("aside_stored")
            order = [src_r, here, kept, inverse]

            with nc.Block() as block:
                @block.scalar
                def _(act):
                    fill(act, FILLS_EARLY, FILLS_MIDDLE, 1)
                    for n, t in enumerate(range(0, GT, TILES_IN_BANK)):
                        act.wait_ge(s_coef_bank, n + 1)
                        count = min(TILES_IN_BANK, GT - t)
                        nc.scalar.activation(coef[:].rearrange("p (g t) b -> p t g b", g=GROUPS)[:, t:t + count, :, :],
                                             coef_ps[n % 2][:, 0:count * GROUPS * B]
                                             .rearrange("p (t g b) -> p t g b", g=GROUPS, b=B), ACT.Copy).then_inc(s_coef, 1)
                    wait_filled(act, FILLS_MIDDLE - 2)
                    wait_filled(act, FILLS_MIDDLE - 1)

                @block.sync
                def _(sp):
                    sp.wait_ge(s_zero, 2)
                    for a, b in ((dst_s, dst_i), (src_s, src_i)):
                        sp.dma_start(b[0:ROWS, :], a.rearrange("(r k) -> r k", k=ROW)).then_inc(s_rows, DMA)
                    sp.wait_ge(s_here, 1)
                    sp.dma_start(dst_f[1:1 + EP].rearrange("(r k) -> r k", k=ROW), here[0:ROWS, :]).then_inc(s_dstf, DMA)
                    sp.wait_ge(s_dstf, DMA)
                    sp.wait_ge(s_zero, 4)
                    sp.dma_start(prev[0:ROWS, :], dst_f[0:EP].rearrange("(r k) -> r k", k=ROW)).then_inc(s_shift, DMA)
                    sp.dma_start(succ[0:ROWS, :], dst_f[2:2 + EP].rearrange("(r k) -> r k", k=ROW)).then_inc(s_shift, DMA)
                    for g in range(GROUPS):
                        sp.dma_start(typ_b[g * R:(g + 1) * R, :], typ_s[g * GT * P:(g + 1) * GT * P]
                                     .partition_broadcast(R)).then_inc(s_typ, DMA)
                    sp.wait_ge(s_zero, 5)
                    for a in z:
                        sp.dma_start(a[N:N + 2 * HALF * P, :].rearrange("(p s) f -> p (s f)", p=P), zeros[:]).then_inc(s_aside, DMA)
                    sp.wait_ge(s_aside, 2 * DMA)

                @block.gpsimd
                def _(pool):
                    nc.gpsimd.iota(aside_i[:], [[0, T // (2 * HALF)], [P, 2 * HALF]], base=N,
                                   channel_multiplier=1).then_inc(s_index, 1)
                    nc.gpsimd.iota(index_i[:], [[1, ROW]], base=0, channel_multiplier=ROW).then_inc(s_index, 1)
                    nc.gpsimd.iota(own_i[:], [[0, GROUPS], [1, R]], base=0, channel_multiplier=0).then_inc(s_index, 1)

                @block.vector
                def _(dve):
                    chain = [0]

                    def link(ins):
                        chain[0] += 1
                        ins.then_inc(s_v, 1)
                        dve.wait_ge(s_v, chain[0])

                    for a in (dst_i, src_i, prev, succ, zeros):
                        nc.vector.memset(a[:], 0).then_inc(s_zero, 1)
                    dve.wait_ge(s_zero, 5)
                    dve.wait_ge(s_rows, 2 * DMA)
                    nc.vector.tensor_copy(here[:], dst_i[:]).then_inc(s_here, 1)
                    dve.wait_ge(s_here, 1)
                    link(nc.vector.tensor_copy(src_r[:], src_i[:]))
                    dve.wait_ge(s_index, 3)
                    link(nc.vector.tensor_copy(index[:], index_i[:]))
                    dve.wait_ge(s_shift, 2 * DMA)
                    link(nc.vector.tensor_tensor(starts[:], here[:], prev[:], ALU.not_equal))
                    link(nc.vector.tensor_tensor(first_in[:], starts[:], index[:], ALU.mult))
                    link(nc.vector.tensor_tensor_scan(first[:], first_in[:], first_in[:], 0.0, ALU.max, ALU.max))
                    dve.wait_ge(s_v, chain[0])
                    nc.vector.tensor_copy(carry_col[:], first[:, ROW - 1:ROW]).then_inc(s_lastcol, 1)
                    dve.wait_ge(s_carry, 1)
                    link(nc.vector.memset(carry[:, 1, 0:1], 0.0))
                    link(nc.vector.tensor_copy(carry[:, 0, :], carry_ps[:]))
                    link(nc.vector.tensor_tensor_scan(carry[:, 1, 1:P], carry[:, 0, 0:P - 1], carry[:, 0, 0:P - 1], 0.0,
                                                      ALU.max, ALU.max))
                    nc.vector.drain().then_inc(s_scan, 1)
                    dve.wait_ge(s_back, 1)
                    link(nc.vector.tensor_copy(carry_col[:], carry_back[:]))
                    link(nc.vector.tensor_scalar(firsts[:], first[:], carry_col[:], None, ALU.max))
                    link(nc.vector.tensor_tensor(degree[:], index[:], firsts[:], ALU.subtract))
                    link(nc.vector.tensor_scalar(degree[:], degree[:], 1.0, None, ALU.add))
                    link(nc.vector.reciprocal(inverse[:], degree[:]))
                    link(nc.vector.tensor_tensor(ends_run[:], here[:], succ[:], ALU.not_equal))
                    link(nc.vector.tensor_scalar(is_node[:], here[:], float(N), None, ALU.is_lt))
                    link(nc.vector.tensor_tensor(kept[:], ends_run[:], is_node[:], ALU.mult))
                    nc.vector.drain().then_inc(s_ready, 1)
                    link(nc.vector.tensor_copy(own[:, 0, :], own_i[:]))
                    link(nc.vector.tensor_tensor(own[:, 1, :], own[:, 0, :], ident[:], ALU.mult))
                    link(nc.vector.reduce_sum(own_type[:], own[:, 1, :], AX.X))
                    dve.wait_ge(s_typ, GROUPS * DMA)
                    nc.vector.tensor_scalar(onehot[:], typ_b[:], own_type[:], None, ALU.is_equal).then_inc(s_one, 1)
                    for k, col in enumerate((src_c, dst_c, kept_c, inv_c)):
                        dve.wait_ge(s_turned, k + 1)
                        nc.vector.tensor_copy(col[:].rearrange("p (r c) -> p c r", c=4),
                                              turned[k][:, :, 0:ROWS]).then_inc(s_col, 1)
                    dve.wait_ge(s_col, 4)
                    link(nc.vector.tensor_copy(aside[:], aside_i[:]))
                    link(nc.vector.tensor_tensor(ahead[:], dst_c[:], aside[:], ALU.subtract))
                    link(nc.vector.tensor_tensor(moved[:], ahead[:], kept_c[:], ALU.mult))
                    link(nc.vector.tensor_tensor(put_c[:], moved[:], aside[:], ALU.add))

                @block.tensor
                def _(pe):
                    pe.wait_ge(s_lastcol, 1)
                    nc.tensor.matmul(carry_ps[:], carry_col[:], ident[:], start=True, stop=True).then_inc(s_carry, 1)
                    pe.wait_ge(s_scan, 1)
                    nc.tensor.matmul(carry_back[:], carry[:, 1, :], ones[0:1, 0:1], start=True, stop=True).then_inc(s_back, 1)
                    pe.wait_ge(s_ready, 1)
                    for k, a in enumerate(order):
                        for c in range(4):
                            last = nc.tensor.transpose(turned[k][:, c, :], a[:, c * P:(c + 1) * P], ident[:])
                        last.then_inc(s_turned, 1)
                    pe.wait_ge(s_one, 1)
                    for t in range(GT):
                        n, at = t // TILES_IN_BANK, t % TILES_IN_BANK * (GROUPS * B)
                        if n >= 2 and at == 0:
                            pe.wait_ge(s_coef, n - 1)
                        last = nc.tensor.matmul(coef_ps[n % 2][:, at:at + GROUPS * B], onehot[:, t * P:(t + 1) * P], comp[:],
                                                start=True, stop=True)
                        if t % TILES_IN_BANK == TILES_IN_BANK - 1 or t == GT - 1:
                            last.then_inc(s_coef_bank, 1)

        def clear(held):
            nc.clear_and_free_semaphores(held)
            nc.all_engine_barrier()

        def relational_pass():
            held = []
            lag = 3
            with ExitStack() as st:
                def buf(name, shape, dt=F32):
                    return st.enter_context(nc.sbuf_tensor(f"{name}_rel", shape, dt))

                def bank(name, shape):
                    return st.enter_context(nc.psum_tensor(f"{name}_rel", shape, F32))

                def psem(name):
                    held.append(nc.alloc_semaphore(f"{name}_rel"))
                    return held[-1]

                gat = buf("gat", [P, 2, HALF, P])
                rows = buf("rows", [P, 2, HALF, P])
                gidx = buf("gidx", [P, 2, HALF], I32)
                pidx = buf("pidx", [P, 2, HALF], I32)
                dst_b = buf("dst_b", [P, 2, HALF * P + 1])
                same = buf("same", [P, 2, HALF, P])
                open_ = buf("open", [P, 2, HALF, P])
                sums = buf("sums", [P, HALF, P])
                sum_ps = [bank(f"sum_ps{i}", [P, 512]) for i in range(2)]
                row_ps = bank("row_ps", [P, 512])
                s_gathered = [[psem(f"gathered{q}{j}") for j in range(HALF)] for q in range(2)]
                s_scattered = [[psem(f"scattered{q}{j}") for j in range(HALF)] for q in range(2)]
                s_gidx, s_pidx = psem("gather_index"), psem("scatter_index")
                s_dstb = [psem(f"dst_b{q}") for q in range(2)]
                s_same, s_open = psem("same_made"), psem("open_made")
                s_summed = psem("summed")
                s_carried = psem("carried")
                s_rowed = psem("rowed")
                s_rows = psem("rows_ready")
                s_start = psem("carry_zeroed")
                s_passed, s_dve_passed = psem("pool_passed"), psem("dve_passed")
                st6 = buf("st6", [P, 2, HALF, 6])
                mv = buf("mv", [P, 2, HALF, 2])
                var = buf("var", [P, 2, HALF])
                std = buf("std", [P, 2, HALF])
                rstd = buf("rstd", [P, 2, HALF])
                shift = buf("shift", [P, 2, HALF])
                h = buf("h", [P, 2, HALF, P])
                ht = buf("ht", [P, 2, HALF, P])
                part = buf("part", [P, 2, BASES_ON_ACT, P])
                two = buf("two", [P, HALF, 2, P])
                sums_b = buf("sums_b", [P, HALF, P])
                y_ps = [bank(f"y_ps{i}", [P, Y]) for i in range(2)]
                ht_ps = bank("ht_ps", [P, 512])
                s_stat, s_mv, s_var = psem("stats"), psem("mean_var"), psem("var_eps")
                s_std, s_rstd, s_shift = psem("std"), psem("rstd"), psem("shift")
                s_h, s_turn, s_ht = psem("h"), psem("turned"), psem("ht")
                s_y_high, s_y, s_part, s_acc = psem("y_high"), psem("y"), psem("part"), psem("acc")
                s_biased = psem("biased")
                EASED = 4
                PAIRS = -(-FILLS // 2)
                border_i = buf("border_i", [1, 2, PAIRS], I32)
                border = buf("border", [1, 2, PAIRS])
                reached = buf("reached", [1, EASED, 2 * PAIRS])
                counts = buf("counts", [1, 2, EASED * 2])
                need = buf("need", [1, EASED * 2], I32)
                s_border, s_counts, s_need = psem("borders_made"), psem("counting"), psem("need_made")

                def tile(m, j):
                    return m * HALF + (j + 1)

                def use(m, q):
                    return (m // 2 + 1) * DMA if isinstance(m, int) else (m - q) * (DMA // 2) + DMA

                def group(m, a):
                    return m * 2 + (a + 1)

                def ago(m, q, j, n, what):
                    if j >= n:
                        what(m, q, j - n)
                    elif at_least(m, 1):
                        what(m - 1, 1 - q, HALF + j - n)

                with nc.Block() as block:
                    @block.gpsimd
                    def _(pool):
                        nc.gpsimd.iota(border_i[:], [[FILL, 2], [2 * FILL, PAIRS]], base=0,
                                       channel_multiplier=0).then_inc(s_border, 1)

                        def wait_bias(pool, o):
                            if o < EASED:
                                if o == 0:
                                    pool.wait_ge(s_need, 1)
                                values = [pool.value_load(need[0:1, o * 2 + k:o * 2 + k + 1], min_val=DMA,
                                                          max_val=DMA * PAIRS) for k in range(2)]
                                for k in range(2):
                                    pool.wait_ge(s_filled[k], values[k])
                            elif o == EASED:
                                wait_filled(pool, FILLS - 2)
                                wait_filled(pool, FILLS - 1)

                        def step(m, q, i):
                            if before(m, HALVES):
                                if at_least(m, 2):
                                    pool.wait_ge(s_h, tile(m - 2, HALF - 1))
                                nc.gpsimd.tensor_copy(gidx[:, q, :], src_c[:, bass.ds(m * HALF, HALF)]).then_inc(s_gidx, 1)
                            if at_least(m, lag):
                                o, oq = m - lag, (q - lag) % 2
                                if at_least(m, lag + 2):
                                    for j in range(HALF):
                                        pool.wait_ge(s_scattered[oq][j], use(o - 2, oq))
                                nc.gpsimd.tensor_copy(pidx[:, oq, :], put_c[:, bass.ds(o * HALF, HALF)]).then_inc(s_pidx, 1)
                            wait_apart(pool, s_passed, *[(s_gidx, m + 1)] * before(m, HALVES),
                                       *[(s_pidx, m + (1 - lag))] * at_least(m, lag))
                            for j in range(HALF):
                                if before(m, HALVES):
                                    nc.gpsimd.indirect_dma_start(
                                        gat[:, q, j, :], None, x,
                                        bass.IndirectOffsetOnAxis(ap=gidx[:, q, j:j + 1], axis=0)).then_inc(s_gathered[q][j], DMA)
                                if at_least(m, lag):
                                    if isinstance(m, int) and j == 0:
                                        wait_bias(pool, o)
                                    wait_apart(pool, s_passed, (s_rows, tile(o, j)))
                                    nc.gpsimd.indirect_dma_start(
                                        agg, bass.IndirectOffsetOnAxis(ap=pidx[:, oq, j:j + 1], axis=0),
                                        rows[:, oq, j, :], None, bounds_check=N - 1,
                                        oob_is_err=False).then_inc(s_scattered[oq][j], DMA)

                        steps(pool, step, lag + EASED + 1, HALVES, HALVES + lag, 2)
                        for q in range(2):
                            for j in range(HALF):
                                pool.wait_ge(s_scattered[q][j], DMA * HALVES // 2)

                    @block.sync
                    def _(sp):
                        SHARES = 4
                        rest = FILLS - FILLS_MIDDLE

                        def step(m, q, i):
                            if at_least(m, 2):
                                sp.wait_ge(s_same, m - 1)
                                sp.wait_ge(s_open, m - 1)
                            sp.dma_start(dst_b[:, q, :], dst_f[bass.ds(m * (HALF * P), HALF * P + 1)]
                                         .partition_broadcast(P)).then_inc(s_dstb[q], DMA)
                            if isinstance(m, int) and m < SHARES:
                                fill(sp, FILLS_MIDDLE + rest * m // SHARES, FILLS_MIDDLE + rest * (m + 1) // SHARES, 2)

                        steps(sp, step, 4, HALVES, HALVES, 2)

                    @block.vector
                    def _(dve):
                        nc.vector.memset(sums[:, HALF - 1, :], 0.0).then_inc(s_start, 1)
                        dve.wait_ge(s_start, 1)

                        dve.wait_ge(s_border, 1)
                        nc.vector.tensor_copy(border[:], border_i[:]).then_inc(s_counts, 1)
                        dve.wait_ge(s_counts, 1)
                        following = dst_c[0:1, :].rearrange("o (m j) -> o m j", j=HALF)[:, 1:1 + EASED, 0]
                        nc.vector.tensor_tensor(reached[:], border[:].rearrange("o a k -> o (a k)").unsqueeze(1)
                                                .to_broadcast([1, EASED, 2 * PAIRS]),
                                                following.unsqueeze(2).to_broadcast([1, EASED, 2 * PAIRS]),
                                                ALU.is_le).then_inc(s_counts, 1)
                        dve.wait_ge(s_counts, 2)
                        nc.vector.reduce_sum(counts[:, 0, :], reached[:].rearrange("o m (a k) -> o (m a) k", k=PAIRS),
                                             AX.X).then_inc(s_counts, 1)
                        dve.wait_ge(s_counts, 3)
                        nc.vector.tensor_scalar(counts[:, 1, :], counts[:, 0, :], 1.0, float(DMA), ALU.max,
                                                ALU.mult).then_inc(s_counts, 1)
                        dve.wait_ge(s_counts, 4)
                        nc.vector.tensor_copy(need[:], counts[:, 1, :]).then_inc(s_need, 1)

                        def columns(q):
                            return dst_b[:, q, 1:HALF * P + 1].rearrange("p (t e) -> p t e", e=P)

                        def select(m, q):
                            dve.wait_ge(s_dstb[q], use(m, q))
                            if at_least(m, 2):
                                dve.wait_ge(s_summed, tile(m - 2, HALF - 1))
                            nc.vector.tensor_tensor(same[:, q, :, :], columns(q),
                                                    dst_c[:, bass.ds(m * HALF, HALF)].unsqueeze(2).to_broadcast([P, HALF, P]),
                                                    ALU.is_equal).then_inc(s_same, 1)

                        def find_open(m, q):
                            dve.wait_ge(s_dstb[q], use(m, q))
                            if at_least(m, 2):
                                dve.wait_ge(s_carried, tile(m - 2, HALF - 1))
                            before_ = dst_b[:, q, 0:HALF * P].rearrange("p (t e) -> p t e", e=P)[:, :, 0:1]
                            nc.vector.tensor_tensor(open_[:, q, :, :], columns(q), before_.to_broadcast([P, HALF, P]),
                                                    ALU.is_equal).then_inc(s_open, 1)

                        def stats(m, q, lo, hi):
                            for j in range(lo, hi):
                                dve.wait_ge(s_gathered[q][j], use(m, q))
                                nc.vector.bn_stats(st6[:, q, j, :], gat[:, q, j, :]).then_inc(s_stat, 1)

                        def mean_var(m, q):
                            for j in range(HALF):
                                wait_apart(dve, s_dve_passed, (s_stat, tile(m, j)))
                                nc.vector.bn_aggr(mv[:, q, j, :], st6[:, q, j, :]).then_inc(s_mv, 1)
                            dve.wait_ge(s_mv, tile(m, HALF - 1))
                            nc.vector.tensor_scalar(var[:, q, :], mv[:, q, :, 1], EPS, None, ALU.add).then_inc(s_var, 1)

                        def scales(m, q):
                            dve.wait_ge(s_std, m + 1)
                            if at_least(m, 2):
                                dve.wait_ge(s_h, tile(m - 2, HALF - 1))
                            nc.vector.reciprocal(rstd[:, q, :], std[:, q, :]).then_inc(s_rstd, 1)
                            dve.wait_ge(s_rstd, m + 1)
                            nc.vector.scalar_tensor_tensor(shift[:, q, :], mv[:, q, :, 0], -1.0, rstd[:, q, :],
                                                           ALU.mult, ALU.mult).then_inc(s_shift, 1)

                        def message(m, q, j):
                            y = y_ps[(q + j) % 2]
                            acc = two[:, j, :, :]
                            dve.wait_ge(s_part, tile(m, j))
                            if at_least(m, 1):
                                dve.wait_ge(s_summed, tile(m, j) - HALF)
                            for n, b in enumerate((4, 5, 0, 1, 2, 3)):
                                a = n % 2
                                c = coef[:, bass.ds(m * HALF + j, 1), b]
                                prior = part[:, (q + j) % 2, a, :] if n < 2 else acc[:, a, :]
                                if n == 2:
                                    dve.wait_ge(s_y, tile(m, j))
                                if n >= 2:
                                    dve.wait_ge(s_acc, (m * HALF + j) * 6 + (n - 1))
                                nc.vector.scalar_tensor_tensor(acc[:, a, :], y[:, b * P:(b + 1) * P], c, prior,
                                                               ALU.mult, ALU.add).then_inc(s_acc, 1)

                        def carry_on(m, q, j):
                            dve.wait_ge(s_summed, tile(m, j))
                            if at_least(m, 1) or j >= 1:
                                dve.wait_ge(s_carried, tile(m, j) - 1)
                            if j == 0:
                                dve.wait_ge(s_open, m + 1)
                            if at_least(m, 1):
                                dve.wait_ge(s_biased, tile(m, j) - HALF)
                            nc.vector.scalar_tensor_tensor(sums[:, j, :], open_[:, q, j, :],
                                                           sums[:, (j - 1) % HALF, P - 1:P], sum_ps[(q + j) % 2][:, 0:P],
                                                           ALU.mult, ALU.add).then_inc(s_carried, 1)

                        def step(m, q, i):
                            more = before(m, HALVES - 1)
                            for j in range(HALF):
                                message(m, q, j)
                                ago(m, q, j, 2, carry_on)
                                if more and j == 0:
                                    stats(m + 1, 1 - q, 0, 4)
                                if more and j == 1:
                                    stats(m + 1, 1 - q, 4, HALF)
                                    mean_var(m + 1, 1 - q)
                                if more and j == 2:
                                    scales(m + 1, 1 - q)
                                if more and j == 4:
                                    select(m + 1, 1 - q)
                                if more and j == 5:
                                    find_open(m + 1, 1 - q)

                        stats(0, 0, 0, HALF)
                        mean_var(0, 0)
                        scales(0, 0)
                        select(0, 0)
                        find_open(0, 0)
                        steps(dve, step, 4, HALVES - 2, HALVES, 2)
                        for j in range(2):
                            ago(HALVES, 0, j, 2, carry_on)

                    @block.scalar
                    def _(act):
                        def deviation(m, q):
                            act.wait_ge(s_var, m + 1)
                            nc.scalar.activation(std[:, q, :], var[:, q, :], ACT.Sqrt).then_inc(s_std, 1)

                        def normalize(m, q, j):
                            act.wait_ge(s_shift, m + 1)
                            if at_least(m, 2):
                                act.wait_ge(s_turn, group(m - 2, 1))
                            nc.scalar.activation(h[:, q, j, :], gat[:, q, j, :], ACT.Relu, bias=shift[:, q, j:j + 1],
                                                 scale=rstd[:, q, j:j + 1]).then_inc(s_h, 1)

                        def keep_turned(m, q, a):
                            lo, hi = (0, 4) if a == 0 else (4, HALF)
                            act.wait_ge(s_turn, group(m, a))
                            if at_least(m, 2):
                                act.wait_ge(s_y, tile(m - 2, HALF - 1))
                            nc.scalar.activation(ht[:, q, lo:hi, :], ht_ps[:, 0:(hi - lo) * P]
                                                 .rearrange("p (t e) -> p t e", e=P), ACT.Copy).then_inc(s_ht, 1)

                        def begin(m, q, j):
                            s = (q + j) % 2
                            act.wait_ge(s_y_high, tile(m, j))
                            if at_least(m, 1) or j >= 2:
                                act.wait_ge(s_acc, (m * HALF + j) * 6 - 10)
                            for a in range(BASES_ON_ACT):
                                b = B - BASES_ON_ACT + a
                                last = nc.scalar.activation(part[:, s, a, :], y_ps[s][:, b * P:(b + 1) * P], ACT.Copy,
                                                            scale=coef[:, bass.ds(m * HALF + j, 1), b])
                            last.then_inc(s_part, 1)

                        def add_bias(m, q, j):
                            act.wait_ge(s_carried, tile(m, j))
                            if at_least(m, 1):
                                act.wait_ge(s_rowed, tile(m, j) - HALF)
                            nc.scalar.activation(sums_b[:, j, :], sums[:, j, :], ACT.Identity,
                                                 bias=hb_col[:]).then_inc(s_biased, 1)

                        def keep_rows(m, q, j):
                            act.wait_ge(s_rowed, tile(m, j))
                            if at_least(m, 2):
                                act.wait_ge(s_scattered[q][j], use(m - 2, q))
                            nc.scalar.activation(rows[:, q, j, :], row_ps[:, 0:P], ACT.Copy).then_inc(s_rows, 1)

                        def step(m, q, i):
                            more = before(m, HALVES - 1)
                            for j in range(HALF):
                                begin(m, q, j)
                                ago(m, q, j, 4, add_bias)
                                ago(m, q, j, 6, keep_rows)
                                if j == 0 and at_least(m, 1):
                                    keep_turned(m, q, 1)
                                if more and j == 2:
                                    deviation(m + 1, 1 - q)
                                if more and j >= 3:
                                    for t in ((0, 1), (2, 3), (4, 5), (6,))[j - 3]:
                                        normalize(m + 1, 1 - q, t)
                                if more and j == 5:
                                    keep_turned(m + 1, 1 - q, 0)

                        deviation(0, 0)
                        for j in range(HALF):
                            normalize(0, 0, j)
                        keep_turned(0, 0, 0)
                        keep_turned(0, 0, 1)
                        steps(act, step, 4, HALVES - 2, HALVES, 2)
                        for j in range(6):
                            if j < 4:
                                ago(HALVES, 0, j, 4, add_bias)
                            ago(HALVES, 0, j, 6, keep_rows)

                    @block.tensor
                    def _(pe):
                        def turn(m, q, a):
                            lo, hi = (0, 4) if a == 0 else (4, HALF)
                            pe.wait_ge(s_h, tile(m, hi - 1))
                            if at_least(m, 1) or a:
                                pe.wait_ge(s_ht, group(m, a) - 1)
                            for t in range(lo, hi):
                                last = nc.tensor.transpose(ht_ps[:, (t - lo) * P:(t - lo + 1) * P], h[:, q, t, :], ident[:])
                            last.then_inc(s_turn, 1)

                        def products(m, q, j):
                            pe.wait_ge(s_ht, group(m, 0 if j < 4 else 1))
                            for c, done in ((1, s_y_high), (0, s_y)):
                                if at_least(m, 1) or j >= 2:
                                    pe.wait_ge(s_acc, (m * HALF + j) * 6 - (10 if c else 6))
                                nc.tensor.matmul(y_ps[(q + j) % 2][:, c * 512:(c + 1) * 512], ht[:, q, j, :],
                                                 w_basis[:, 4 * c:4 * c + 4, :], start=True, stop=True).then_inc(done, 1)

                        def sum_runs(m, q, j):
                            pe.wait_ge(s_acc, (m * HALF + j) * 6 + 6)
                            if j == 0:
                                pe.wait_ge(s_same, m + 1)
                            if at_least(m, 1) or j >= 2:
                                pe.wait_ge(s_carried, tile(m, j) - 2)
                            s = (q + j) % 2
                            for a in range(2):
                                last = nc.tensor.matmul(sum_ps[s][:, 0:P], two[:, j, a, :], same[:, q, j, :],
                                                        start=(a == 0), stop=(a == 1))
                            last.then_inc(s_summed, 1)

                        def to_rows(m, q, j):
                            pe.wait_ge(s_biased, tile(m, j))
                            if at_least(m, 1) or j >= 1:
                                pe.wait_ge(s_rows, tile(m, j) - 1)
                            nc.tensor.transpose(row_ps[:, 0:P], sums_b[:, j, :], ident[:]).then_inc(s_rowed, 1)

                        def step(m, q, i):
                            for j in range(HALF):
                                products(m, q, j)
                                ago(m, q, j, 2, sum_runs)
                                ago(m, q, j, 6, to_rows)
                                if before(m, HALVES - 1) and j in (5, 6):
                                    turn(m + 1, 1 - q, j - 5)

                        turn(0, 0, 0)
                        turn(0, 0, 1)
                        steps(pe, step, 4, HALVES - 2, HALVES, 2)
                        for j in range(6):
                            if j < 2:
                                ago(HALVES, 0, j, 2, sum_runs)
                            ago(HALVES, 0, j, 6, to_rows)
            clear(held)

        def norm_pass():
            TAIL = BLOCKS // SLOTS * SLOTS
            held = []
            with ExitStack() as st:
                def buf(name, shape, dt=F32):
                    return st.enter_context(nc.sbuf_tensor(f"{name}_norm", shape, dt))

                def bank(name):
                    return st.enter_context(nc.psum_tensor(f"{name}_norm", [P, BLOCK], F32))

                def psem(name):
                    held.append(nc.alloc_semaphore(f"{name}_norm"))
                    return held[-1]

                node = buf("node", [P, SLOTS, BLOCK])
                term = buf("term", [P, SLOTS, BLOCK])
                base = buf("base", [P, SLOTS, BLOCK])
                done = buf("done", [P, SLOTS, BLOCK])
                st6 = buf("st6", [P, SLOTS, NB, 6])
                mv = buf("mv", [P, SLOTS, NB, 2])
                var = buf("var", [P, SLOTS, NB])
                std = buf("std", [P, SLOTS, NB])
                rstd = buf("rstd", [P, SLOTS, NB])
                shift = buf("shift", [P, SLOTS, NB])
                h = buf("h", [P, 2, BLOCK])
                ht = buf("ht", [P, 2, BLOCK])
                tmp = buf("tmp", [P, 2, BLOCK])
                ht_ps = [bank(f"ht_ps{i}") for i in range(2)]
                z_ps = [bank(f"z_ps{i}") for i in range(2)]
                s_node = [psem(f"node{q}") for q in range(SLOTS)]
                s_x1 = [psem(f"x1_{q}") for q in range(SLOTS)]
                s_kept = [psem(f"stored{q}") for q in range(SLOTS)]
                s_base, s_stat, s_mv, s_var = psem("base"), psem("stats"), psem("mean_var"), psem("var_eps")
                s_std, s_rstd, s_shift, s_h = psem("std"), psem("rstd"), psem("shift"), psem("h")
                s_turn, s_ht, s_z = psem("turned"), psem("ht"), psem("z")
                s_tenth, s_done, s_passed = psem("tenth"), psem("done"), psem("dve_passed")

                def use(i, n=1):
                    return i * (n * DMA) + n * DMA

                def earlier(m, q, i, n, what):
                    what(m - n, (q - n) % SLOTS, i if q >= n else i - 1)

                with nc.Block() as block:
                    @block.sync
                    def _(sp):
                        def load(m, q, i):
                            if at_least(m, SLOTS):
                                sp.wait_ge(s_base, m - (SLOTS - 1))
                            sp.dma_start(node[:, q, :], rows_of(x, base_of(m))).then_inc(s_node[q], DMA)
                            sp.dma_start(term[:, q, :], rows_of(agg, base_of(m))).then_inc(s_node[q], DMA)

                        def store_x1(m, q, i):
                            sp.wait_ge(s_h, m + 1)
                            if isinstance(m, int) and m == BLOCKS - 1:
                                sp.wait_ge(s_x1[(q - 1) % SLOTS], use(i))
                            sp.dma_start(rows_of(x1, base_of(m)), base[:, q, :]).then_inc(s_x1[q], DMA)

                        def store(m, q, i):
                            sp.wait_ge(s_done, m + 1)
                            if isinstance(m, int) and m == BLOCKS - 1:
                                sp.wait_ge(s_kept[(q - 1) % SLOTS], use(i))
                            sp.dma_start(rows_of(g0, base_of(m)), done[:, q, :]).then_inc(s_kept[q], DMA)

                        def step(m, q, i):
                            if before(m, BLOCKS):
                                load(m, q, i)
                            if at_least(m, 6) and before(m, BLOCKS + 6):
                                earlier(m, q, i, 6, store_x1)
                            if at_least(m, SLOTS):
                                store(m - SLOTS, q, i - 1)

                        steps(sp, step, SLOTS, TAIL, BLOCKS + SLOTS, SLOTS)
                        for q in range(SLOTS):
                            sp.wait_ge(s_kept[q], DMA * len(range(q, BLOCKS, SLOTS)))
                            sp.wait_ge(s_x1[q], DMA * len(range(q, BLOCKS, SLOTS)))

                    @block.tensor
                    def _(pe):
                        def turn(m, q, i):
                            pe.wait_ge(s_h, m + 1)
                            if at_least(m, 2):
                                pe.wait_ge(s_ht, m - 1)
                            for j in range(NB):
                                last = nc.tensor.transpose(ht_ps[q % 2][:, j * P:(j + 1) * P],
                                                           h[:, q % 2, j * P:(j + 1) * P], ident[:])
                            last.then_inc(s_turn, 1)

                        def product(m, q, i):
                            pe.wait_ge(s_ht, m + 1)
                            if at_least(m, 2):
                                pe.wait_ge(s_done, m - 1)
                            nc.tensor.matmul(z_ps[q % 2][:], ones_bf[0:96, :],
                                             bias_parts[0:96, 0, :].unsqueeze(1).to_broadcast([96, NB, P]),
                                             start=True, stop=False)
                            for j in range(NB):
                                last = nc.tensor.matmul(z_ps[q % 2][:, j * P:(j + 1) * P], ht[:, q % 2, j * P:(j + 1) * P],
                                                        w_enc[:], start=False, stop=(j == NB - 1))
                            last.then_inc(s_z, 1)

                        def step(m, q, i):
                            if before(m, BLOCKS):
                                turn(m, q, i)
                            if at_least(m, 1):
                                earlier(m, q, i, 1, product)

                        steps(pe, step, SLOTS, TAIL, BLOCKS + 1, SLOTS)

                    @block.scalar
                    def _(act):
                        def deviation(m, q):
                            act.wait_ge(s_var, m + 1)
                            nc.scalar.activation(std[:, q, :], var[:, q, :], ACT.Sqrt).then_inc(s_std, 1)

                        def normalize(m, q, i):
                            s = q % 2
                            act.wait_ge(s_shift, m + 1)
                            if at_least(m, 2):
                                act.wait_ge(s_turn, m - 1)
                            for j in range(NB):
                                last = nc.scalar.activation(h[:, s, j * P:(j + 1) * P], base[:, q, j * P:(j + 1) * P],
                                                            ACT.Relu, bias=shift[:, q, j:j + 1], scale=rstd[:, q, j:j + 1])
                            last.then_inc(s_h, 1)

                        def tenth(m, q, i):
                            act.wait_ge(s_z, m + 1)
                            if at_least(m, 2):
                                act.wait_ge(s_done, m - 1)
                            nc.scalar.activation(tmp[:, q % 2, :], z_ps[q % 2][:], ACT.Copy, scale=SLOPE).then_inc(s_tenth, 1)

                        def keep_turned(m, q, i):
                            act.wait_ge(s_turn, m + 1)
                            if at_least(m, 2):
                                act.wait_ge(s_z, m - 1)
                            nc.scalar.activation(ht[:, q % 2, :], ht_ps[q % 2][:], ACT.Copy).then_inc(s_ht, 1)

                        def step(m, q, i):
                            if before(m, BLOCKS):
                                normalize(m, q, i)
                            if at_least(m, 2):
                                earlier(m, q, i, 2, tenth)
                            if at_least(m, 1) and before(m, BLOCKS + 1):
                                earlier(m, q, i, 1, keep_turned)
                            if before(m, BLOCKS - 2):
                                deviation(m + 2, (q + 2) % SLOTS)

                        deviation(0, 0)
                        deviation(1, 1)
                        steps(act, step, SLOTS, TAIL, BLOCKS + 2, SLOTS)

                    @block.vector
                    def _(dve):
                        def add(m, q, i):
                            dve.wait_ge(s_node[q], use(i, 2))
                            if at_least(m, SLOTS):
                                dve.wait_ge(s_h, m - (SLOTS - 1))
                                dve.wait_ge(s_x1[q], use(i - 1))
                            nc.vector.tensor_tensor(base[:, q, :], node[:, q, :], term[:, q, :], ALU.add).then_inc(s_base, 1)

                        def stats(m, q):
                            dve.wait_ge(s_base, m + 1)
                            for j in range(NB):
                                nc.vector.bn_stats(st6[:, q, j, :], base[:, q, j * P:(j + 1) * P]).then_inc(s_stat, 1)
                            for j in range(NB):
                                wait_apart(dve, s_passed, (s_stat, m * NB + (j + 1)))
                                nc.vector.bn_aggr(mv[:, q, j, :], st6[:, q, j, :]).then_inc(s_mv, 1)
                            dve.wait_ge(s_mv, m * NB + NB)
                            nc.vector.tensor_scalar(var[:, q, :], mv[:, q, :, 1], EPS, None, ALU.add).then_inc(s_var, 1)

                        def invert(m, q):
                            dve.wait_ge(s_std, m + 1)
                            nc.vector.reciprocal(rstd[:, q, :], std[:, q, :]).then_inc(s_rstd, 1)

                        def shifts(m, q):
                            dve.wait_ge(s_rstd, m + 1)
                            nc.vector.scalar_tensor_tensor(shift[:, q, :], mv[:, q, :, 0], -1.0, rstd[:, q, :],
                                                           ALU.mult, ALU.mult).then_inc(s_shift, 1)

                        def leaky(m, q, i):
                            dve.wait_ge(s_tenth, m + 1)
                            if at_least(m, SLOTS):
                                dve.wait_ge(s_kept[q], use(i - 1))
                            nc.vector.tensor_tensor(done[:, q, :], z_ps[q % 2][:], tmp[:, q % 2, :],
                                                    ALU.max).then_inc(s_done, 1)

                        def step(m, q, i):
                            if before(m, BLOCKS - 2):
                                add(m + 2, (q + 2) % SLOTS, i if q < SLOTS - 2 else i + 1)
                            if before(m, BLOCKS - 1):
                                invert(m + 1, (q + 1) % SLOTS)
                            if at_least(m, 3):
                                earlier(m, q, i, 3, leaky)
                            if before(m, BLOCKS - 1):
                                shifts(m + 1, (q + 1) % SLOTS)
                            if before(m, BLOCKS - 2):
                                stats(m + 2, (q + 2) % SLOTS)

                        for m in range(2):
                            add(m, m, 0)
                            stats(m, m)
                        invert(0, 0)
                        shifts(0, 0)
                        steps(dve, step, 2 * SLOTS, TAIL, BLOCKS + 3, SLOTS)
            clear(held)

        class Sweep:
            def __init__(self, psem, name, layer, first, walk):
                self.layer, self.first, self.walk = layer, first, walk
                self.source, self.result = (g0, z[0]) if layer == 0 else (z[0], z[1])
                self.s_node = [psem(f"{name}_node{c}") for c in range(walk)]
                self.s_stored = [psem(f"{name}_stored{c}") for c in range(walk)]
                self.s_leaky, self.s_turn = psem(f"{name}_leaky"), psem(f"{name}_turned")
                self.s_ht, self.s_z, self.s_done = psem(f"{name}_ht"), psem(f"{name}_z"), psem(f"{name}_done")

            def block(self, i, c):
                return base_of(self.first + (i * self.walk + c))

            def bank_used(self, i, c):
                return i * self.walk + (c if c == 0 and self.walk % 2 else c - 1)

            def earlier(self, i, c, n, what):
                if c >= n:
                    what(i, c - n)
                elif at_least(i, 1):
                    what(i - 1, self.walk + c - n)

        def layer_pass(l, source, result):
            held = []
            with ExitStack() as st:
                def buf(name, shape, dt=F32):
                    return st.enter_context(nc.sbuf_tensor(f"{name}_l{l}", shape, dt))

                def bank(name):
                    return st.enter_context(nc.psum_tensor(f"{name}_l{l}", [P, 512], F32))

                def psem(name):
                    held.append(nc.alloc_semaphore(f"{name}_l{l}"))
                    return held[-1]

                gat = buf("gat", [P, 2, HALF, P])
                act_gat = buf("act_gat", [P, 2, HALF, P]) if l else gat
                rows = buf("rows", [P, 2, HALF, P])
                gidx = buf("gidx", [P, 2, HALF], I32)
                pidx = buf("pidx", [P, 2, HALF], I32)
                dst_b = buf("dst_b", [P, 2, HALF * P + 1])
                same = buf("same", [P, 2, HALF, P])
                open_ = buf("open", [P, 2, HALF, P])
                sums = buf("sums", [P, HALF, P])
                sum_ps = [bank(f"sum_ps{i}") for i in range(2)]
                row_ps = [bank(f"row_ps{i}") for i in range(2)]
                s_gathered = [[psem(f"gathered{q}{j}") for j in range(HALF)] for q in range(2)]
                s_added = [[psem(f"added{q}{j}") for j in range(HALF)] for q in range(2)]
                s_gidx, s_pidx, s_passed = psem("gather_index"), psem("scatter_index"), psem("pool_passed")
                s_dstb = [psem(f"dst_b{q}") for q in range(2)]
                s_same, s_open, s_leaked = psem("same_made"), psem("open_made"), psem("leaked")
                s_summed, s_carried, s_rowed = psem("summed"), psem("carried"), psem("rowed")
                s_rows, s_start = psem("rows_ready"), psem("carry_zeroed")
                s_spilled = [psem(f"spilled{q}") for q in range(2)]
                s_back = [psem(f"back{q}") for q in range(2)]
                node = buf("node", [P, WALK, BLOCK])
                ht = buf("ht", [P, 2, BLOCK])
                done = buf("done", [P, WALK, BLOCK])
                ht_ps = [bank(f"ht_ps{i}") for i in range(2)]
                z_ps = [bank(f"z_ps{i}") for i in range(2)]
                sweep = Sweep(psem, "sweep", 0, 0, WALK) if l == 0 else Sweep(psem, "sweep", 1, AHEAD, 6)
                span = 4 if l else 2
                walks = HALVES // span
                ahead = Sweep(psem, "ahead", 1, 0, WALK) if l == 0 else None

                def tile(m, j):
                    return m * HALF + (j + 1)

                def use(m, q):
                    return (m // 2 + 1) * DMA if isinstance(m, int) else (m - q) * (DMA // 2) + DMA

                def turn_of(i):
                    return (i + 1) * DMA

                def blocks(r):
                    if l:
                        return [[(2, 0)], [(0, 1), (4, 2)], [(2, 3)], [(0, 4), (4, 5)]][r]
                    return [[(0, 0), (2, 1), (4, 2), (6, 3)], [(1, 4), (3, 5), (5, 6)]][r]

                def load_node(eng, w, i, c):
                    eng.dma_start(node[:, c, :], rows_of(w.source, w.block(i, c))).then_inc(w.s_node[c], DMA)

                def leak_node(dve, w, i, c):
                    dve.wait_ge(w.s_node[c], turn_of(i))
                    nc.vector.scalar_tensor_tensor(node[:, c, :], node[:, c, :], SLOPE, node[:, c, :],
                                                   ALU.mult, ALU.max).then_inc(w.s_leaky, 1)

                def turn(pe, w, i, c):
                    if w.layer:
                        pe.wait_ge(w.s_leaky, i * w.walk + (c + 1))
                    else:
                        pe.wait_ge(w.s_node[c], turn_of(i))
                    if at_least(i, 1) or c >= 2:
                        pe.wait_ge(w.s_ht, w.bank_used(i, c))
                    for j in range(NB):
                        last = nc.tensor.transpose(ht_ps[c % 2][:, j * P:(j + 1) * P],
                                                   node[:, c, j * P:(j + 1) * P], ident[:])
                    last.then_inc(w.s_turn, 1)

                def keep_turned(act, w, i, c):
                    act.wait_ge(w.s_turn, i * w.walk + (c + 1))
                    if at_least(i, 1) or c >= 2:
                        act.wait_ge(w.s_z, w.bank_used(i, c))
                    nc.scalar.activation(ht[:, c % 2, :], ht_ps[c % 2][:], ACT.Copy).then_inc(w.s_ht, 1)

                def product(pe, w, i, c):
                    pe.wait_ge(w.s_ht, i * w.walk + (c + 1))
                    if at_least(i, 1) or c >= 2:
                        pe.wait_ge(w.s_done, w.bank_used(i, c))
                    nc.tensor.matmul(z_ps[c % 2][:], ones_bf[0:96, :],
                                     bias_parts[0:96, 1 + w.layer, :].unsqueeze(1).to_broadcast([96, NB, P]),
                                     start=True, stop=False)
                    for j in range(NB):
                        last = nc.tensor.matmul(z_ps[c % 2][:, j * P:(j + 1) * P], ht[:, c % 2, j * P:(j + 1) * P],
                                                w_r[:, w.layer, :], start=False, stop=(j == NB - 1))
                    last.then_inc(w.s_z, 1)

                def keep_product(act, w, i, c):
                    act.wait_ge(w.s_z, i * w.walk + (c + 1))
                    if at_least(i, 1):
                        act.wait_ge(w.s_stored[c], turn_of(i - 1))
                    nc.scalar.activation(done[:, c, :], z_ps[c % 2][:], ACT.Copy).then_inc(w.s_done, 1)

                def store(act, w, i, c):
                    act.wait_ge(w.s_done, i * w.walk + (c + 1))
                    if isinstance(i, int) and w.first + i * w.walk + c == BLOCKS - 1:
                        act.wait_ge(w.s_stored[c - 1], turn_of(i))
                    act.dma_start(rows_of(w.result, w.block(i, c)), done[:, c, :]).then_inc(w.s_stored[c], DMA)

                def ago(m, q, i, j, n, what):
                    if j >= n:
                        what(m, q, j - n)
                    elif at_least(m, 1):
                        what(m - 1, 1 - q, HALF + j - n)

                SIZE, COUNT = (LAST, -(-N // LAST)) if l else (BLOCK, AHEAD)
                assert COUNT % WALK == 0
                if l:
                    last_z = buf("last_z", [P, WALK, LAST // P * P])
                    last_x1 = buf("last_x1", [P, WALK, LAST // P * P])
                    s_in = [psem(f"last_loaded{c}") for c in range(WALK)]
                    s_out = [psem(f"out_stored{c}") for c in range(WALK)]
                    s_leaky, s_sum = psem("leaky"), psem("sum")
                    below = last_z[0:1].rearrange("o c f -> o (c f)")[:, 0:COUNT * HALVES]
                else:
                    below = buf("below", [1, COUNT * HALVES])[:]
                limit_i = buf("limit_i", [1, COUNT], I32)
                limit = buf("limit", [1, COUNT])
                count = buf("count", [1, 2, COUNT])
                need = buf("need", [1, COUNT], I32)
                s_final, s_limits, s_need = psem("half_steps_added"), psem("limits_made"), psem("need_made")
                s_count = psem("counting")

                def part(ap, k):
                    first = N - LAST if isinstance(k, int) and k == COUNT - 1 else k * LAST
                    return ap[bass.ds(first, LAST), :].rearrange("(p j) f -> p (j f)", p=P)

                def count_needed(dve):
                    dve.wait_ge(s_limits, 1)
                    nc.vector.tensor_copy(limit[:], limit_i[:]).then_inc(s_count, 1)
                    dve.wait_ge(s_count, 1)
                    is_below = below.rearrange("o (k m) -> o k m", m=HALVES)
                    firsts = dst_c[0:1, :].rearrange("o (m j) -> o m j", j=HALF)[:, :, 0]
                    nc.vector.tensor_tensor(is_below, firsts.unsqueeze(1).to_broadcast([1, COUNT, HALVES]),
                                            limit[:].unsqueeze(2).to_broadcast([1, COUNT, HALVES]),
                                            ALU.is_lt).then_inc(s_count, 1)
                    dve.wait_ge(s_count, 2)
                    nc.vector.reduce_sum(count[:, 0, :], is_below, AX.X).then_inc(s_count, 1)
                    dve.wait_ge(s_count, 3)
                    nc.vector.tensor_scalar(count[:, 1, :], count[:, 0, :], 1.0, None, ALU.max).then_inc(s_count, 1)
                    dve.wait_ge(s_count, 4)
                    nc.vector.tensor_copy(need[:], count[:, 1, :]).then_inc(s_need, 1)

                def add_up(dve):
                    def combine(k, c, i):
                        dve.wait_ge(s_in[c], i * (2 * DMA) + 2 * DMA)
                        nc.vector.scalar_tensor_tensor(last_z[:, c, :], last_z[:, c, :], SLOPE, last_z[:, c, :],
                                                       ALU.mult, ALU.max).then_inc(s_leaky, 1)
                        dve.wait_ge(s_leaky, k + 1)
                        nc.vector.tensor_tensor(last_z[:, c, :], last_z[:, c, :], last_x1[:, c, :],
                                                ALU.add).then_inc(s_sum, 1)

                    steps(dve, combine, 0, COUNT, COUNT, WALK)

                def wait_final(act, k):
                    act.wait_ge(s_final, act.value_load(need[0:1, bass.ds(k, 1)], min_val=1, max_val=HALVES))

                def wait_base(act):
                    act.wait_ge(s_need, 1)
                    for c in range(sweep.walk):
                        act.wait_ge(sweep.s_stored[c], DMA * walks)

                def work_ahead(act):
                    def step(k, c, i):
                        if at_least(k, WALK):
                            act.wait_ge(ahead.s_turn, k - (WALK - 1))
                        wait_final(act, k)
                        load_node(act, ahead, i, c)
                        ahead.earlier(i, c, 3, lambda i, c: keep_turned(act, ahead, i, c))
                        ahead.earlier(i, c, 4, lambda i, c: keep_product(act, ahead, i, c))
                        ahead.earlier(i, c, 5, lambda i, c: store(act, ahead, i, c))

                    wait_base(act)
                    steps(act, step, 2 * WALK, AHEAD, AHEAD, WALK)
                    for k in range(AHEAD, AHEAD + 5):
                        for late, what in ((3, keep_turned), (4, keep_product), (5, store)):
                            if k - late < AHEAD:
                                what(act, ahead, (k - late) // WALK, (k - late) % WALK)
                    for c in range(WALK):
                        act.wait_ge(ahead.s_stored[c], DMA * AHEAD // WALK)

                def write_out(act):
                    LATE = 4

                    def load(k, c, i):
                        if at_least(k, WALK):
                            act.wait_ge(s_out[c], i * DMA)
                        act.dma_start(last_x1[:, c, :], part(x1, k)).then_inc(s_in[c], DMA)
                        wait_final(act, k)
                        act.dma_start(last_z[:, c, :], part(result, k)).then_inc(s_in[c], DMA)

                    def store(k, c, i):
                        act.wait_ge(s_sum, k + 1)
                        if isinstance(k, int) and k == COUNT - 1:
                            act.wait_ge(s_out[c - 1], (i + 1) * DMA)
                        act.dma_start(part(out, k), last_z[:, c, :]).then_inc(s_out[c], DMA)

                    def step(k, c, i):
                        load(k, c, i)
                        if at_least(k, LATE):
                            store(k - LATE, (c - LATE) % WALK, i if c >= LATE else i - 1)

                    wait_base(act)
                    steps(act, step, WALK, COUNT - WALK, COUNT, WALK)
                    for k in range(COUNT - LATE, COUNT):
                        store(k, k % WALK, k // WALK)
                    for c in range(WALK):
                        act.wait_ge(s_out[c], DMA * COUNT // WALK)

                with nc.Block() as block:
                    @block.gpsimd
                    def _(pool):
                        nc.gpsimd.iota(limit_i[:], pattern=[[SIZE, COUNT]], base=SIZE,
                                       channel_multiplier=0).then_inc(s_limits, 1)

                        def gather(m, q, i):
                            if at_least(m, 2):
                                if l:
                                    pool.wait_ge(s_leaked, m - 1)
                                else:
                                    pool.wait_ge(s_summed, tile(m - 2, HALF - 1))
                            nc.gpsimd.tensor_copy(gidx[:, q, :], src_c[:, bass.ds(m * HALF, HALF)]).then_inc(s_gidx, 1)
                            wait_apart(pool, s_passed, (s_gidx, m + 1))
                            for j in range(HALF):
                                nc.gpsimd.indirect_dma_start(
                                    gat[:, q, j, :], None, source[0:N, :],
                                    bass.IndirectOffsetOnAxis(ap=gidx[:, q, j:j + 1], axis=0)).then_inc(s_gathered[q][j], DMA)

                        def add(m, q, i):
                            if at_least(m, 2):
                                for j in range(HALF):
                                    pool.wait_ge(s_added[q][j], use(m - 2, q))
                                pool.sem_inc(s_final, 1)
                            nc.gpsimd.tensor_copy(pidx[:, q, :], put_c[:, bass.ds(m * HALF, HALF)]).then_inc(s_pidx, 1)
                            wait_apart(pool, s_passed, (s_pidx, m + 1), (s_back[q], use(m, q)))
                            for j in range(HALF):
                                nc.gpsimd.indirect_dma_start(
                                    result, bass.IndirectOffsetOnAxis(ap=pidx[:, q, j:j + 1], axis=0),
                                    rows[:, q, j, :], None, compute_op=ALU.add).then_inc(s_added[q][j], DMA)

                        steps(pool, gather, 4, HALVES, HALVES, 2)
                        for c in range(sweep.walk):
                            pool.wait_ge(sweep.s_stored[c], DMA * walks)
                        steps(pool, add, 4, HALVES, HALVES, 2)
                        for q in range(2):
                            for j in range(HALF):
                                pool.wait_ge(s_added[q][j], DMA * HALVES // 2)
                            pool.sem_inc(s_final, 1)

                    @block.sync
                    def _(sp):
                        def load(m, r, i):
                            q = r % 2
                            if at_least(m, 2):
                                sp.wait_ge(s_same, m - 1)
                                sp.wait_ge(s_open, m - 1)
                            sp.dma_start(dst_b[:, q, :], dst_f[bass.ds(m * (HALF * P), HALF * P + 1)]
                                         .partition_broadcast(P)).then_inc(s_dstb[q], DMA)
                            for _, c in blocks(r):
                                if at_least(i, 1):
                                    sp.wait_ge(sweep.s_turn, i * sweep.walk + (c - sweep.walk + 1))
                                load_node(sp, sweep, i, c)

                        def back(m, q, i):
                            if at_least(m, 2):
                                for j in range(HALF):
                                    sp.wait_ge(s_added[q][j], use(m - 2, q))
                            sp.dma_start(rows[:, q, :, :], spill[bass.ds(m, 1), :, :]
                                         .rearrange("o p (j f) -> (o p) j f", f=P)).then_inc(s_back[q], DMA)

                        steps(sp, load, 2 * span, HALVES - span, HALVES, span)
                        for q in range(2):
                            sp.wait_ge(s_spilled[q], DMA * HALVES // 2)
                        steps(sp, back, 4, HALVES, HALVES, 2)

                    @block.vector
                    def _(dve):
                        nc.vector.memset(sums[:, HALF - 1, :], 0.0).then_inc(s_start, 1)
                        dve.wait_ge(s_start, 1)
                        count_needed(dve)

                        def columns(q):
                            return dst_b[:, q, 1:HALF * P + 1].rearrange("p (t e) -> p t e", e=P)

                        def select(m, q):
                            dve.wait_ge(s_dstb[q], use(m, q))
                            if at_least(m, 2):
                                dve.wait_ge(s_summed, tile(m - 2, HALF - 1))
                            nc.vector.tensor_tensor(same[:, q, :, :], columns(q),
                                                    dst_c[:, bass.ds(m * HALF, HALF)].unsqueeze(2).to_broadcast([P, HALF, P]),
                                                    ALU.is_equal).then_inc(s_same, 1)

                        def find_open(m, q):
                            dve.wait_ge(s_dstb[q], use(m, q))
                            if at_least(m, 2):
                                dve.wait_ge(s_carried, tile(m - 2, HALF - 1))
                            last_before = dst_b[:, q, 0:HALF * P].rearrange("p (t e) -> p t e", e=P)[:, :, 0:1]
                            nc.vector.tensor_tensor(open_[:, q, :, :], columns(q), last_before.to_broadcast([P, HALF, P]),
                                                    ALU.is_equal).then_inc(s_open, 1)

                        def leak(m, q):
                            for j in range(HALF):
                                dve.wait_ge(s_gathered[q][j], use(m, q))
                            nc.vector.scalar_tensor_tensor(act_gat[:, q, :, :], gat[:, q, :, :], SLOPE, gat[:, q, :, :],
                                                           ALU.mult, ALU.max).then_inc(s_leaked, 1)

                        def carry_on(m, q, j):
                            dve.wait_ge(s_summed, tile(m, j))
                            if at_least(m, 1) or j >= 1:
                                dve.wait_ge(s_carried, tile(m, j) - 1)
                            if j == 0:
                                dve.wait_ge(s_open, m + 1)
                            if at_least(m, 1):
                                dve.wait_ge(s_rowed, tile(m, j) - HALF)
                            nc.vector.scalar_tensor_tensor(sums[:, j, :], open_[:, q, j, :],
                                                           sums[:, (j - 1) % HALF, P - 1:P], sum_ps[(q + j) % 2][:, 0:P],
                                                           ALU.mult, ALU.add).then_inc(s_carried, 1)

                        def step(m, r, i):
                            q = r % 2
                            more = before(m, HALVES - 1)
                            for j in range(HALF):
                                if l:
                                    for after, c in blocks(r):
                                        if after == j:
                                            leak_node(dve, sweep, i, c)
                                carry_on(m, q, j)
                                if more and j == 2:
                                    select(m + 1, 1 - q)
                                if more and j == 3:
                                    find_open(m + 1, 1 - q)
                                if more and j == 5 and l:
                                    leak(m + 1, 1 - q)

                        select(0, 0)
                        find_open(0, 0)
                        if l:
                            leak(0, 0)
                        steps(dve, step, 2 * span, HALVES - span, HALVES, span)
                        if ahead:
                            steps(dve, lambda k, c, i: leak_node(dve, ahead, i, c), WALK, AHEAD, AHEAD, WALK)
                        else:
                            add_up(dve)

                    @block.scalar
                    def _(act):
                        def finish(m, q, j):
                            act.wait_ge(s_rowed, tile(m, j))
                            if at_least(m, 2) and j == 0:
                                act.wait_ge(s_spilled[q], use(m - 2, q))
                            nc.scalar.activation(rows[:, q, j, :], row_ps[(q + j) % 2][:, 0:P], ACT.Copy,
                                                 scale=inv_c[:, bass.ds(m * HALF + j, 1)]).then_inc(s_rows, 1)
                            if j == HALF - 1:
                                act.wait_ge(s_rows, tile(m, j))
                                act.dma_start(spill[bass.ds(m, 1), :, :].rearrange("o p (j f) -> (o p) j f", f=P),
                                              rows[:, q, :, :]).then_inc(s_spilled[q], DMA)

                        def step(m, r, i):
                            q = r % 2
                            for j in range(HALF):
                                for after, c in blocks(r):
                                    if after == j:
                                        sweep.earlier(i, c, 3, lambda i, c: keep_product(act, sweep, i, c))
                                        sweep.earlier(i, c, 1, lambda i, c: keep_turned(act, sweep, i, c))
                                        sweep.earlier(i, c, 4, lambda i, c: store(act, sweep, i, c))
                                ago(m, q, i, j, 3, finish)

                        steps(act, step, 2 * span, HALVES - span, HALVES, span)
                        last = walks - 1
                        keep_product(act, sweep, last, sweep.walk - 3)
                        keep_turned(act, sweep, last, sweep.walk - 1)
                        for c in (sweep.walk - 2, sweep.walk - 1):
                            keep_product(act, sweep, last, c)
                        for c in range(sweep.walk - 4, sweep.walk):
                            store(act, sweep, last, c)
                        for j in range(3):
                            ago(HALVES, 0, 0, j, 3, finish)
                        if ahead:
                            work_ahead(act)
                        else:
                            write_out(act)

                    @block.tensor
                    def _(pe):
                        def sum_runs(m, q, j):
                            if l:
                                if j == 0:
                                    pe.wait_ge(s_leaked, m + 1)
                            else:
                                pe.wait_ge(s_gathered[q][j], use(m, q))
                            if j == 0:
                                pe.wait_ge(s_same, m + 1)
                            if at_least(m, 1) or j >= 2:
                                pe.wait_ge(s_carried, tile(m, j) - 2)
                            nc.tensor.matmul(sum_ps[(q + j) % 2][:, 0:P], act_gat[:, q, j, :], same[:, q, j, :],
                                             start=True, stop=True).then_inc(s_summed, 1)

                        def to_rows(m, q, j):
                            s = (q + j) % 2
                            pe.wait_ge(s_carried, tile(m, j))
                            if at_least(m, 1) or j >= 2:
                                pe.wait_ge(s_rows, tile(m, j) - 2)
                            nc.tensor.matmul(row_ps[s][:, 0:P], sums[:, j, :], w_l[:, l, :],
                                             start=True, stop=True).then_inc(s_rowed, 1)

                        def step(m, r, i):
                            q = r % 2
                            for j in range(HALF):
                                sum_runs(m, q, j)
                                for after, c in blocks(r):
                                    if after == j:
                                        sweep.earlier(i, c, 1, lambda i, c: turn(pe, sweep, i, c))
                                        sweep.earlier(i, c, 2, lambda i, c: product(pe, sweep, i, c))
                                ago(m, q, i, j, 2, to_rows)

                        steps(pe, step, 2 * span, HALVES - span, HALVES, span)
                        turn(pe, sweep, walks - 1, sweep.walk - 1)
                        product(pe, sweep, walks - 1, sweep.walk - 2)
                        product(pe, sweep, walks - 1, sweep.walk - 1)
                        ago(HALVES, 0, 0, 0, 2, to_rows)
                        ago(HALVES, 0, 0, 1, 2, to_rows)
                        if ahead:
                            pe.wait_ge(sweep.s_ht, BLOCKS)
                            pe.wait_ge(sweep.s_done, BLOCKS)

                            def step_ahead(k, c, i):
                                turn(pe, ahead, i, c)
                                ahead.earlier(i, c, 1, lambda i, c: product(pe, ahead, i, c))

                            steps(pe, step_ahead, WALK, AHEAD, AHEAD, WALK)
                            product(pe, ahead, AHEAD // WALK - 1, WALK - 1)
            clear(held)

        relational_pass()
        norm_pass()
        layer_pass(0, g0, z[0])
        layer_pass(1, z[0], z[1])


_INS = ['x', 'src', 'dst', 'edge_type_16', 'L0_gnn_weight', 'L0_gnn_w_comp', 'L0_gnn_h_bias', 'L1_gnn_enc_w',
        'L1_gnn_enc_b', 'L1_gnn_lin_l_w', 'L1_gnn_lin_l_b', 'L1_gnn_lin_r_w']
_OUTS = [((100000, 128), 'float32')]


def kernel(**inputs):
    import numpy as _np
    import concourse.bacc as _bacc
    from concourse import mybir as _mybir
    from concourse.bass_utils import run_bass_kernel_spmd as _run

    nc = _bacc.Bacc("TRN2", target_bir_lowering=False, num_devices=1)
    arrays, args = {}, []
    for name in _INS:
        a = _np.ascontiguousarray(inputs[name])
        arrays[f"in_{name}_dram"] = a
        args.append(nc.dram_tensor(f"in_{name}_dram", a.shape, _mybir.dt.from_np(a.dtype), kind="ExternalInput").ap())
    for i, (shape, dtype) in enumerate(_OUTS):
        dt = _mybir.dt.from_np(_np.dtype(dtype))
        args.append(nc.dram_tensor(f"out_{i}_dram", shape, dt, kind="ExternalOutput").ap())
    gnn_kernel(nc, *args)
    r = _run(nc, [arrays], core_ids=[0])
    got = tuple(r.results[0][f"out_{i}_dram"] for i in range(len(_OUTS)))
    return got[0]
```
